# Optimizing a Trainium2 kernel written in Bass

```python
import numpy as np
import jax
import jax.numpy as jnp

def _softmax(x, axis=-1):
    return jax.nn.softmax(x, axis=axis)

def _gelu(x):
    return jax.nn.gelu(x, approximate=True)

def _silu(x):
    return jax.nn.silu(x)

def _sigmoid(x):
    return jax.nn.sigmoid(x)

def _layernorm(x, axis=-1, eps=1e-05):
    m = jnp.mean(x, axis=axis, keepdims=True)
    v = jnp.var(x, axis=axis, keepdims=True)
    return (x - m) / jnp.sqrt(v + eps)

def _scatter_add(tgt, idx, src, axis=0):
    return tgt.at[idx].add(src)

def _segment_sum(src, seg, n):
    return jax.ops.segment_sum(src, seg, n)
kernel_name = 'mk_gnn_resnorm_d2_gnn_r8_3a8b81'

def setup_inputs(seed: int=0):
    np.random.seed(seed)
    _w = jnp.asarray

    def _rec_inputs():
        import jax
        import jax.numpy as jnp
        _gk = jax.random.key(seed)
        x = -6.415e-05 + 1 * jax.random.normal(jax.random.fold_in(_gk, 1), (1250, 512), jnp.float32)
        _s = jax.random.randint(jax.random.fold_in(_gk, 2), (10000,), 0, 1250, jnp.int32)
        _d = jax.random.randint(jax.random.fold_in(_gk, 3), (10000,), 0, 1250, jnp.int32)
        _loop = jnp.arange(1250, dtype=jnp.int32)
        src = jnp.concatenate([_s, _d, _loop])
        dst = jnp.concatenate([_d, _s, _loop])
        _o = jnp.argsort(dst, stable=True)
        src = src[_o]
        dst = dst[_o]
        edge_attr_20 = jax.random.uniform(jax.random.fold_in(_gk, 12), (21250, 20), jnp.float32, 0.0, 0.999999)
        edge_attr_3 = -0.0005747 + 0.998114 * jax.random.normal(jax.random.fold_in(_gk, 13), (21250, 3), jnp.float32)
        edge_weight = jax.random.uniform(jax.random.fold_in(_gk, 14), (21250,), jnp.float32, 0.0, 0.999973)
        return (x, src, dst, edge_attr_20, edge_attr_3, edge_weight)
    x, src, dst, edge_attr_20, edge_attr_3, edge_weight = _rec_inputs()

    def _L0_gnn_setup():
        import jax, jax.numpy as jnp
        import numpy as np
        N_NODES = 2500
        N_EDGES = 40000
        D = 512
        L = 3
        key = jax.random.key(seed)
        ks = jax.random.split(key, 6)
        x = jax.random.normal(ks[0], (N_NODES, D), dtype=jnp.float32)
        Ws_self = jax.random.normal(ks[1], (L, D, D), dtype=jnp.float32) * 0.05
        Ws_neigh = jax.random.normal(ks[2], (L, D, D), dtype=jnp.float32) * 0.05
        bs = jax.random.normal(ks[3], (L, D), dtype=jnp.float32) * 0.05
        src = jax.random.randint(ks[4], (N_EDGES,), 0, N_NODES, dtype=jnp.int64)
        dst = jax.random.randint(ks[5], (N_EDGES,), 0, N_NODES, dtype=jnp.int64)
        return {'x': x, 'Ws_self': Ws_self, 'Ws_neigh': Ws_neigh, 'bs': bs, 'src': src, 'dst': dst}
    _L0_gnn_all = _L0_gnn_setup()
    _L0_gnn_in = {k: v for k, v in _L0_gnn_all.items() if k in ('Ws_self', 'Ws_neigh', 'bs')}
    del _L0_gnn_all

    def _L1_gnn_setup():
        import jax, jax.numpy as jnp
        import numpy as np
        N_ATOMS = 625
        N_EDGES = 6250
        C = 128
        F = 128
        N_RBF = 20
        LOG2 = float(np.log(2.0))
        Y0 = float(1.0 / np.sqrt(4.0 * np.pi))
        Y1_SCALE = float(np.sqrt(3.0 / (4.0 * np.pi)))

        def shifted_softplus(x):
            return jax.nn.softplus(x) - LOG2

        def _forward(x, idx_i, idx_j, f_ij, rcut_ij, r_ij, W_in2f_s, W_in2f_v, Wf1, bf1, Wf2, bf2, W1_s, W1_v, W2_s, W2_v):
            n = x.shape[0]
            e = r_ij.shape[0]
            xs = x[:, :C] @ (W_in2f_s / np.sqrt(C))
            xv = jnp.einsum('nci,cf->nfi', x[:, C:].reshape(n, C, 3), W_in2f_v) / np.sqrt(C)
            sj = xs[idx_j]
            vj = xv[idx_j]
            u = r_ij / jnp.linalg.norm(r_ij, axis=-1, keepdims=True)
            Yv = Y1_SCALE * u
            o0a = sj * Y0
            o0b = jnp.einsum('efi,ei->ef', vj, Yv) / np.sqrt(3.0)
            s2 = jnp.stack([o0a, o0b], axis=-1).reshape(e, 2 * F)
            ova = sj[:, :, None] * Yv[:, None, :]
            ovb = vj * Y0
            v2 = jnp.stack([ova, ovb], axis=2)
            w1 = jnp.cross(vj, Yv[:, None, :]) / np.sqrt(2.0)
            ax, ay, az = (vj[..., 0], vj[..., 1], vj[..., 2])
            bx, by, bz = (Yv[:, None, 0], Yv[:, None, 1], Yv[:, None, 2])
            t = jnp.stack([(ax * by + ay * bx) / np.sqrt(2.0), (ay * bz + az * by) / np.sqrt(2.0), (2.0 * az * bz - ax * bx - ay * by) / np.sqrt(6.0), (az * bx + ax * bz) / np.sqrt(2.0), (ax * bx - ay * by) / np.sqrt(2.0)], axis=-1)
            h = shifted_softplus(f_ij @ Wf1 + bf1)
            W = (h @ Wf2 + bf2) * rcut_ij[:, None]
            m_s = s2 * W[:, :2 * F]
            m_v = (v2.reshape(e, 2 * F, 3) * W[:, 2 * F:4 * F, None]).reshape(e, 6 * F)
            m_w = (w1 * W[:, 4 * F:5 * F, None]).reshape(e, 3 * F)
            m_t = (t * W[:, 5 * F:6 * F, None]).reshape(e, 5 * F)
            x_ij = jnp.concatenate([m_s, m_v, m_w, m_t], axis=1)
            agg = jax.ops.segment_sum(x_ij, idx_i, num_segments=n)
            S = agg[:, :2 * F] @ (W1_s / np.sqrt(2 * F))
            V = jnp.einsum('nmi,mc->nci', agg[:, 2 * F:8 * F].reshape(n, 2 * F, 3), W1_v) / np.sqrt(2 * F)
            S = shifted_softplus(S)
            S = S @ (W2_s / np.sqrt(C))
            V = jnp.einsum('nci,cd->ndi', V, W2_v) / np.sqrt(C)
            return jnp.concatenate([S, V.reshape(n, 3 * C)], axis=1)
        key = jax.random.key(seed)
        ks = jax.random.split(key, 16)
        f32 = jnp.float32
        x = jax.random.normal(ks[0], (N_ATOMS, 4 * C), f32)
        idx_i = jnp.sort(jax.random.randint(ks[1], (N_EDGES,), 0, N_ATOMS))
        idx_j = jax.random.randint(ks[2], (N_EDGES,), 0, N_ATOMS)
        f_ij = jax.random.uniform(ks[3], (N_EDGES, N_RBF), f32)
        rcut_ij = jax.random.uniform(ks[4], (N_EDGES,), f32)
        r_ij = jax.random.normal(ks[5], (N_EDGES, 3), f32)
        W_in2f_s = jax.random.normal(ks[6], (C, F), f32)
        W_in2f_v = jax.random.normal(ks[7], (C, F), f32)
        Wf1 = jax.random.normal(ks[8], (N_RBF, F), f32) / np.sqrt(N_RBF)
        bf1 = 0.1 * jax.random.normal(ks[9], (F,), f32)
        Wf2 = jax.random.normal(ks[10], (F, 6 * F), f32) / np.sqrt(F)
        bf2 = 0.1 * jax.random.normal(ks[11], (6 * F,), f32)
        W1_s = jax.random.normal(ks[12], (2 * F, C), f32)
        W1_v = jax.random.normal(ks[13], (2 * F, C), f32)
        W2_s = jax.random.normal(ks[14], (C, C), f32)
        W2_v = jax.random.normal(ks[15], (C, C), f32)
        return dict(x=x, idx_i=idx_i, idx_j=idx_j, f_ij=f_ij, rcut_ij=rcut_ij, r_ij=r_ij, W_in2f_s=W_in2f_s, W_in2f_v=W_in2f_v, Wf1=Wf1, bf1=bf1, Wf2=Wf2, bf2=bf2, W1_s=W1_s, W1_v=W1_v, W2_s=W2_s, W2_v=W2_v)
    _L1_gnn_all = _L1_gnn_setup()
    _L1_gnn_in = {k: v for k, v in _L1_gnn_all.items() if k in ('W_in2f_s', 'W_in2f_v', 'Wf1', 'bf1', 'Wf2', 'bf2', 'W1_s', 'W1_v', 'W2_s', 'W2_v')}
    del _L1_gnn_all
    return {'x': x, 'src': src, 'dst': dst, 'edge_attr_20': edge_attr_20, 'edge_attr_3': edge_attr_3, 'edge_weight': edge_weight, 'L0_gnn_Ws_self': _L0_gnn_in['Ws_self'], 'L0_gnn_Ws_neigh': _L0_gnn_in['Ws_neigh'], 'L0_gnn_bs': _L0_gnn_in['bs'], 'L1_gnn_W_in2f_s': _L1_gnn_in['W_in2f_s'], 'L1_gnn_W_in2f_v': _L1_gnn_in['W_in2f_v'], 'L1_gnn_Wf1': _L1_gnn_in['Wf1'], 'L1_gnn_bf1': _L1_gnn_in['bf1'], 'L1_gnn_Wf2': _L1_gnn_in['Wf2'], 'L1_gnn_bf2': _L1_gnn_in['bf2'], 'L1_gnn_W1_s': _L1_gnn_in['W1_s'], 'L1_gnn_W1_v': _L1_gnn_in['W1_v'], 'L1_gnn_W2_s': _L1_gnn_in['W2_s'], 'L1_gnn_W2_v': _L1_gnn_in['W2_v']}

def reference(x, src, dst, edge_attr_20, edge_attr_3, edge_weight, L0_gnn_Ws_self, L0_gnn_Ws_neigh, L0_gnn_bs, L1_gnn_W_in2f_s, L1_gnn_W_in2f_v, L1_gnn_Wf1, L1_gnn_bf1, L1_gnn_Wf2, L1_gnn_bf2, L1_gnn_W1_s, L1_gnn_W1_v, L1_gnn_W2_s, L1_gnn_W2_v):
    import jax
    import jax.numpy as jnp

    def _L0_gnn_ref(x, Ws_self, Ws_neigh, bs, src, dst):
        import jax, jax.numpy as jnp
        import numpy as np
        N_NODES = 2500
        N_EDGES = 40000
        D = 512
        L = 3
        n = x.shape[0]
        deg = jax.ops.segment_sum(jnp.ones_like(dst, dtype=x.dtype), dst, num_segments=n)
        inv_deg = (1.0 / jnp.clip(deg, 1.0))[:, None]
        h = x
        n_layers = Ws_self.shape[0]
        for l in range(n_layers):
            neigh = jax.ops.segment_sum(h[src], dst, num_segments=n) * inv_deg
            h = h @ Ws_self[l] + neigh @ Ws_neigh[l] + bs[l]
            if l != n_layers - 1:
                h = jax.nn.relu(h)
        return h

    def _L1_gnn_ref(x, idx_i, idx_j, f_ij, rcut_ij, r_ij, W_in2f_s, W_in2f_v, Wf1, bf1, Wf2, bf2, W1_s, W1_v, W2_s, W2_v):
        import jax, jax.numpy as jnp
        import numpy as np
        N_ATOMS = 625
        N_EDGES = 6250
        C = 128
        F = 128
        N_RBF = 20
        LOG2 = float(np.log(2.0))
        Y0 = float(1.0 / np.sqrt(4.0 * np.pi))
        Y1_SCALE = float(np.sqrt(3.0 / (4.0 * np.pi)))

        def shifted_softplus(x):
            return jax.nn.softplus(x) - LOG2

        def _forward(x, idx_i, idx_j, f_ij, rcut_ij, r_ij, W_in2f_s, W_in2f_v, Wf1, bf1, Wf2, bf2, W1_s, W1_v, W2_s, W2_v):
            n = x.shape[0]
            e = r_ij.shape[0]
            xs = x[:, :C] @ (W_in2f_s / np.sqrt(C))
            xv = jnp.einsum('nci,cf->nfi', x[:, C:].reshape(n, C, 3), W_in2f_v) / np.sqrt(C)
            sj = xs[idx_j]
            vj = xv[idx_j]
            u = r_ij / jnp.linalg.norm(r_ij, axis=-1, keepdims=True)
            Yv = Y1_SCALE * u
            o0a = sj * Y0
            o0b = jnp.einsum('efi,ei->ef', vj, Yv) / np.sqrt(3.0)
            s2 = jnp.stack([o0a, o0b], axis=-1).reshape(e, 2 * F)
            ova = sj[:, :, None] * Yv[:, None, :]
            ovb = vj * Y0
            v2 = jnp.stack([ova, ovb], axis=2)
            w1 = jnp.cross(vj, Yv[:, None, :]) / np.sqrt(2.0)
            ax, ay, az = (vj[..., 0], vj[..., 1], vj[..., 2])
            bx, by, bz = (Yv[:, None, 0], Yv[:, None, 1], Yv[:, None, 2])
            t = jnp.stack([(ax * by + ay * bx) / np.sqrt(2.0), (ay * bz + az * by) / np.sqrt(2.0), (2.0 * az * bz - ax * bx - ay * by) / np.sqrt(6.0), (az * bx + ax * bz) / np.sqrt(2.0), (ax * bx - ay * by) / np.sqrt(2.0)], axis=-1)
            h = shifted_softplus(f_ij @ Wf1 + bf1)
            W = (h @ Wf2 + bf2) * rcut_ij[:, None]
            m_s = s2 * W[:, :2 * F]
            m_v = (v2.reshape(e, 2 * F, 3) * W[:, 2 * F:4 * F, None]).reshape(e, 6 * F)
            m_w = (w1 * W[:, 4 * F:5 * F, None]).reshape(e, 3 * F)
            m_t = (t * W[:, 5 * F:6 * F, None]).reshape(e, 5 * F)
            x_ij = jnp.concatenate([m_s, m_v, m_w, m_t], axis=1)
            agg = jax.ops.segment_sum(x_ij, idx_i, num_segments=n)
            S = agg[:, :2 * F] @ (W1_s / np.sqrt(2 * F))
            V = jnp.einsum('nmi,mc->nci', agg[:, 2 * F:8 * F].reshape(n, 2 * F, 3), W1_v) / np.sqrt(2 * F)
            S = shifted_softplus(S)
            S = S @ (W2_s / np.sqrt(C))
            V = jnp.einsum('nci,cd->ndi', V, W2_v) / np.sqrt(C)
            return jnp.concatenate([S, V.reshape(n, 3 * C)], axis=1)
        return _forward(x, idx_i, idx_j, f_ij, rcut_ij, r_ij, W_in2f_s, W_in2f_v, Wf1, bf1, Wf2, bf2, W1_s, W1_v, W2_s, W2_v)
    x = _layernorm(x + _L0_gnn_ref(x, L0_gnn_Ws_self, L0_gnn_Ws_neigh, L0_gnn_bs, src, dst), axis=-1)
    x = _layernorm(x + _L1_gnn_ref(x, src, dst, edge_attr_20, edge_weight, edge_attr_3, L1_gnn_W_in2f_s, L1_gnn_W_in2f_v, L1_gnn_Wf1, L1_gnn_bf1, L1_gnn_Wf2, L1_gnn_bf2, L1_gnn_W1_s, L1_gnn_W1_v, L1_gnn_W2_s, L1_gnn_W2_v), axis=-1)
    return x

_drawn_inputs = setup_inputs


def setup_inputs(seed=0):
    import zlib

    import numpy as np

    out = dict(_drawn_inputs(seed))
    spreads = {}
    factors = {}
    for name, (base, spread) in spreads.items():
        noise = np.random.default_rng([zlib.crc32(name.encode()), seed]).standard_normal(out[name].shape)
        drawn = base * np.exp(spread * noise) if base else spread * noise
        out[name] = jnp.asarray(drawn.astype(out[name].dtype))
    for name, factor in factors.items():
        out[name] = (out[name] * factor).astype(out[name].dtype)
    return out
```

```python
from contextlib import ExitStack

import concourse.bass as bass
from concourse import mybir

F32 = mybir.dt.float32
BF16 = mybir.dt.bfloat16
I32 = mybir.dt.int32
I16 = mybir.dt.int16
ALU = mybir.AluOpType
ACT = mybir.ActivationFunctionType
AX = mybir.AxisListType

P = 128
LN_EPS = 1e-5
PI = 3.141592653589793
Y0 = (1.0 / (4.0 * PI)) ** 0.5
Y1 = (3.0 / (4.0 * PI)) ** 0.5

REC = 32
C_ONE, C_CUT, C_DIR, C_DST, C_OWN = 20, 21, 22, 25, 26
NF = C_ONE + 1

M_SCALED, M_SA, M_SB, M_VA, M_VB, M_ALL = 0, 1, 2, 3, 6, 9


def plan(n_nodes, n_edges):
    nb = -(-n_nodes // P)
    gt = 4
    gsz = gt * P
    groups = (n_edges + nb * (gsz - 1)) // gsz
    groups += 1 - groups % 2
    ep = max(k for k in range(1, P + 1) if n_edges % k == 0)
    return nb, gt, gsz, groups, ep, n_edges // ep


def over_groups(engine, groups, body):
    body(0, 0)
    with engine.Fori(0, (groups - 3) // 2, 1) as i:
        body(2 * i + 1, 1)
        body(2 * i + 2, 0)
    body(groups - 2, 1)
    body(groups - 1, 0)


def gnn_resnorm(nc, x, src, dst, edge_f, edge_r, edge_w, ws_self, ws_neigh, bs,
                w_in_s, w_in_v, wf1, bf1, wf2, bf2, w1_s, w1_v, w2_s, w2_v, out):
    N, D = x.shape
    E = src.shape[0]
    LAYERS = ws_self.shape[0]
    C = w_in_s.shape[0]
    K = D // P
    NB, GT, GSZ, G, EP, ET = plan(N, E)
    T = G * GT
    NP = NB * P
    TAIL = N - (NB - 1) * P
    SH = GSZ.bit_length() - 1
    SLICES = [(s, min(s + 512, NP)) for s in range(0, NP, 512)]
    ST = 5
    assert C == P and D == 4 * P and ET % (2 * ST) == 0 and GSZ == 1 << SH and LAYERS == 3

    slots = nc.dram_tensor("edge_slots", (P * T, REC), F32, kind="Internal").ap()
    table = nc.dram_tensor("node_rows", (NP, D), F32, kind="Internal").ap()

    with ExitStack() as ctx:
        def sb(name, shape, dt=F32):
            return ctx.enter_context(nc.sbuf_tensor(name, shape, dt))

        def sem(name):
            return ctx.enter_context(nc.semaphore(name))

        ps = ctx.enter_context(nc.psum_tensor("ps", [P, 8, 512], F32))
        psf = ps[:, :, :].rearrange("p b n -> p (b n)")

        X = sb("X", [P, NB, D])
        H = sb("H", [P, NB, D])
        HT = sb("HT", [P, K, NP])
        NT = sb("NT", [P, K, NP])
        AT = sb("AT", [P, NB * NP])
        rec = sb("rec", [P, T * REC])
        Wl = sb("Wl", [P, 2, K, D])
        bias = sb("bias", [P, D])
        wf2_raw = sb("wf2_raw", [P, 6 * P])
        WF = sb("WF", [P, 4, P])
        WIN = sb("WIN", [P, 2, P])
        W1 = sb("W1", [P, 2, 2, P])
        W2 = sb("W2", [P, 2, P])
        WF1 = sb("WF1", [NF, P])
        tmp = sb("tmp", [P, 2, 2, D])
        bf_raw = tmp[0:3, 0, 0, :]
        bf_perm = tmp[0:3, 0, 1, :].rearrange("p (j f) -> p j f", j=4)
        bf_rest = tmp[0:3, 1, :, :]
        bf_part = sb("bf_part", [3, 2, 4 * P], BF16)
        bf3 = sb("bf3", [3, 4 * P], BF16)
        ones3 = sb("ones3", [3, P], BF16)
        sel3 = sb("sel3", [3, 3])
        ident = sb("ident", [P, P])
        lower = sb("lower", [P, P])
        ones = sb("ones", [P, P])
        half = sb("half", [P, 1])
        iota_n = sb("iota_n", [P, NP], I16)
        iota_g = sb("iota_g", [1, G, NB])
        dst_idx = sb("dst_idx", [P, T], I32)
        blocks_before = sb("blocks_before", [1, G])
        group_block = sb("group_block", [1, G], I32)
        inv_deg = sb("inv_deg", [P, NB])
        stats = sb("stats", [P, NB, 6])
        mv = sb("mv", [P, NB, 2])
        rstd = sb("rstd", [P, 3, NB])
        gather_idx = sb("gather_idx", [P, 2, GT], I32)
        rec_f = sb("rec_f", [P, GT, NF])
        small = sb("small", [P, 10, NB])

        at = AT[0:EP, :]
        n_buckets = NB * ET
        bucket = at[:, 0:n_buckets]
        in_bucket = at[:, n_buckets:2 * n_buckets]
        running = at[:, 2 * n_buckets:3 * n_buckets]
        all_ones = at[:, 3 * n_buckets:4 * n_buckets]
        E_rec = at[:, 4 * n_buckets:4 * n_buckets + ET * REC]
        nt = NT[0:EP, :, :].rearrange("p k n -> p (k n)")
        f_raw = nt[:, 0:20 * ET]
        ht = HT[0:EP, :, :].rearrange("p k n -> p (k n)")
        r_raw = ht[:, 0:3 * ET]
        r_sq = ht[:, 3 * ET:6 * ET]
        dst_i = ht[:, 6 * ET:7 * ET].bitcast(I32)
        src_i = ht[:, 7 * ET:8 * ET].bitcast(I32)
        w_raw = ht[:, 8 * ET:9 * ET]
        blk_i = ht[:, 9 * ET:10 * ET].bitcast(I32)
        blk_f = ht[:, 10 * ET:11 * ET]
        place_f = ht[:, 11 * ET:12 * ET]
        place_i = ht[:, 12 * ET:13 * ET].bitcast(I32)
        place_lo = ht[:, 13 * ET:14 * ET].bitcast(I32)
        place_hi = ht[:, 14 * ET:15 * ET].bitcast(I32)
        row_i = ht[:, 15 * ET:16 * ET].bitcast(I32)
        norm = ht[:, 16 * ET:19 * ET]
        stage = sb("stage", [EP, 2, ST, REC])
        stage_idx = sb("stage_idx", [EP, 2, ST], I32)
        bucket_end = sb("bucket_end", [EP, NB + 1])

        ntf = NT[:, :, :].rearrange("p k n -> p (k n)")
        n_oh = 2 * GT * NP // 2
        oh_dst = ntf[:, 0:n_oh].bitcast(BF16).rearrange("p (h k n) -> p h k n", h=2, k=GT)
        oh_own = sb("oh_own", [P, 2, GT, P], BF16)

        rows = H[:, 0:2 * GT, :].rearrange("p (h k) d -> p h k d", h=2)
        msg = ntf[:, 0:2 * M_ALL * P].rearrange("p (h m f) -> p h m f", h=2, m=M_ALL)
        at0 = 2 * M_ALL * P
        hid = ntf[:, at0:at0 + 2 * GSZ].rearrange("p (h e) -> p h e", h=2)
        at0 += 2 * GSZ
        f_t = NT[0:NF, :, :].rearrange("p k n -> p (k n)")[:, at0:at0 + GSZ]
        at0 += GSZ
        assert at0 <= K * NP
        htf = HT[:, :, :].rearrange("p k n -> p (k n)")
        h_abs = htf[:, 0:GSZ]
        h_exp = htf[:, GSZ:2 * GSZ]
        h_ln = htf[:, 2 * GSZ:3 * GSZ]
        dots = htf[:, 3 * GSZ:3 * GSZ + 6 * P].rearrange("p (h m f) -> p h m f", h=2, m=3)
        hot = htf[:, 3 * GSZ + 6 * P:3 * GSZ + 8 * P].rearrange("p (h f) -> p h f", h=2)
        NA = (M_ALL - 1) * P
        agg = AT[:, 0:NB * NA]
        TAB = NT

        agg_t = HT[:, 0:2, 0:8 * P].rearrange("p h (m n) -> p h m n", m=8)
        sv = HT[:, 2, 0:8 * P].rearrange("p (h m n) -> p h m n", h=2, m=4)
        s_tmp = HT[:, 3, 0:6 * P].rearrange("p (h m n) -> p h m n", h=2, m=3)

        s = {name: sem(name) for name in (
            "edges_loaded", "nodes_loaded", "weights_loaded", "layer_loaded", "pads_written",
            "consts_made", "zeroed", "sort_step", "counts_ready", "totals_ready", "edge_copied", "norm_sq",
            "norm_ready", "staged", "scattered_0", "scattered_1", "rec_loaded", "rec_split",
            "one_hots", "block_summed", "block_added", "deg_part", "deg_ready", "inv_ready",
            "h_turned", "ht_copied", "n_summed", "nt_copied", "dense_ready", "dense_step",
            "h_ready", "var_ready", "std_ready", "x1_ready", "table_ready", "table_copied",
            "table_written", "prep", "staged_f", "f_turned", "ft_copied", "hid_ready",
            "hid_abs", "hid_exp", "hid_ln", "hid_done", "w_ready", "msg_ready", "dot_step",
            "va_ready", "edges_summed", "agg_added", "idx_copied", "gathered_0", "gathered_1",
            "turns", "agg_turned", "agg_copied", "s_ready", "s_step", "v_copied", "sv_ready", "o_ready",
            "z_step", "out_ready", "written")}

        block = ctx.enter_context(nc.Block())

        def atleast(eng, semaphore, value):
            if not isinstance(value, int) or value > 0:
                eng.wait_ge(semaphore, value)

        class Chain:

            def __init__(self, eng, semaphore):
                self.eng, self.semaphore, self.n = eng, semaphore, 0

            def __call__(self, instruction):
                instruction.then_inc(self.semaphore, 1)
                self.n += 1
                self.eng.wait_ge(self.semaphore, self.n)

        HALVES = ET // (2 * ST)
        TURNS_1 = NB
        DENSE = NB

        @block.sync
        def _(sp):
            sp.dma_start(dst_i, dst.rearrange("(p t) -> p t", p=EP)).then_inc(s["edges_loaded"], 16)
            sp.dma_start(src_i, src.rearrange("(p t) -> p t", p=EP)).then_inc(s["edges_loaded"], 16)
            sp.dma_start(r_raw, edge_r.rearrange("(p t) c -> p (t c)", p=EP)).then_inc(s["edges_loaded"], 16)
            sp.dma_start(w_raw, edge_w.rearrange("(p t) -> p t", p=EP)).then_inc(s["edges_loaded"], 16)
            sp.dma_start(f_raw, edge_f.rearrange("(p t) c -> p (t c)", p=EP)).then_inc(s["edges_loaded"], 16)
            sp.wait_ge(s["zeroed"], 2)
            for buf in (X, H):
                sp.dma_start(buf[:, 0:NB - 1, :], x[0:(NB - 1) * P, :].rearrange("(b p) d -> p b d", p=P)
                             ).then_inc(s["nodes_loaded"], 16)
                sp.dma_start(buf[0:TAIL, NB - 1, :], x[(NB - 1) * P:N, :]).then_inc(s["nodes_loaded"], 16)
            sp.wait_ge(s["zeroed"], 4)
            sp.dma_start(slots.rearrange("(p t) c -> p (t c)", p=P), rec[:, :]).then_inc(s["pads_written"], 16)
            for buf, w in ((wf2_raw[:, :], wf2), (WIN[:, 0, :], w_in_s), (WIN[:, 1, :], w_in_v),
                           (W1[:, 0, :, :], w1_s.rearrange("(f u) c -> f u c", u=2)),
                           (W1[:, 1, :, :], w1_v.rearrange("(f u) c -> f u c", u=2)),
                           (W2[:, 0, :], w2_s), (W2[:, 1, :], w2_v), (WF1[0:NF - 1, :], wf1),
                           (WF1[NF - 1:NF, :], bf1.rearrange("(a f) -> a f", a=1)),
                           (bf_raw[:, :], bf2[0:4 * P].rearrange("(a f) -> a f", a=1).to_broadcast([3, 4 * P]))):
                sp.dma_start(buf, w).then_inc(s["weights_loaded"], 16)

            def load_layer(layer):
                w_s = ws_self[bass.ds(layer, 1), :, :].rearrange("a (k p) n -> p (a k) n", p=P)
                w_n = ws_neigh[bass.ds(layer, 1), :, :].rearrange("a (k p) n -> p (a k) n", p=P)
                sp.dma_start(Wl[:, 0, :, :], w_s).then_inc(s["layer_loaded"], 16)
                sp.dma_start(Wl[:, 1, :, :], w_n).then_inc(s["layer_loaded"], 16)
                sp.dma_start(bias[:, :], bs[bass.ds(layer, 1), :].to_broadcast([P, D])).then_inc(s["layer_loaded"], 16)

            load_layer(0)
            sp.wait_ge(s["scattered_0"], 16 * ST * HALVES)
            sp.wait_ge(s["scattered_1"], 16 * ST * HALVES)
            sp.dma_start(rec[:, :], slots.rearrange("(p t) c -> p (t c)", p=P)).then_inc(s["rec_loaded"], 16)
            with sp.Fori(0, LAYERS - 1, 1) as i:
                sp.wait_ge(s["dense_ready"], DENSE * i + DENSE)
                sp.wait_ge(s["dense_step"], 2 * DENSE * i + 2 * DENSE)
                load_layer(i + 1)
            for b in range(NB):
                sp.wait_ge(s["table_copied"], b + 1)
                sp.dma_start(table[b * P:(b + 1) * P, :],
                             TAB[:, :, b * P:(b + 1) * P]).then_inc(s["table_written"], 16)
            for b in range(NB):
                n = P if b < NB - 1 else TAIL
                sp.wait_ge(s["out_ready"], b + 1)
                sp.dma_start(out[b * P:b * P + n, :], X[0:n, b, :]).then_inc(s["written"], 16)
            sp.wait_ge(s["written"], 16 * NB)

        @block.gpsimd
        def _(pool):
            bk = bucket.rearrange("p (b t) -> p b t", b=NB)
            pool.iota(bk, pattern=[[1, NB], [0, ET]], base=0, channel_multiplier=0,
                      allow_small_or_imprecise_dtypes=True).then_inc(s["consts_made"], 1)
            pool.memset(ident[:, :], 0.0).then_inc(s["consts_made"], 1)
            pool.memset(lower[:, :], 1.0).then_inc(s["consts_made"], 1)
            pool.memset(sel3[:, :], 0.0).then_inc(s["consts_made"], 1)
            pool.wait_ge(s["consts_made"], 4)
            pool.affine_select(out=ident[:, :], in_=ident[:, :], compare_op=ALU.not_equal, fill=1.0, base=0,
                               pattern=[[-1, P]], channel_multiplier=1).then_inc(s["consts_made"], 1)
            pool.affine_select(out=lower[:, :], in_=lower[:, :], compare_op=ALU.is_gt, fill=0.0, base=0,
                               pattern=[[1, P]], channel_multiplier=-1).then_inc(s["consts_made"], 1)
            pool.affine_select(out=sel3[:, :], in_=sel3[:, :], compare_op=ALU.not_equal, fill=1.0, base=0,
                               pattern=[[-1, 3]], channel_multiplier=1).then_inc(s["consts_made"], 1)
            pool.iota(iota_g[:, :, :], pattern=[[1, G], [0, NB]], base=0, channel_multiplier=0,
                      allow_small_or_imprecise_dtypes=True).then_inc(s["consts_made"], 1)
            pool.iota(iota_n[:, :], pattern=[[1, NP]], base=0, channel_multiplier=0).then_inc(s["consts_made"], 1)

            pool.wait_ge(s["pads_written"], 16)
            with pool.Fori(0, HALVES, 1) as i:
                for h in range(2):
                    pool.wait_ge(s["staged"], 4 * i + 2 * h + 2)
                    pool.sem_inc(s["turns"], 1)
                    for k in range(ST):
                        pool.indirect_dma_start(
                            out=slots[:, :], out_offset=bass.IndirectOffsetOnAxis(ap=stage_idx[:, h, k:k + 1], axis=0),
                            in_=stage[:, h, k, :], in_offset=None).then_inc(s[f"scattered_{h}"], 16)

            pool.wait_ge(s["rec_split"], 1)
            pool.wait_ge(s["table_written"], 16 * NB)

            def gather(g, h):
                atleast(pool, s["msg_ready"], 16 * (g - 1))
                pool.tensor_copy(gather_idx[:, h, :], dst_idx[:, bass.ds(g * GT, GT)]).then_inc(s["idx_copied"], 1)
                pool.wait_ge(s["idx_copied"], g + 1)
                pool.sem_inc(s["turns"], 1)
                for k in range(GT):
                    pool.indirect_dma_start(
                        out=rows[:, h, k, :], out_offset=None, in_=table[:, :],
                        in_offset=bass.IndirectOffsetOnAxis(ap=gather_idx[:, h, k:k + 1], axis=0),
                    ).then_inc(s[f"gathered_{h}"], 16)

            over_groups(pool, G, gather)

        @block.scalar
        def _(act):
            act.preload_act_table_set("natural_log_exp_and_others")
            er = E_rec.rearrange("p (t c) -> p t c", c=REC)
            act.wait_ge(s["edges_loaded"], 80)
            act.activation(er[:, :, C_DST], dst_i, ACT.Copy).then_inc(s["edge_copied"], 1)
            act.activation(er[:, :, C_CUT], w_raw, ACT.Copy).then_inc(s["edge_copied"], 1)
            act.activation(er[:, :, 0:20], f_raw.rearrange("p (t c) -> p t c", c=20), ACT.Copy).then_inc(s["edge_copied"], 1)
            act.wait_ge(s["norm_sq"], 1)
            act.activation(norm[:, 0:ET], norm[:, ET:2 * ET], ACT.Sqrt).then_inc(s["norm_ready"], 1)
            act.preload_act_table_set("natural_log_exp_and_others")

            def copy_ht(b, done):
                act.wait_ge(s["h_turned"], done + 1)
                act.activation(HT[:, :, b * P:(b + 1) * P],
                               ps[:, b % 2, :].rearrange("p (k n) -> p k n", k=K), ACT.Copy).then_inc(s["ht_copied"], 1)

            act.wait_ge(s["staged"], 4 * HALVES)
            for b in range(NB):
                copy_ht(b, b)

            def layer(l, last):
                for f in range(K):
                    for j, (a, z) in enumerate(SLICES):
                        n = f * len(SLICES) + j
                        act.wait_ge(s["n_summed"], l * (K * len(SLICES)) + n + 1)
                        act.activation(NT[:, f, a:z], ps[:, 2 + n % 2, 0:z - a], ACT.Copy).then_inc(s["nt_copied"], 1)
                if last:
                    return
                for b in range(NB):
                    act.wait_ge(s["dense_step"], l * (2 * DENSE) + 2 * b + 2)
                    act.activation(H[:, b, :], tmp[:, b % 2, 1, :], ACT.Relu).then_inc(s["h_ready"], 1)
                for b in range(NB):
                    copy_ht(b, l * NB + NB + b)

            with act.Fori(0, LAYERS - 1, 1) as i:
                layer(i, False)
            layer(LAYERS - 1, True)

            act.wait_ge(s["var_ready"], 1)
            act.activation(rstd[:, 1, :], rstd[:, 0, :], ACT.Sqrt).then_inc(s["std_ready"], 1)
            act.preload_act_table_set("natural_log_exp_and_others")
            for b in range(NB):
                copy_ht(b, LAYERS * NB + b)
            for b in range(NB):
                act.wait_ge(s["table_ready"], b + 1)
                act.activation(TAB[:, :, b * P:(b + 1) * P],
                               ps[:, 2 + b % 2, :].rearrange("p (k n) -> p k n", k=K), ACT.Copy).then_inc(s["table_copied"], 1)

            def stage_features(g):
                atleast(act, s["f_turned"], g)
                act.activation(rec_f[:, :, :],
                               rec[:, bass.ds(g * GT * REC, GT * REC)].rearrange("p (k c) -> p k c", c=REC)[:, :, 0:NF],
                               ACT.Copy).then_inc(s["staged_f"], 1)

            def copy_features(g):
                act.wait_ge(s["f_turned"], g + 1)
                atleast(act, s["hid_ready"], g)
                act.activation(f_t, ps[0:NF, 0, :], ACT.Copy).then_inc(s["ft_copied"], 1)

            def hid_1(g):
                act.wait_ge(s["hid_ready"], g + 1)
                act.activation(h_abs, ps[:, 1, :], ACT.Abs).then_inc(s["hid_abs"], 1)
                act.wait_ge(s["hid_abs"], g + 1)
                act.activation(h_exp, h_abs, ACT.Exp, scale=-1.0).then_inc(s["hid_exp"], 1)

            def hid_2(g):
                act.wait_ge(s["hid_exp"], g + 1)
                atleast(act, s["hid_done"], g)
                act.activation(h_ln, h_exp, ACT.Ln, bias=half[:, :], scale=0.5).then_inc(s["hid_ln"], 1)

            def direct(g, h, k):
                act.wait_ge(s["msg_ready"], 16 * g + 4 * k + 1)
                for i in range(3):
                    act.activation(msg[:, k % 2, M_VA + i, :], msg[:, k % 2, M_SCALED, :], ACT.Copy,
                                   scale=rec[:, bass.ds((g * GT + k) * REC + C_DIR + i, 1)]).then_inc(s["va_ready"], 1)

            def group(g, h):
                left = G - 1 - g if isinstance(g, int) else G
                if left >= 2:
                    stage_features(g + 2)
                direct(g, h, 0)
                if left >= 1:
                    hid_1(g + 1)
                direct(g, h, 1)
                if left >= 1:
                    hid_2(g + 1)
                direct(g, h, 2)
                if left >= 2:
                    copy_features(g + 2)
                direct(g, h, 3)

            act.wait_ge(s["table_copied"], NB)
            act.wait_ge(s["prep"], 12)
            act.wait_ge(s["table_written"], 16 * NB)
            stage_features(0)
            copy_features(0)
            stage_features(1)
            hid_1(0)
            hid_2(0)
            copy_features(1)
            over_groups(act, G, group)

            for b in range(NB):
                act.wait_ge(s["agg_turned"], b + 1)
                if b >= 2:
                    act.wait_ge(s["s_ready"], b - 1)
                for u in range(2):
                    act.activation(agg_t[:, b % 2, 4 * u:4 * u + 4, :],
                                   ps[:, u, :].rearrange("p (m n) -> p m n", m=4), ACT.Copy).then_inc(s["agg_copied"], 1)
                act.wait_ge(s["s_ready"], b + 1)
                if b >= 2:
                    act.wait_ge(s["o_ready"], b - 1)
                    act.wait_ge(s["sv_ready"], b - 1)
                pb = ps[:, 2 + b % 2, :].rearrange("p (m n) -> p m n", m=4)
                act.activation(sv[:, b % 2, 1:4, :], pb[:, 1:4, :], ACT.Copy).then_inc(s["v_copied"], 1)
                act.activation(s_tmp[:, b % 2, 0, :], pb[:, 0, :], ACT.Abs).then_inc(s["s_step"], 1)
                act.wait_ge(s["s_step"], 3 * b + 1)
                act.activation(s_tmp[:, b % 2, 1, :], s_tmp[:, b % 2, 0, :], ACT.Exp, scale=-1.0).then_inc(s["s_step"], 1)
                act.wait_ge(s["s_step"], 3 * b + 2)
                act.activation(s_tmp[:, b % 2, 2, :], s_tmp[:, b % 2, 1, :], ACT.Ln, bias=half[:, :], scale=0.5
                               ).then_inc(s["s_step"], 1)
            act.wait_ge(s["var_ready"], 2)
            act.activation(rstd[:, 1, :], rstd[:, 0, :], ACT.Sqrt).then_inc(s["std_ready"], 1)

        @block.vector
        def _(dve):
            v = nc.vector
            v.memset(X[96:P, NB - 1, :], 0.0).then_inc(s["zeroed"], 1)
            v.memset(H[96:P, NB - 1, :], 0.0).then_inc(s["zeroed"], 1)
            v.memset(rec[:, :], 0.0).then_inc(s["zeroed"], 1)
            dve.wait_ge(s["zeroed"], 3)
            v.memset(rec[:, :].rearrange("p (t c) -> p t c", c=REC)[:, :, C_OWN], -1.0).then_inc(s["zeroed"], 1)
            v.memset(ones[:, :], 1.0).then_inc(s["zeroed"], 1)
            v.memset(half[:, :], 0.5).then_inc(s["zeroed"], 1)
            v.memset(ones3[:, :], 1.0).then_inc(s["zeroed"], 1)
            v.memset(bucket_end[:, 0:1], 0.0).then_inc(s["zeroed"], 1)
            er = E_rec.rearrange("p (t c) -> p t c", c=REC)
            v.memset(er[:, :, C_ONE], 1.0).then_inc(s["zeroed"], 1)
            v.memset(er[:, :, C_OWN + 1:REC], 0.0).then_inc(s["zeroed"], 1)

            step = Chain(dve, s["sort_step"])
            step(v.memset(all_ones, 1.0))
            dve.wait_ge(s["edges_loaded"], 80)
            dve.wait_ge(s["consts_made"], 1)
            step(v.tensor_scalar(blk_i, src_i, 7, None, ALU.arith_shift_right))
            step(v.tensor_copy(blk_f, blk_i))
            step(v.scalar_tensor_tensor(out=er[:, :, C_OWN], in0=blk_f, scalar=-float(P), in1=src_i,
                                        op0=ALU.mult, op1=ALU.add))
            pbt = lambda a: a.rearrange("p (b t) -> p b t", b=NB)
            step(v.tensor_tensor(pbt(in_bucket), blk_f.rearrange("p (a t) -> p a t", a=1).to_broadcast([EP, NB, ET]),
                                 pbt(bucket), ALU.is_equal))
            step(v.tensor_tensor_scan(running, all_ones, in_bucket, 0.0, ALU.mult, ALU.add))
            dve.wait_ge(s["zeroed"], 8)
            step(v.tensor_copy(bucket_end[:, 1:NB + 1], pbt(running)[:, :, ET - 1]))
            counts = small[0:EP, 0, :]
            v.tensor_tensor(counts, bucket_end[:, 1:NB + 1], bucket_end[:, 0:NB], ALU.subtract).then_inc(s["counts_ready"], 1)
            r3 = lambda a: a.rearrange("p (t c) -> p t c", c=3)
            step(v.tensor_tensor(r_sq, r_raw, r_raw, ALU.mult))
            v.tensor_reduce(norm[:, ET:2 * ET], r3(r_sq), axis=AX.X, op=ALU.add).then_inc(s["norm_sq"], 1)
            dve.wait_ge(s["totals_ready"], 1)
            g_i, g_s = small[:, 1, :].bitcast(I32), small[:, 2, :].bitcast(I32)
            g_f, g_end, g_start = small[:, 3, :], small[:, 4, :], small[:, 5, :]
            first, base = small[0:EP, 6, :], small[0:EP, 7, :]
            step(v.tensor_scalar(g_i, ps[:, 7, 16:16 + NB], float(GSZ - 1), None, ALU.add))
            step(v.tensor_scalar(g_s, g_i, SH, None, ALU.arith_shift_right))
            step(v.tensor_copy(g_f, g_s))
            step(v.tensor_tensor_scan(g_end, ones[:, 0:NB], g_f, 0.0, ALU.mult, ALU.add))
            step(v.tensor_tensor(g_start, g_end, g_f, ALU.subtract))
            step(v.scalar_tensor_tensor(out=first, in0=g_start[0:EP, :], scalar=float(GSZ), in1=ps[0:EP, 7, 0:NB],
                                        op0=ALU.mult, op1=ALU.add))
            step(v.scalar_tensor_tensor(out=base, in0=first, scalar=-1.0, in1=bucket_end[:, 0:NB],
                                        op0=ALU.add, op1=ALU.subtract))
            step(v.tensor_tensor(pbt(running), pbt(running),
                                 base.rearrange("p (b a) -> p b a", a=1).to_broadcast([EP, NB, ET]), ALU.add))
            step(v.tensor_tensor(running, running, in_bucket, ALU.mult))
            step(v.tensor_reduce(place_f, running.rearrange("p (b t) -> p t b", b=NB), axis=AX.X, op=ALU.add))
            step(v.tensor_copy(place_i, place_f))
            step(v.tensor_scalar(place_lo, place_i, P - 1, None, ALU.bitwise_and))
            step(v.tensor_scalar(place_hi, place_i, 7, None, ALU.arith_shift_right))
            step(v.scalar_tensor_tensor(out=row_i, in0=place_lo, scalar=float(T), in1=place_hi,
                                        op0=ALU.mult, op1=ALU.add))
            dve.wait_ge(s["norm_ready"], 1)
            step(v.reciprocal(norm[:, 2 * ET:3 * ET], norm[:, 0:ET]))
            step(v.tensor_tensor(er[:, :, C_DIR:C_DIR + 3], r3(r_raw),
                                 norm[:, 2 * ET:3 * ET].rearrange("p (t a) -> p t a", a=1).to_broadcast([EP, ET, 3]), ALU.mult))
            dve.wait_ge(s["edge_copied"], 3)
            dve.wait_ge(s["zeroed"], 10)
            with v.Fori(0, HALVES, 1) as i:
                for h in range(2):
                    dve.wait_ge(s[f"scattered_{h}"], 16 * ST * i)
                    v.tensor_copy(stage[:, h, :, :].rearrange("p k c -> p (k c)"),
                                  E_rec[:, bass.ds((i * 2 + h) * (ST * REC), ST * REC)]).then_inc(s["staged"], 1)
                    v.tensor_copy(stage_idx[:, h, :], row_i[:, bass.ds((i * 2 + h) * ST, ST)]).then_inc(s["staged"], 1)

            dve.wait_ge(s["consts_made"], 9)
            step(v.tensor_tensor(iota_g[:, :, :], iota_g[:, :, :],
                                 g_end[0:1, :].rearrange("p (a b) -> p a b", a=1).to_broadcast([1, G, NB]), ALU.is_ge))
            step(v.tensor_reduce(blocks_before[:, :], iota_g[:, :, :], axis=AX.X, op=ALU.add))
            step(v.tensor_scalar(group_block[:, :], blocks_before[:, :], float(NB - 1), None, ALU.min))

            dve.wait_ge(s["weights_loaded"], 160)
            c = C ** -0.5
            pair = lambda a, lo: a[:, lo:lo + 2 * P].rearrange("p (f u) -> p u f", u=2)
            k3 = 3.0 ** -0.5
            for j, (lo, u, scale) in enumerate(((2 * P, 0, Y1), (0, 0, Y0), (0, 1, Y1 * k3), (2 * P, 1, Y0))):
                v.tensor_scalar(WF[:, j, :], pair(wf2_raw, lo)[:, u, :], scale, None, ALU.mult).then_inc(s["prep"], 1)
                step(v.tensor_scalar(bf_perm[:, j, :], pair(bf_raw, lo)[:, u, :], scale, None, ALU.mult))
            bfp = bf_perm[:, :, :].rearrange("p j f -> p (j f)")
            step(v.tensor_copy(bf_part[:, 0, :], bfp))
            step(v.tensor_tensor(bf_rest[:, 0, :], bfp, bf_part[:, 0, :], ALU.subtract))
            step(v.tensor_copy(bf_part[:, 1, :], bf_rest[:, 0, :]))
            step(v.tensor_tensor(bf_rest[:, 1, :], bf_rest[:, 0, :], bf_part[:, 1, :], ALU.subtract))
            step(v.tensor_scalar(bfp, bf_part[:, 0, :], sel3[:, 0:1], None, ALU.mult))
            step(v.scalar_tensor_tensor(out=bf_rest[:, 0, :], in0=bf_part[:, 1, :], scalar=sel3[:, 1:2], in1=bfp,
                                        op0=ALU.mult, op1=ALU.add))
            v.scalar_tensor_tensor(out=bf3[:, :], in0=bf_rest[:, 1, :], scalar=sel3[:, 2:3], in1=bf_rest[:, 0, :],
                                   op0=ALU.mult, op1=ALU.add).then_inc(s["prep"], 1)
            for wt, scale in ((WIN, c), (W1[:, 0, :, :], (2 * C) ** -0.5), (W1[:, 1, :, :], (2 * C) ** -0.5), (W2, c)):
                t = wt[:, :, :]
                v.tensor_scalar(t, t, scale, None, ALU.mult).then_inc(s["prep"], 1)
            dve.wait_ge(s["scattered_0"], 16 * ST * HALVES)
            dve.wait_ge(s["scattered_1"], 16 * ST * HALVES)
            v.memset(AT[:, :], 0.0).then_inc(s["prep"], 1)
            dve.wait_ge(s["rec_loaded"], 16)
            r_tc = rec[:, :].rearrange("p (t c) -> p t c", c=REC)
            v.tensor_copy(dst_idx[:, :], r_tc[:, :, C_DST]).then_inc(s["rec_split"], 1)
            dve.wait_ge(s["prep"], 10)

            def one_hots(g, h):
                atleast(dve, s["block_summed"], g - 1)
                for k in range(GT):
                    at_t = (g * GT + k) * REC
                    v.tensor_scalar(oh_dst[:, h, k, :], iota_n[:, :], rec[:, bass.ds(at_t + C_DST, 1)], None,
                                    ALU.is_equal).then_inc(s["one_hots"], 1)
                    v.tensor_scalar(oh_own[:, h, k, :], iota_n[:, 0:P], rec[:, bass.ds(at_t + C_OWN, 1)], None,
                                    ALU.is_equal).then_inc(s["one_hots"], 1)

            def add_block(g, h):
                dve.wait_ge(s["block_summed"], g + 1)
                atleast(dve, s["block_added"], g)
                b = v.value_load(group_block[0:1, bass.ds(g, 1)], min_val=0, max_val=NB - 1)
                a = AT[:, bass.ds(b * NP, NP)]
                v.tensor_tensor(a, a, psf[:, 1536 * h:1536 * h + NP], ALU.add).then_inc(s["block_added"], 1)

            def count_group(g, h):
                one_hots(g, h)
                if not (isinstance(g, int) and g == 0):
                    add_block(g - 1, 1 - h)

            over_groups(v, G, count_group)
            add_block(G - 1, (G - 1) % 2)

            dve.wait_ge(s["block_added"], G)
            dve.wait_ge(s["block_summed"], G)
            deg_part = NT[:, 0, 0:NP]
            v.tensor_reduce(deg_part, AT[:, :].rearrange("p (j n) -> p n j", j=NB), axis=AX.X, op=ALU.add
                            ).then_inc(s["deg_part"], 1)
            dve.wait_ge(s["deg_ready"], 1)
            step(v.tensor_scalar(small[:, 8, :], ps[:, 7, 0:NB], 1.0, None, ALU.max))
            v.reciprocal(inv_deg[:, :], small[:, 8, :]).then_inc(s["inv_ready"], 1)
            dve.wait_ge(s["inv_ready"], 1)

            def combine(l, b):
                dve.wait_ge(s["layer_loaded"], 48 * l + 48)
                dve.wait_ge(s["dense_ready"], l * DENSE + b + 1)
                pd = 4 + 2 * (b % 2)
                v.scalar_tensor_tensor(out=tmp[:, b % 2, 0, :], in0=ps[:, pd + 1, :], scalar=inv_deg[:, b:b + 1],
                                       in1=bias[:, :], op0=ALU.mult, op1=ALU.add).then_inc(s["dense_step"], 1)
                dve.wait_ge(s["dense_step"], l * (2 * DENSE) + 2 * b + 1)
                v.tensor_tensor(tmp[:, b % 2, 1, :], tmp[:, b % 2, 0, :], ps[:, pd, :], ALU.add).then_inc(s["dense_step"], 1)

            with v.Fori(0, LAYERS - 1, 1) as i:
                for b in range(NB):
                    if b < 2:
                        dve.wait_ge(s["h_ready"], i * NB)
                    else:
                        dve.wait_ge(s["h_ready"], i * NB + b - 1)
                    combine(i, b)

            dve.wait_ge(s["h_ready"], NB * (LAYERS - 1))
            for b in range(NB):
                combine(LAYERS - 1, b)
                dve.wait_ge(s["dense_step"], 2 * DENSE * (LAYERS - 1) + 2 * b + 2)
                step(v.tensor_tensor(X[:, b, :], X[:, b, :], tmp[:, b % 2, 1, :], ALU.add))
                step(v.bn_stats(stats[:, b, :], X[:, b, :]))
                step(v.bn_aggr(mv[:, b, :], stats[:, b, :]))
            v.tensor_scalar(rstd[:, 0, :], mv[:, :, 1], LN_EPS, None, ALU.add).then_inc(s["var_ready"], 1)
            dve.wait_ge(s["std_ready"], 1)
            step(v.reciprocal(rstd[:, 2, :], rstd[:, 1, :]))
            for b in range(NB):
                v.tensor_scalar(X[:, b, :], X[:, b, :], mv[:, b, 0:1], rstd[:, 2, b:b + 1], ALU.subtract, ALU.mult
                                ).then_inc(s["x1_ready"], 1)
            v.memset(agg, 0.0).then_inc(s["prep"], 1)
            dve.wait_ge(s["x1_ready"], NB)
            dve.wait_ge(s["prep"], 11)

            def finish_hidden(g, h):
                dve.wait_ge(s["hid_ln"], g + 1)
                atleast(dve, s["w_ready"], GT * (g - 1))
                v.scalar_tensor_tensor(out=hid[:, h, :], in0=ps[:, 1, :], scalar=0.0, in1=h_ln,
                                       op0=ALU.max, op1=ALU.add).then_inc(s["hid_done"], 1)

            def messages(g, h, k):
                n = g * GT + k
                u = k % 2
                dve.wait_ge(s["w_ready"], n + 1)
                if k == 0:
                    dve.wait_ge(s[f"gathered_{h}"], 16 * GT * (g // 2 + 1) if isinstance(g, int) else
                                32 * g + (64 if h == 0 else 32))
                atleast(dve, s["edges_summed"], n - 1)
                atleast(dve, s["va_ready"], 3 * (n - 1))
                w = ps[:, 2 + u, :].rearrange("p (m f) -> p m f", m=4)
                r = rows[:, h, k, :].rearrange("p (m f) -> p m f", m=4)
                y = lambda i: rec[:, bass.ds(n * REC + C_DIR + i, 1)]
                v.tensor_tensor(msg[:, u, M_SCALED:M_SA + 1, :], w[:, 0:2, :], r[:, 0:1, :].to_broadcast([P, 2, P]),
                                ALU.mult).then_inc(s["msg_ready"], 1)
                v.tensor_scalar(dots[:, u, 0, :], r[:, 1, :], y(0), None, ALU.mult).then_inc(s["dot_step"], 1)
                v.tensor_tensor(msg[:, u, M_VB:M_VB + 3, :], r[:, 1:4, :], w[:, 3:4, :].to_broadcast([P, 3, P]),
                                ALU.mult).then_inc(s["msg_ready"], 1)
                dve.wait_ge(s["dot_step"], 3 * n + 1)
                v.scalar_tensor_tensor(out=dots[:, u, 1, :], in0=r[:, 2, :], scalar=y(1), in1=dots[:, u, 0, :],
                                       op0=ALU.mult, op1=ALU.add).then_inc(s["dot_step"], 1)
                v.tensor_scalar(hot[:, u, :], iota_n[:, 0:P], rec[:, bass.ds(n * REC + C_OWN, 1)],
                                rec[:, bass.ds(n * REC + C_CUT, 1)], ALU.is_equal, ALU.mult).then_inc(s["msg_ready"], 1)
                dve.wait_ge(s["dot_step"], 3 * n + 2)
                v.scalar_tensor_tensor(out=dots[:, u, 2, :], in0=r[:, 3, :], scalar=y(2), in1=dots[:, u, 1, :],
                                       op0=ALU.mult, op1=ALU.add).then_inc(s["dot_step"], 1)
                dve.wait_ge(s["dot_step"], 3 * n + 3)
                v.tensor_tensor(msg[:, u, M_SB, :], dots[:, u, 2, :], w[:, 2, :], ALU.mult).then_inc(s["msg_ready"], 1)

            def add_sums(g, h):
                dve.wait_ge(s["edges_summed"], GT * (g + 1))
                atleast(dve, s["agg_added"], g)
                b = v.value_load(group_block[0:1, bass.ds(g, 1)], min_val=0, max_val=NB - 1)
                a = agg[:, bass.ds(b * NA, NA)]
                v.tensor_tensor(a, a, psf[:, (4 + 2 * h) * 512:(6 + 2 * h) * 512], ALU.add).then_inc(s["agg_added"], 1)

            def edge_group(g, h):
                is_first = isinstance(g, int) and g == 0
                is_last = isinstance(g, int) and g == G - 1
                messages(g, h, 0)
                messages(g, h, 1)
                if not is_last:
                    finish_hidden(g + 1, 1 - h)
                messages(g, h, 2)
                if not is_first:
                    add_sums(g - 1, 1 - h)
                messages(g, h, 3)

            dve.wait_ge(s["table_written"], 16 * NB)
            v.memset(dots[:, 0, 0, 0:1], 0.0).then_inc(s["prep"], 1)
            dve.wait_ge(s["prep"], 12)
            finish_hidden(0, 0)
            over_groups(v, G, edge_group)
            add_sums(G - 1, (G - 1) % 2)

            for b in range(NB):
                dve.wait_ge(s["s_step"], 3 * b + 3)
                dve.wait_ge(s["v_copied"], b + 1)
                if b >= 2:
                    dve.wait_ge(s["o_ready"], b - 1)
                v.scalar_tensor_tensor(out=sv[:, b % 2, 0, :], in0=ps[:, 2 + b % 2, 0:P], scalar=0.0,
                                       in1=s_tmp[:, b % 2, 2, :], op0=ALU.max, op1=ALU.add).then_inc(s["sv_ready"], 1)
                dve.wait_ge(s["o_ready"], b + 1)
                po = ps[:, 4 + b % 2, :]
                n = b * 4
                v.tensor_tensor(X[:, b, 0:P], X[:, b, 0:P], po[:, 0:P], ALU.add).then_inc(s["z_step"], 1)
                xv = X[:, b, P:].rearrange("p (f i) -> p i f", i=3)
                v.tensor_tensor(xv, xv, po[:, P:].rearrange("p (i f) -> p i f", i=3), ALU.add).then_inc(s["z_step"], 1)
                dve.wait_ge(s["z_step"], n + 2)
                v.bn_stats(stats[:, b, :], X[:, b, :]).then_inc(s["z_step"], 1)
                dve.wait_ge(s["z_step"], n + 3)
                v.bn_aggr(mv[:, b, :], stats[:, b, :]).then_inc(s["z_step"], 1)
            dve.wait_ge(s["z_step"], 4 * NB)
            v.tensor_scalar(rstd[:, 0, :], mv[:, :, 1], LN_EPS, None, ALU.add).then_inc(s["var_ready"], 1)
            dve.wait_ge(s["std_ready"], 2)
            step(v.reciprocal(rstd[:, 2, :], rstd[:, 1, :]))
            for b in range(NB):
                v.tensor_scalar(X[:, b, :], X[:, b, :], mv[:, b, 0:1], rstd[:, 2, b:b + 1], ALU.subtract, ALU.mult
                                ).then_inc(s["out_ready"], 1)

        @block.tensor
        def _(pe):
            mm = nc.tensor.matmul
            pe.wait_ge(s["consts_made"], 7)
            pe.wait_ge(s["zeroed"], 5)
            pe.wait_ge(s["counts_ready"], 1)
            counts = small[0:EP, 0, :]
            mm(ps[0:EP, 7, 0:NB], lower[0:EP, 0:EP], counts, start=True, stop=True)
            mm(ps[:, 7, 16:16 + NB], ones[0:EP, :], counts, start=True, stop=True).then_inc(s["totals_ready"], 1)

            def turn_h(source, b, done, strided=False):
                atleast(pe, s["ht_copied"], done - 1)
                for f in range(K):
                    if strided:
                        a = source[:, b, 0:P] if f == 0 else source[:, b, P + f - 1:D:3]
                    else:
                        a = source[:, b, f * P:(f + 1) * P]
                    last = nc.tensor.transpose(ps[:, b % 2, f * P:(f + 1) * P], a, ident[:, :])
                last.then_inc(s["h_turned"], 1)

            pe.wait_ge(s["nodes_loaded"], 64)
            for b in range(NB):
                turn_h(H, b, b)

            pe.wait_ge(s["ht_copied"], NB)

            def count_group(g, h):
                pe.wait_ge(s["one_hots"], 2 * GT * g + 2 * GT)
                atleast(pe, s["block_added"], g - 1)
                for a, z in SLICES:
                    for k in range(GT):
                        last = mm(psf[:, 1536 * h + a:1536 * h + z], oh_own[:, h, k, :], oh_dst[:, h, k, a:z],
                                  start=(k == 0), stop=(k == GT - 1))
                last.then_inc(s["block_summed"], 1)

            over_groups(pe, G, count_group)

            pe.wait_ge(s["deg_part"], 1)
            for b in range(NB):
                last = mm(ps[:, 7, b:b + 1], NT[:, 0, b * P:(b + 1) * P], ones[:, 0:1], start=True, stop=True)
            last.then_inc(s["deg_ready"], 1)

            a_t = AT[:, :].rearrange("p (j n) -> p j n", j=NB)

            def layer(l, last_layer):
                pe.wait_ge(s["h_ready"], l * NB)
                pe.wait_ge(s["ht_copied"], l * NB + NB)
                ns = len(SLICES)
                for f in range(K):
                    for j, (a, z) in enumerate(SLICES):
                        n = f * ns + j
                        if n >= 2:
                            pe.wait_ge(s["nt_copied"], l * (K * ns) + n - 1)
                        else:
                            pe.wait_ge(s["nt_copied"], l * (K * ns))
                        for q in range(NB):
                            last = mm(ps[:, 2 + n % 2, 0:z - a], H[:, q, f * P:(f + 1) * P],
                                      a_t[:, q, a:z], start=(q == 0), stop=(q == NB - 1))
                        last.then_inc(s["n_summed"], 1)
                pe.wait_ge(s["nt_copied"], l * (K * ns) + K * ns)
                pe.wait_ge(s["layer_loaded"], 48 * l + 48)
                for b in range(NB):
                    if b >= 2:
                        pe.wait_ge(s["dense_step"], l * (2 * DENSE) + 2 * b - 2)
                    else:
                        pe.wait_ge(s["dense_step"], l * (2 * DENSE))
                    for u, a in ((0, HT), (1, NT)):
                        for f in range(K):
                            last = mm(ps[:, 4 + 2 * (b % 2) + u, :], a[:, f, b * P:(b + 1) * P], Wl[:, u, f, :],
                                      start=(f == 0), stop=(f == K - 1))
                    last.then_inc(s["dense_ready"], 1)
                if last_layer:
                    return
                for b in range(NB):
                    pe.wait_ge(s["h_ready"], l * NB + b + 1)
                    turn_h(H, b, l * NB + NB + b)

            pe.wait_ge(s["inv_ready"], 1)
            with pe.Fori(0, LAYERS - 1, 1) as i:
                layer(i, False)
            layer(LAYERS - 1, True)

            for b in range(NB):
                pe.wait_ge(s["x1_ready"], b + 1)
                turn_h(X, b, LAYERS * NB + b, strided=True)
            for b in range(NB):
                pe.wait_ge(s["ht_copied"], LAYERS * NB + b + 1)
                if b >= 2:
                    pe.wait_ge(s["table_copied"], b - 1)
                for f in range(K):
                    last = mm(ps[:, 2 + b % 2, f * P:(f + 1) * P], HT[:, f, b * P:(b + 1) * P],
                              WIN[:, min(f, 1), :], start=True, stop=True)
                last.then_inc(s["table_ready"], 1)

            def turn_features(g):
                pe.wait_ge(s["staged_f"], g + 1)
                atleast(pe, s["ft_copied"], g)
                for k in range(GT):
                    last = nc.tensor.transpose(ps[0:NF, 0, k * P:(k + 1) * P], rec_f[:, k, :], ident[:, :])
                last.then_inc(s["f_turned"], 1)

            def hidden(g):
                pe.wait_ge(s["ft_copied"], g + 1)
                atleast(pe, s["hid_done"], g)
                mm(ps[:, 1, :], WF1[:, :], f_t, start=True, stop=True).then_inc(s["hid_ready"], 1)

            def weights(g, h, k):
                if k == 0:
                    pe.wait_ge(s["hid_done"], g + 1)
                mm(ps[:, 2 + k % 2, :], ones3[:, :], bf3[:, :], start=True, stop=False)
                mm(ps[:, 2 + k % 2, :], hid[:, h, k * P:(k + 1) * P], WF[:, :, :], start=False, stop=True
                   ).then_inc(s["w_ready"], 1)

            def edge_group(g, h):
                left = G - 1 - g if isinstance(g, int) else G
                for k in range(GT):
                    if k == 0 and left >= 1:
                        hidden(g + 1)
                    if k == 2 and left >= 2:
                        turn_features(g + 2)
                    pe.wait_ge(s["msg_ready"], 16 * g + 4 * k + 4)
                    if k + 2 < GT:
                        weights(g, h, k + 2)
                    elif left >= 1:
                        weights(g + 1, 1 - h, k + 2 - GT)
                    pe.wait_ge(s["va_ready"], 12 * g + 3 * k + 3)
                    if k == 0:
                        atleast(pe, s["agg_added"], g - 1)
                    for u in range(2):
                        last = mm(ps[:, 4 + 2 * h + u, :], hot[:, k % 2, :], msg[:, k % 2, 1 + 4 * u:5 + 4 * u, :],
                                  start=(k == 0), stop=(k == GT - 1))
                    last.then_inc(s["edges_summed"], 1)

            pe.wait_ge(s["table_copied"], NB)
            pe.wait_ge(s["prep"], 12)
            turn_features(0)
            hidden(0)
            turn_features(1)
            weights(0, 0, 0)
            weights(0, 0, 1)
            over_groups(pe, G, edge_group)

            pe.wait_ge(s["agg_added"], G)
            ag = agg.rearrange("p (b m f) -> p b m f", b=NB, m=8)
            for b in range(NB):
                if b >= 1:
                    pe.wait_ge(s["agg_copied"], 2 * b)
                for m in range(8):
                    last = nc.tensor.transpose(ps[:, m // 4, (m % 4) * P:(m % 4 + 1) * P], ag[:, b, m, :], ident[:, :])
                last.then_inc(s["agg_turned"], 1)
                pe.wait_ge(s["agg_copied"], 2 * b + 2)
                if b >= 2:
                    pe.wait_ge(s["sv_ready"], b - 1)
                a = agg_t[:, b % 2, :, :]
                pb = ps[:, 2 + b % 2, :]
                mm(pb[:, 0:P], W1[:, 0, 0, :], a[:, 0, :], start=True, stop=False)
                mm(pb[:, 0:P], W1[:, 0, 1, :], a[:, 1, :], start=False, stop=True)
                mm(pb[:, P:], W1[:, 1, 0, :], a[:, 2:5, :], start=True, stop=False)
                mm(pb[:, P:], W1[:, 1, 1, :], a[:, 5:8, :], start=False, stop=True).then_inc(s["s_ready"], 1)
                pe.wait_ge(s["sv_ready"], b + 1)
                if b >= 2:
                    pe.wait_ge(s["z_step"], 4 * (b - 1))
                for m in range(4):
                    last = mm(ps[:, 4 + b % 2, m * P:(m + 1) * P], sv[:, b % 2, m, :], W2[:, min(m, 1), :],
                              start=True, stop=True)
                last.then_inc(s["o_ready"], 1)


INS = ("x", "src", "dst", "edge_attr_20", "edge_attr_3", "edge_weight",
       "L0_gnn_Ws_self", "L0_gnn_Ws_neigh", "L0_gnn_bs",
       "L1_gnn_W_in2f_s", "L1_gnn_W_in2f_v", "L1_gnn_Wf1", "L1_gnn_bf1", "L1_gnn_Wf2", "L1_gnn_bf2",
       "L1_gnn_W1_s", "L1_gnn_W1_v", "L1_gnn_W2_s", "L1_gnn_W2_v")


def kernel(**inputs):
    import numpy as np
    import concourse.bacc as bacc
    from concourse.bass_utils import run_bass_kernel_spmd

    nc = bacc.Bacc("TRN2", target_bir_lowering=False, num_devices=1)
    arrays, args = {}, []
    for name in INS:
        a = np.ascontiguousarray(inputs[name])
        arrays[f"in_{name}"] = a
        args.append(nc.dram_tensor(f"in_{name}", a.shape, mybir.dt.from_np(a.dtype), kind="ExternalInput").ap())
    shape = inputs["x"].shape
    out = nc.dram_tensor("out", shape, F32, kind="ExternalOutput").ap()
    gnn_resnorm(nc, *args, out)
    result = run_bass_kernel_spmd(nc, [arrays], core_ids=[0])
    return result.results[0]["out"]
```

```python
from contextlib import ExitStack

import concourse.bass as bass
from concourse import mybir

F32 = mybir.dt.float32
F32R = mybir.dt.float32r
BF16 = mybir.dt.bfloat16
I32 = mybir.dt.int32
I16 = mybir.dt.int16
ALU = mybir.AluOpType
ACT = mybir.ActivationFunctionType
AX = mybir.AxisListType

P = 128
LN_EPS = 1e-5
PI = 3.141592653589793
Y0 = (1.0 / (4.0 * PI)) ** 0.5
Y1 = (3.0 / (4.0 * PI)) ** 0.5

REC = 32
C_ONE, C_CUT, C_DIR, C_DST, C_OWN = 20, 21, 22, 25, 26
NF = C_ONE + 1

M_SCALED, M_SA, M_SB, M_VA, M_ALL = 0, 1, 2, 3, 6
N_SUMS = 8


def plan(n_nodes, n_edges):
    nb = -(-n_nodes // P)
    gt = 4
    gsz = gt * P
    groups = (n_edges + nb * (gsz - 1)) // gsz
    groups += 1 - groups % 2
    ep = max(k for k in range(1, P + 1) if n_edges % k == 0)
    return nb, gt, gsz, groups, ep, n_edges // ep


def over_groups(engine, groups, body):
    body(0, 0)
    body(1, 1)
    with engine.Fori(0, (groups - 5) // 2, 1) as i:
        body(2 * i + 2, 0)
        body(2 * i + 3, 1)
    body(groups - 3, 0)
    body(groups - 2, 1)
    body(groups - 1, 0)


def gnn_resnorm(nc, x, src, dst, edge_f, edge_r, edge_w, ws_self, ws_neigh, bs,
                w_in_s, w_in_v, wf1, bf1, w_f2, bf2, w1_s, w1_v, w2_s, w2_v, out):
    N, D = x.shape
    E = src.shape[0]
    LAYERS = ws_self.shape[0]
    C = w_in_s.shape[0]
    K = D // P
    NB, GT, GSZ, G, EP, ET = plan(N, E)
    T = G * GT
    NP = NB * P
    TAIL = N - (NB - 1) * P
    SH = GSZ.bit_length() - 1
    SLICES = [(s, min(s + 512, NP)) for s in range(0, NP, 512)]
    ST = 5
    assert C == P and D == 4 * P and ET % (2 * ST) == 0 and GSZ == 1 << SH and LAYERS == 3

    slots = nc.dram_tensor("edge_slots", (P * T, REC), F32, kind="Internal").ap()
    table = nc.dram_tensor("node_rows", (NP, D), F32, kind="Internal").ap()

    with ExitStack() as ctx:
        def sb(name, shape, dt=F32):
            return ctx.enter_context(nc.sbuf_tensor(name, shape, dt))

        def sem(name):
            return ctx.enter_context(nc.semaphore(name))

        def at(offset, name, shape, dt=F32):
            return nc.alloc_sbuf_tensor_at(name, shape, dt, offset=offset)

        ps = ctx.enter_context(nc.psum_tensor("ps", [P, 8, 512], F32))
        psf = ps[:, :, :].rearrange("p b n -> p (b n)")

        bias = sb("bias", [P, D])
        WIN = sb("WIN", [P, 2, P])
        WF1 = sb("WF1", [P, P], F32R)
        wf1_raw = sb("wf1_raw", [P, P])
        x_in = sb("x_in", [P, 4, D])
        tmp = sb("tmp", [P, 2, 2, D])
        bf_raw = tmp[0:3, 0, 0, :]
        bf_perm = tmp[0:3, 0, 1, :].rearrange("p (j f) -> p j f", j=4)
        bf_rest = tmp[0:3, 1, :, :]
        ones3 = sb("ones3", [3, P], BF16)
        sel3 = sb("sel3", [3, 3])
        ident = sb("ident", [P, P])
        lower = sb("lower", [P, P])
        ones = sb("ones", [P, P])
        half = sb("half", [P, 1])
        iota_n = sb("iota_n", [P, NP], I16)
        iota_g = sb("iota_g", [1, G, NB])
        dst_f = sb("dst_f", [P, T])
        own_f = sb("own_f", [P, T])
        dst_idx = sb("dst_idx", [P, T], I32)
        blocks_before = sb("blocks_before", [1, G])
        group_block = sb("group_block", [1, G], I32)
        pair_block = sb("pair_block", [1, G], I32)
        inv_deg = sb("inv_deg", [P, NB])
        stats = sb("stats", [P, NB, 6])
        mv = sb("mv", [P, NB, 2])
        rstd = sb("rstd", [P, 3, NB])
        gather_idx = sb("gather_idx", [P, 2, GT], I32)
        small = sb("small", [P, 10, NB])
        degree_row = sb("degree_row", [1, 1])
        many = sb("many", [1, 1], I32)
        stage = sb("stage", [EP, 2, ST, REC])
        stage_idx = sb("stage_idx", [EP, 2, ST], I32)
        bucket_end = sb("bucket_end", [EP, NB + 1])

        R_AT = -(-nc.sbuf_base // 64) * 64
        R_HT = R_AT + 4 * NB * NP
        R_G = R_HT + 8 * K * NP
        R_WS = R_G + 8 * NB * D
        R_WN = R_WS + 8 * K * D
        R_RAW = R_WN + 8 * K * D
        assert R_RAW + 4 * K * D + 4 * ET <= nc.sbuf_usable_end, (R_RAW + 4 * K * D + 4 * ET, nc.sbuf_usable_end)

        AT = at(R_AT, "AT", [P, NB * NP])
        AT_r = at(R_AT, "AT_r", [P, NB, NP], F32R)
        HT = at(R_HT, "HT", [P, 2, K, NP], F32R)
        GN = at(R_G, "GN", [P, 2, NB, D], F32R)
        Ws = at(R_WS, "Ws", [P, 2, K, D], F32R)
        Wn = at(R_WN, "Wn", [P, 2, K, D], F32R)
        raw = at(R_RAW, "raw", [P, K, D])

        pads = at(R_WS, "pads", [P, T // 4 * REC])
        n_buckets = NB * ET
        srt = at(R_AT, "srt", [EP, 4 * n_buckets + ET * REC])
        bucket = srt[:, 0:n_buckets]
        in_bucket = srt[:, n_buckets:2 * n_buckets]
        running = srt[:, 2 * n_buckets:3 * n_buckets]
        all_ones = srt[:, 3 * n_buckets:4 * n_buckets]
        E_rec = srt[:, 4 * n_buckets:4 * n_buckets + ET * REC]
        lists = at(R_G, "lists", [EP, 38 * ET])
        f_raw = lists[:, 18 * ET:38 * ET]
        ht = lists[:, 0:18 * ET]
        row_i = at(R_RAW + 4 * K * D, "row_i", [EP, ET], I32)[:, :]
        r_raw = ht[:, 0:3 * ET]
        r_sq = ht[:, 3 * ET:6 * ET]
        dst_i = ht[:, 6 * ET:7 * ET].bitcast(I32)
        src_i = ht[:, 7 * ET:8 * ET].bitcast(I32)
        w_raw = ht[:, 8 * ET:9 * ET]
        blk_i = ht[:, 9 * ET:10 * ET].bitcast(I32)
        blk_f = ht[:, 10 * ET:11 * ET]
        place_f = ht[:, 11 * ET:12 * ET]
        place_i = ht[:, 12 * ET:13 * ET].bitcast(I32)
        place_lo = ht[:, 13 * ET:14 * ET].bitcast(I32)
        place_hi = ht[:, 14 * ET:15 * ET].bitcast(I32)
        norm = ht[:, 15 * ET:18 * ET]

        SHARE = T // 2
        share = at(R_WS, "share", [P, SHARE * REC])
        oh_dst = at(R_WN, "oh_dst", [P, 4, NP], BF16)
        oh_own = at(R_WN + 8 * NP, "oh_own", [P, 4, P], BF16)
        deg_part = at(R_WN, "deg_part", [P, NP])[:, :]

        NC = 1024
        counts_sb = x_in[:, :, :].rearrange("p u n -> p (u n)")

        X = at(R_WN, "X", [P, NB, D])
        XT = at(R_HT + 4 * K * NP, "XT", [P, K, NP])
        TAB = at(R_AT + 4 * K * NP, "TAB", [P, K, NP])

        NA = N_SUMS * P
        agg = at(R_AT, "agg", [P, NB * NA])
        o = R_AT + 4 * NB * NA
        WF = at(o, "WF", [P, 2, 4, P], F32R)
        W1 = at(o + 4096, "W1", [P, 2, 2, P])
        W2 = at(o + 6144, "W2", [P, 2, P])
        bf3 = at(o + 7168, "bf3", [3, 4 * P], BF16)
        bf_part = at(o + 8192, "bf_part", [3, 2, 4 * P], BF16)
        rec = at(R_G, "rec", [P, T * REC])
        o = R_G + 4 * T * REC
        wf2_raw = at(o, "wf2_raw", [P, 6 * P])
        wf2 = at(o + 3072, "wf2_scaled", [P, 4, P])
        wf1_part = at(o + 5120, "wf1_part", [P, 2, P], F32R)
        rows = at(R_WS, "rows", [P, 2, GT, D])
        o = R_HT
        hid = at(o, "hid", [P, 2, 2, GSZ], F32R)
        o += 16 * GSZ
        h_full = at(o, "h_full", [P, GSZ])[:, :]
        o += 4 * GSZ
        f_t = at(o, "f_t", [P, GSZ], F32R)[:, :]
        o += 4 * GSZ
        h_exp, h_ln = (at(o + 4 * GSZ * i, f"hid_{i}", [P, GSZ])[:, :] for i in range(2))
        o += 8 * GSZ
        h_abs = x_in[:, :, 3 * P:]
        rec_f = at(o, "rec_f", [P, GT, 4, 32])
        o += 4 * GT * P
        rec_hi = at(o, "rec_hi", [P, GT, NF], F32R)
        o += -(-4 * GT * NF // 64) * 64
        assert o <= R_HT + 4 * K * NP
        vb = at(o, "vb", [P, 4, 3, P])
        vb_hi = at(o + 48 * P, "vb_hi", [P, 4, 3, P], F32R)
        vb_lo = at(o + 96 * P, "vb_lo", [P, 4, 3, P], F32R)
        o += 144 * P
        hot = at(o, "hot", [P, 4, P], F32R)
        o += 16 * P
        dots = x_in[:, :, 0:3 * P].rearrange("p u (i f) -> p u i f", i=3)
        msg = at(R_G + 4 * T * REC, "msg", [P, 4, M_ALL, P])
        assert 4 * T * REC + 16 * M_ALL * P <= 8 * NB * D
        assert o <= R_G

        half_agg = NB * NA // 2
        assert half_agg == K * NP

        agg_t = at(R_HT, "agg_t", [P, 2, 8, P])
        sv = at(R_HT + 8192, "sv", [P, 2, 4, P])
        s_tmp = at(R_HT + 12288, "s_tmp", [P, 2, 3, P])

        s = {name: sem(name) for name in (
            "edges_loaded", "x_loaded_0", "x_loaded_1", "x_loaded_2", "x_loaded_3", "weights_loaded",
            "edge_weights_loaded", "raw_loaded", "bias_loaded", "w_hi", "w_split", "pads_written",
            "consts_made", "zeroed", "sort_step", "counts_ready", "blocks_known", "totals_ready", "edge_copied", "norm_sq",
            "norm_ready", "staged", "scattered_0", "scattered_1", "rec_loaded", "rec_split",
            "one_hots", "tile_summed", "block_added", "counts_copied", "counts_added", "deg_part", "deg_ready", "inv_ready",
            "max_ready", "max_turned", "many_ready", "at_ready", "h_turned", "ht_hi", "ht_done", "g_ready", "g_hi",
            "g_done", "dense_ready", "dense_step", "h_ready", "z_ready", "x_turned", "xt_copied", "var_ready", "std_ready", "x1_ready", "table_ready", "table_copied",
            "table_written", "prep", "staged_f", "f_turned", "ft_copied", "hid_ready",
            "hid_abs", "hid_exp", "hid_ln", "hid_done", "w_ready", "msg_ready", "dot_step", "dot_begun", "act_turns", "hid_full", "hid_hi", "vb_hi", "vb_lo", "rec_hi",
            "va_ready", "edges_summed", "agg_added", "agg_zeroed", "filter_prep", "idx_copied",
            "turns", "agg_turned", "agg_copied", "s_ready", "s_step", "v_copied", "sv_ready", "o_ready",
            "z_step", "out_ready", "written")}

        gathered = [[sem(f"gathered_{h}_{k}") for k in range(GT)] for h in range(2)]

        block = ctx.enter_context(nc.Block())

        def atleast(eng, semaphore, value):
            if not isinstance(value, int) or value > 0:
                eng.wait_ge(semaphore, value)

        class Chain:

            def __init__(self, eng, semaphore):
                self.eng, self.semaphore, self.n = eng, semaphore, 0

            def __call__(self, instruction):
                instruction.then_inc(self.semaphore, 1)
                self.n += 1
                self.eng.wait_ge(self.semaphore, self.n)

        PREPARED = 11
        SORTED = 24
        HALVES = ET // ST

        @block.sync
        def _(sp):
            sp.dma_start(dst_i, dst.rearrange("(p t) -> p t", p=EP)).then_inc(s["edges_loaded"], 16)
            sp.dma_start(src_i, src.rearrange("(p t) -> p t", p=EP)).then_inc(s["edges_loaded"], 16)
            sp.dma_start(r_raw, edge_r.rearrange("(p t) c -> p (t c)", p=EP)).then_inc(s["edges_loaded"], 16)
            sp.dma_start(w_raw, edge_w.rearrange("(p t) -> p t", p=EP)).then_inc(s["edges_loaded"], 16)
            sp.dma_start(f_raw, edge_f.rearrange("(p t) c -> p (t c)", p=EP)).then_inc(s["edges_loaded"], 16)
            sp.dma_start(raw[:, :, :], ws_neigh[0, :, :].rearrange("(k p) n -> p k n", p=P)).then_inc(s["raw_loaded"], 16)

            def load_x(b, load):
                n = P if b < NB - 1 else TAIL
                sp.dma_start(x_in[0:n, load % 4, :], x[b * P:b * P + n, :]).then_inc(s[f"x_loaded_{load % 4}"], 16)

            for b in range(4):
                load_x(b, b)
            sp.wait_ge(s["zeroed"], 2)
            slot_rows = slots.rearrange("(p t) c -> p (t c)", p=P)
            n = T // 4 * REC
            for i in range(4):
                sp.dma_start(slot_rows[:, i * n:(i + 1) * n], pads[:, :]).then_inc(s["pads_written"], 16)
            sp.wait_ge(s["zeroed"], 3)
            for buf, w in ((WIN[:, 0, :], w_in_s), (WIN[:, 1, :], w_in_v), *((wf1_raw[q:q + NF - 1, :], wf1) for q in range(0, P, 32)),
                           *((wf1_raw[q + NF - 1:q + NF, :], bf1.rearrange("(a f) -> a f", a=1))
                             for q in range(0, P, 32))):
                sp.dma_start(buf, w).then_inc(s["weights_loaded"], 16)
            sp.dma_start(bias[:, :], bs[0:1, :].to_broadcast([P, D])).then_inc(s["bias_loaded"], 16)
            for b in range(4, NB):
                sp.wait_ge(s["h_turned"], b - 3)
                load_x(b, b)
            sp.wait_ge(s["w_split"], 1)
            sp.dma_start(raw[:, :, :], ws_self[0, :, :].rearrange("(k p) n -> p k n", p=P)).then_inc(s["raw_loaded"], 16)
            sp.wait_ge(s["scattered_0"], 16 * ST * (HALVES // 2))
            sp.wait_ge(s["scattered_1"], 16 * ST * (HALVES // 2))
            for i in range(2):
                sp.wait_ge(s["rec_split"], 2 * i)
                sp.dma_start(share[:, :], slot_rows[:, i * SHARE * REC:(i + 1) * SHARE * REC]).then_inc(s["rec_loaded"], 16)
            with sp.Fori(0, LAYERS - 1, 1) as i:
                for u, w in ((0, ws_neigh), (1, ws_self)):
                    sp.wait_ge(s["w_split"], 2 * i + 2 + u)
                    sp.dma_start(raw[:, :, :], w[bass.ds(i + 1, 1), :, :].rearrange("a (k p) n -> p (a k) n", p=P)
                                 ).then_inc(s["raw_loaded"], 16)
                sp.wait_ge(s["dense_step"], 2 * NB * i + 2 * NB)
                sp.dma_start(bias[:, :], bs[bass.ds(i + 1, 1), :].to_broadcast([P, D])).then_inc(s["bias_loaded"], 16)
            for b in range(4):
                load_x(b, NB + b)
            for b in range(4, NB):
                sp.wait_ge(s["z_ready"], b - 3)
                load_x(b, NB + b)
            sp.wait_ge(s["dense_ready"], LAYERS * NB)
            for buf, w in ((rec[:, :], slot_rows), (wf2_raw[:, :], w_f2),
                           (W1[:, 0, :, :], w1_s.rearrange("(f u) c -> f u c", u=2)),
                           (W1[:, 1, :, :], w1_v.rearrange("(f u) c -> f u c", u=2)),
                           (W2[:, 0, :], w2_s), (W2[:, 1, :], w2_v)):
                sp.dma_start(buf, w).then_inc(s["edge_weights_loaded"], 16)
            sp.wait_ge(s["z_ready"], NB)
            sp.dma_start(bf_raw, bf2[0:4 * P].rearrange("(a f) -> a f", a=1).to_broadcast([3, 4 * P])
                         ).then_inc(s["edge_weights_loaded"], 16)
            for b in range(NB):
                sp.wait_ge(s["table_copied"], b + 1)
                sp.dma_start(table[b * P:(b + 1) * P, :],
                             TAB[:, :, b * P:(b + 1) * P]).then_inc(s["table_written"], 16)
            for b in range(NB):
                n = P if b < NB - 1 else TAIL
                sp.wait_ge(s["out_ready"], b + 1)
                sp.dma_start(out[b * P:b * P + n, :], X[0:n, b, :]).then_inc(s["written"], 16)
            sp.wait_ge(s["written"], 16 * NB)

        @block.gpsimd
        def _(pool):
            bk = bucket.rearrange("p (b t) -> p b t", b=NB)
            pool.iota(bk, pattern=[[1, NB], [0, ET]], base=0, channel_multiplier=0,
                      allow_small_or_imprecise_dtypes=True).then_inc(s["consts_made"], 1)
            pool.memset(ident[:, :], 0.0).then_inc(s["consts_made"], 1)
            pool.memset(lower[:, :], 1.0).then_inc(s["consts_made"], 1)
            pool.memset(sel3[:, :], 0.0).then_inc(s["consts_made"], 1)
            pool.wait_ge(s["consts_made"], 4)
            pool.affine_select(out=ident[:, :], in_=ident[:, :], compare_op=ALU.not_equal, fill=1.0, base=0,
                               pattern=[[-1, P]], channel_multiplier=1).then_inc(s["consts_made"], 1)
            pool.affine_select(out=lower[:, :], in_=lower[:, :], compare_op=ALU.is_gt, fill=0.0, base=0,
                               pattern=[[1, P]], channel_multiplier=-1).then_inc(s["consts_made"], 1)
            pool.affine_select(out=sel3[:, :], in_=sel3[:, :], compare_op=ALU.not_equal, fill=1.0, base=0,
                               pattern=[[-1, 3]], channel_multiplier=1).then_inc(s["consts_made"], 1)
            pool.iota(iota_g[:, :, :], pattern=[[1, G], [0, NB]], base=0, channel_multiplier=0,
                      allow_small_or_imprecise_dtypes=True).then_inc(s["consts_made"], 1)
            pool.iota(iota_n[:, :], pattern=[[1, NP]], base=0, channel_multiplier=0).then_inc(s["consts_made"], 1)

            pool.wait_ge(s["pads_written"], 64)
            with pool.Fori(0, HALVES // 2, 1) as i:
                for h in range(2):
                    pool.wait_ge(s["staged"], 4 * i + 2 * h + 2)
                    pool.sem_inc(s["turns"], 1)
                    for k in range(ST):
                        pool.indirect_dma_start(
                            out=slots[:, :], out_offset=bass.IndirectOffsetOnAxis(ap=stage_idx[:, h, k:k + 1], axis=0),
                            in_=stage[:, h, k, :], in_offset=None).then_inc(s[f"scattered_{h}"], 16)

            pool.wait_ge(s["blocks_known"], 1)
            pool.wait_ge(s["prep"], 1)

            def add_counts(g, h):
                pool.wait_ge(s["counts_copied"], g + 1)
                atleast(pool, s["counts_added"], g)
                pool.sem_inc(s["turns"], 1)
                b = nc.gpsimd.value_load(group_block[0:1, bass.ds(g, 1)], min_val=0, max_val=NB - 1)
                a = AT[:, bass.ds(b * NP, NC)]
                pool.tensor_tensor(a, a, counts_sb[:, h * NC:(h + 1) * NC], ALU.add).then_inc(s["counts_added"], 1)

            over_groups(pool, G, add_counts)

            pool.wait_ge(s["rec_split"], 5)

            def copy_index(g, h):
                atleast(pool, s["msg_ready"], 16 * (g - 1))
                pool.tensor_copy(gather_idx[:, h, :], dst_idx[:, bass.ds(g * GT, GT)]).then_inc(s["idx_copied"], 1)
                pool.wait_ge(s["idx_copied"], g + 1)
                pool.sem_inc(s["turns"], 1)

            def gather(h, k):
                pool.indirect_dma_start(
                    out=rows[:, h, k, :], out_offset=None, in_=table[:, :],
                    in_offset=bass.IndirectOffsetOnAxis(ap=gather_idx[:, h, k:k + 1], axis=0),
                ).then_inc(gathered[h][k], 16)

            def edge_group(g, h):
                left = G - 1 - g if isinstance(g, int) else G
                if left >= 1:
                    copy_index(g + 1, 1 - h)
                for k in range(GT):
                    n = g * GT + k
                    if left >= 1:
                        gather(1 - h, k)
                    if k == 1 and left >= 2:
                        pool.wait_ge(s["rec_hi"], 2 * (g + 2) + 1)
                        split_features(g + 2)
                    pool.wait_ge(s["vb_hi"], n + 1)
                    atleast(pool, s["edges_summed"], n - 3)
                    pool.tensor_tensor(vb_lo[:, k, :, :], vb[:, k, :, :], vb_hi[:, k, :, :].bitcast(F32),
                                       ALU.subtract).then_inc(s["vb_lo"], 1)
                    if k == 1 and left >= 1:
                        split_hidden(g + 1, 1 - h)

            def split_features(g):
                pool.tensor_tensor(rec_f[:, :, 2:4, 0:NF],
                                   rec[:, bass.ds(g * GT * REC, GT * REC)].rearrange("p (k u c) -> p k u c", u=1, c=REC)
                                   [:, :, :, 0:NF].to_broadcast([P, GT, 2, NF]),
                                   rec_hi[:, :, :].rearrange("p k (u c) -> p k u c", u=1).bitcast(F32)
                                   .to_broadcast([P, GT, 2, NF]), ALU.subtract).then_inc(s["staged_f"], 1)

            def split_hidden(g, h):
                pool.wait_ge(s["hid_hi"], g + 1)
                pool.tensor_tensor(hid[:, h, 1, :], h_full, hid[:, h, 0, :].bitcast(F32), ALU.subtract
                                   ).then_inc(s["hid_done"], 1)

            pool.wait_ge(s["dense_ready"], LAYERS * NB)
            pool.memset(agg[:, 0:half_agg], 0.0).then_inc(s["agg_zeroed"], 1)
            pool.wait_ge(s["rec_hi"], 1)
            split_features(0)
            copy_index(0, 0)
            pool.wait_ge(s["table_written"], 16 * NB)
            for k in range(GT):
                gather(0, k)
                if k == 1:
                    pool.wait_ge(s["rec_hi"], 3)
                    split_features(1)
            split_hidden(0, 0)
            over_groups(pool, G, edge_group)

        @block.scalar
        def _(act):
            act.preload_act_table_set("natural_log_exp_and_others")
            er = E_rec.rearrange("p (t c) -> p t c", c=REC)
            act.wait_ge(s["edges_loaded"], 80)
            act.activation(er[:, :, C_DST], dst_i, ACT.Copy).then_inc(s["edge_copied"], 1)
            act.activation(er[:, :, C_CUT], w_raw, ACT.Copy).then_inc(s["edge_copied"], 1)
            act.activation(er[:, :, 0:20], f_raw.rearrange("p (t c) -> p t c", c=20), ACT.Copy).then_inc(s["edge_copied"], 1)
            act.wait_ge(s["norm_sq"], 1)
            act.activation(norm[:, 0:ET], norm[:, ET:2 * ET], ACT.Sqrt).then_inc(s["norm_ready"], 1)
            act.preload_act_table_set("natural_log_exp_and_others")

            def w_hi(w, n):
                act.wait_ge(s["raw_loaded"], 16 * (n + 1))
                act.activation(w[:, 0, :, :], raw[:, :, :], ACT.Copy).then_inc(s["w_hi"], 1)

            def ht_hi(b, done):
                act.wait_ge(s["h_turned"], done + 1)
                act.activation(HT[:, 0, :, b * P:(b + 1) * P], ps[:, b % 2, :].rearrange("p (k n) -> p k n", k=K),
                               ACT.Copy).then_inc(s["ht_hi"], 1)

            def g_hi(b, done):
                act.wait_ge(s["g_ready"], done + 1)
                act.activation(GN[:, 0, b, :], ps[:, 2 + b % 2, :], ACT.Copy).then_inc(s["g_hi"], 1)

            w_hi(Wn, 0)
            act.wait_ge(s["sort_step"], SORTED)
            for b in range(NB):
                ht_hi(b, b)
                g_hi(b, b)
            def copy_counts(g, h):
                act.wait_ge(s["tile_summed"], GT * (g + 1))
                atleast(act, s["counts_added"], g - 1)
                act.activation(counts_sb[:, h * NC:(h + 1) * NC], psf[:, 1536 * h:1536 * h + NC], ACT.Copy
                               ).then_inc(s["counts_copied"], 1)

            act.wait_ge(s["rec_split"], 5)
            w_hi(Ws, 1)
            over_groups(act, G, copy_counts)
            act.wait_ge(s["deg_ready"], 1)

            with act.Fori(0, LAYERS - 1, 1) as i:
                w_hi(Wn, 2 * i + 2)
                for b in range(NB):
                    act.wait_ge(s["dense_step"], 2 * NB * i + 2 * b + 2)
                    act.activation(tmp[:, b % 2, 0, :], tmp[:, b % 2, 1, :], ACT.Relu).then_inc(s["h_ready"], 1)
                    if b >= 1:
                        ht_hi(b - 1, NB * i + NB + b - 1)
                ht_hi(NB - 1, NB * i + 2 * NB - 1)
                w_hi(Ws, 2 * i + 3)
                for b in range(NB):
                    g_hi(b, NB * i + NB + b)

            act.wait_ge(s["var_ready"], 1)
            act.activation(rstd[:, 1, :], rstd[:, 0, :], ACT.Sqrt).then_inc(s["std_ready"], 1)
            act.preload_act_table_set("natural_log_exp_and_others")
            def stage_features(g):
                atleast(act, s["f_turned"], g)
                atleast(act, s["staged_f"], g)
                act.activation(rec_hi[:, :, :],
                               rec[:, bass.ds(g * GT * REC, GT * REC)].rearrange("p (k c) -> p k c", c=REC)[:, :, 0:NF],
                               ACT.Copy).then_inc(s["rec_hi"], 1)
                act.wait_ge(s["rec_hi"], 2 * g + 1)
                act.activation(rec_f[:, :, 0:2, 0:NF], rec_hi[:, :, :].rearrange("p k (u c) -> p k u c", u=1)
                               .bitcast(F32).to_broadcast([P, GT, 2, NF]), ACT.Copy).then_inc(s["rec_hi"], 1)

            for b in range(NB + 1):
                if b < NB:
                    act.wait_ge(s["x_turned"], b + 1)
                    act.activation(XT[:, :, b * P:(b + 1) * P], ps[:, b % 2, :].rearrange("p (k n) -> p k n", k=K),
                                   ACT.Copy).then_inc(s["xt_copied"], 1)
                if b == NB:
                    act.wait_ge(s["edge_weights_loaded"], 16 * 7)
                    act.wait_ge(s["filter_prep"], 7)
                    stage_features(0)
                if b >= 1:
                    act.wait_ge(s["table_ready"], b)
                    act.activation(TAB[:, :, (b - 1) * P:b * P],
                                   ps[:, 2 + (b - 1) % 2, :].rearrange("p (k n) -> p k n", k=K), ACT.Copy
                                   ).then_inc(s["table_copied"], 1)

            def copy_features(g):
                act.wait_ge(s["f_turned"], g + 1)
                atleast(act, s["hid_ready"], g)
                act.activation(f_t, ps[:, 0, :], ACT.Copy).then_inc(s["ft_copied"], 1)

            def hid_1(g):
                act.wait_ge(s["hid_ready"], g + 1)
                act.activation(h_abs, ps[:, 1, :].rearrange("p (u f) -> p u f", f=P), ACT.Abs).then_inc(s["hid_abs"], 1)
                act.wait_ge(s["hid_abs"], g + 1)
                act.activation(h_exp.rearrange("p (u f) -> p u f", f=P), h_abs, ACT.Exp, scale=-1.0).then_inc(s["hid_exp"], 1)

            def hid_2(g):
                act.wait_ge(s["hid_exp"], g + 1)
                act.activation(h_ln, h_exp, ACT.Ln, bias=half[:, :], scale=0.5).then_inc(s["hid_ln"], 1)

            def hid_hi(g, h):
                act.wait_ge(s["hid_full"], g + 1)
                atleast(act, s["w_ready"], GT * (g - 1))
                act.activation(hid[:, h, 0, :], h_full, ACT.Copy).then_inc(s["hid_hi"], 1)

            def gathered_all(g, h):
                return 16 * (g // 2 + 1) if isinstance(g, int) else 8 * g + (16 if h == 0 else 8)

            def begin_dot(g, h, k):
                n = g * GT + k
                act.wait_ge(gathered[h][k], gathered_all(g, h))
                act.sem_inc(s["act_turns"], 1)
                act.activation(dots[:, k, 0, :], rows[:, h, k, P:2 * P], ACT.Copy,
                               scale=rec[:, bass.ds(n * REC + C_DIR, 1)]).then_inc(s["dot_begun"], 1)

            def direct(g, h, k):
                n = g * GT + k
                act.wait_ge(s["msg_ready"], 4 * n + 2)
                act.activation(vb_hi[:, k, :, :], vb[:, k, :, :], ACT.Copy).then_inc(s["vb_hi"], 1)
                for i in range(3):
                    act.activation(msg[:, k, M_VA + i, :], msg[:, k, M_SCALED, :], ACT.Copy,
                                   scale=rec[:, bass.ds(n * REC + C_DIR + i, 1)]).then_inc(s["va_ready"], 1)

            def group(g, h):
                left = G - 1 - g if isinstance(g, int) else G
                direct(g, h, 0)
                begin_dot(g, h, 2)
                if left >= 1:
                    hid_2(g + 1)
                if left >= 2:
                    stage_features(g + 2)
                direct(g, h, 1)
                begin_dot(g, h, 3)
                if left >= 1:
                    hid_hi(g + 1, 1 - h)
                direct(g, h, 2)
                if left >= 1:
                    begin_dot(g + 1, 1 - h, 0)
                if left >= 2:
                    copy_features(g + 2)
                direct(g, h, 3)
                if left >= 1:
                    begin_dot(g + 1, 1 - h, 1)
                if left >= 2:
                    hid_1(g + 2)

            copy_features(0)
            stage_features(1)
            hid_1(0)
            hid_2(0)
            hid_hi(0, 0)
            copy_features(1)
            begin_dot(0, 0, 0)
            begin_dot(0, 0, 1)
            hid_1(1)
            over_groups(act, G, group)

            def copy_agg(b):
                act.wait_ge(s["agg_turned"], b + 1)
                if b >= 2:
                    act.wait_ge(s["s_ready"], b - 1)
                for u in range(2):
                    act.activation(agg_t[:, b % 2, 4 * u:4 * u + 4, :],
                                   ps[:, u, :].rearrange("p (m n) -> p m n", m=4), ACT.Copy).then_inc(s["agg_copied"], 1)

            copy_agg(0)
            for b in range(NB):
                if b + 1 < NB:
                    copy_agg(b + 1)
                act.wait_ge(s["s_ready"], b + 1)
                if b >= 2:
                    act.wait_ge(s["o_ready"], b - 1)
                    act.wait_ge(s["sv_ready"], b - 1)
                pb = ps[:, 2 + b % 2, :].rearrange("p (m n) -> p m n", m=4)
                act.activation(s_tmp[:, b % 2, 0, :], pb[:, 0, :], ACT.Abs).then_inc(s["s_step"], 1)
                act.activation(sv[:, b % 2, 1:4, :], pb[:, 1:4, :], ACT.Copy).then_inc(s["v_copied"], 1)
                act.wait_ge(s["s_step"], 3 * b + 1)
                act.activation(s_tmp[:, b % 2, 1, :], s_tmp[:, b % 2, 0, :], ACT.Exp, scale=-1.0).then_inc(s["s_step"], 1)
                act.wait_ge(s["s_step"], 3 * b + 2)
                act.activation(s_tmp[:, b % 2, 2, :], s_tmp[:, b % 2, 1, :], ACT.Ln, bias=half[:, :], scale=0.5
                               ).then_inc(s["s_step"], 1)
            act.wait_ge(s["var_ready"], 2)
            act.activation(rstd[:, 1, :], rstd[:, 0, :], ACT.Sqrt).then_inc(s["std_ready"], 1)

        @block.vector
        def _(dve):
            v = nc.vector
            v.memset(pads[:, :], 0.0).then_inc(s["zeroed"], 1)
            dve.wait_ge(s["zeroed"], 1)
            v.memset(pads[:, :].rearrange("p (t c) -> p t c", c=REC)[:, :, C_OWN], -1.0).then_inc(s["zeroed"], 1)
            v.memset(wf1_raw[:, :], 0.0).then_inc(s["zeroed"], 1)
            v.memset(ones[:, :], 1.0).then_inc(s["zeroed"], 1)
            v.memset(half[:, :], 0.5).then_inc(s["zeroed"], 1)
            v.memset(ones3[:, :], 1.0).then_inc(s["zeroed"], 1)
            v.memset(bucket_end[:, 0:1], 0.0).then_inc(s["zeroed"], 1)
            er = E_rec.rearrange("p (t c) -> p t c", c=REC)
            v.memset(er[:, :, C_ONE], 1.0).then_inc(s["zeroed"], 1)
            v.memset(er[:, :, C_OWN + 1:REC], 0.0).then_inc(s["zeroed"], 1)

            step = Chain(dve, s["sort_step"])
            step(v.memset(all_ones, 1.0))
            dve.wait_ge(s["edges_loaded"], 80)
            dve.wait_ge(s["consts_made"], 1)
            step(v.tensor_scalar(blk_i, src_i, 7, None, ALU.arith_shift_right))
            step(v.tensor_copy(blk_f, blk_i))
            step(v.scalar_tensor_tensor(out=er[:, :, C_OWN], in0=blk_f, scalar=-float(P), in1=src_i,
                                        op0=ALU.mult, op1=ALU.add))
            pbt = lambda a: a.rearrange("p (b t) -> p b t", b=NB)
            step(v.tensor_tensor(pbt(in_bucket), blk_f.rearrange("p (a t) -> p a t", a=1).to_broadcast([EP, NB, ET]),
                                 pbt(bucket), ALU.is_equal))
            step(v.tensor_tensor_scan(running, all_ones, in_bucket, 0.0, ALU.mult, ALU.add))
            dve.wait_ge(s["zeroed"], 7)
            step(v.tensor_copy(bucket_end[:, 1:NB + 1], pbt(running)[:, :, ET - 1]))
            counts = small[0:EP, 0, :]
            v.tensor_tensor(counts, bucket_end[:, 1:NB + 1], bucket_end[:, 0:NB], ALU.subtract).then_inc(s["counts_ready"], 1)
            r3 = lambda a: a.rearrange("p (t c) -> p t c", c=3)
            step(v.tensor_tensor(r_sq, r_raw, r_raw, ALU.mult))
            v.tensor_reduce(norm[:, ET:2 * ET], r3(r_sq), axis=AX.X, op=ALU.add).then_inc(s["norm_sq"], 1)
            dve.wait_ge(s["totals_ready"], 1)
            g_i, g_s = small[:, 1, :].bitcast(I32), small[:, 2, :].bitcast(I32)
            g_f, g_end, g_start = small[:, 3, :], small[:, 4, :], small[:, 5, :]
            first, base = small[0:EP, 6, :], small[0:EP, 7, :]
            step(v.tensor_scalar(g_i, ps[:, 7, 16:16 + NB], float(GSZ - 1), None, ALU.add))
            step(v.tensor_scalar(g_s, g_i, SH, None, ALU.arith_shift_right))
            step(v.tensor_copy(g_f, g_s))
            step(v.tensor_tensor_scan(g_end, ones[:, 0:NB], g_f, 0.0, ALU.mult, ALU.add))
            step(v.tensor_tensor(g_start, g_end, g_f, ALU.subtract))
            step(v.scalar_tensor_tensor(out=first, in0=g_start[0:EP, :], scalar=float(GSZ), in1=ps[0:EP, 7, 0:NB],
                                        op0=ALU.mult, op1=ALU.add))
            step(v.scalar_tensor_tensor(out=base, in0=first, scalar=-1.0, in1=bucket_end[:, 0:NB],
                                        op0=ALU.add, op1=ALU.subtract))
            step(v.tensor_tensor(pbt(running), pbt(running),
                                 base.rearrange("p (b a) -> p b a", a=1).to_broadcast([EP, NB, ET]), ALU.add))
            step(v.tensor_tensor(running, running, in_bucket, ALU.mult))
            step(v.tensor_reduce(place_f, running.rearrange("p (b t) -> p t b", b=NB), axis=AX.X, op=ALU.add))
            step(v.tensor_copy(place_i, place_f))
            step(v.tensor_scalar(place_lo, place_i, P - 1, None, ALU.bitwise_and))
            step(v.tensor_scalar(place_hi, place_i, 7, None, ALU.arith_shift_right))
            step(v.scalar_tensor_tensor(out=row_i, in0=place_lo, scalar=float(T), in1=place_hi,
                                        op0=ALU.mult, op1=ALU.add))
            dve.wait_ge(s["norm_ready"], 1)
            step(v.reciprocal(norm[:, 2 * ET:3 * ET], norm[:, 0:ET]))
            step(v.tensor_tensor(er[:, :, C_DIR:C_DIR + 3], r3(r_raw),
                                 norm[:, 2 * ET:3 * ET].rearrange("p (t a) -> p t a", a=1).to_broadcast([EP, ET, 3]), ALU.mult))
            dve.wait_ge(s["edge_copied"], 3)
            dve.wait_ge(s["zeroed"], 9)
            assert step.n == SORTED

            def w_lo(w, n):
                dve.wait_ge(s["w_hi"], n + 1)
                v.tensor_tensor(w[:, 1, :, :], raw[:, :, :], w[:, 0, :, :].bitcast(F32), ALU.subtract).then_inc(s["w_split"], 1)

            def ht_lo(b, u, done):
                dve.wait_ge(s["ht_hi"], done + 1)
                v.tensor_tensor(HT[:, 1, :, bass.ds(b * P, P)], ps[:, u, :].rearrange("p (k n) -> p k n", k=K),
                                HT[:, 0, :, bass.ds(b * P, P)].bitcast(F32), ALU.subtract).then_inc(s["ht_done"], 1)

            def g_lo(b, u, done):
                dve.wait_ge(s["g_hi"], done + 1)
                v.tensor_tensor(GN[:, 1, bass.ds(b, 1), :], ps[:, 2 + u:3 + u, :],
                                GN[:, 0, bass.ds(b, 1), :].bitcast(F32), ALU.subtract).then_inc(s["g_done"], 1)

            def stage_edges(i, h):
                atleast(dve, s[f"scattered_{h}"], 16 * ST * i)
                v.tensor_copy(stage[:, h, :, :].rearrange("p k c -> p (k c)"),
                              E_rec[:, bass.ds((i * 2 + h) * (ST * REC), ST * REC)]).then_inc(s["staged"], 1)
                v.tensor_copy(stage_idx[:, h, :], row_i[:, bass.ds((i * 2 + h) * ST, ST)]).then_inc(s["staged"], 1)

            stage_edges(0, 0)
            stage_edges(0, 1)
            w_lo(Wn, 0)
            with v.Fori(0, NB // 2, 1) as i:
                for h in range(2):
                    stage_edges(i + 1, h)
                    ht_lo(2 * i + h, h, 2 * i + h)
                    g_lo(2 * i + h, h, 2 * i + h)
            with v.Fori(NB // 2 + 1, HALVES // 2, 1) as i:
                for h in range(2):
                    stage_edges(i, h)

            dve.wait_ge(s["consts_made"], 9)
            step(v.tensor_tensor(iota_g[:, :, :], iota_g[:, :, :],
                                 g_end[0:1, :].rearrange("p (a b) -> p a b", a=1).to_broadcast([1, G, NB]), ALU.is_ge))
            step(v.tensor_reduce(blocks_before[:, :], iota_g[:, :, :], axis=AX.X, op=ALU.add))
            v.tensor_scalar(group_block[:, :], blocks_before[:, :], float(NB - 1), None, ALU.min).then_inc(s["blocks_known"], 1)
            dve.wait_ge(s["blocks_known"], 1)
            assert NB <= 16
            step(v.scalar_tensor_tensor(out=pair_block[:, 0:G - 1], in0=group_block[:, 1:G], scalar=16.0,
                                        in1=group_block[:, 0:G - 1], op0=ALU.mult, op1=ALU.add))

            dve.wait_ge(s["scattered_0"], 16 * ST * (HALVES // 2))
            dve.wait_ge(s["scattered_1"], 16 * ST * (HALVES // 2))
            v.memset(AT[:, :], 0.0).then_inc(s["prep"], 1)
            sh = share[:, :].rearrange("p (t c) -> p t c", c=REC)
            for i in range(2):
                dve.wait_ge(s["rec_loaded"], 16 * (i + 1))
                v.tensor_copy(dst_f[:, i * SHARE:(i + 1) * SHARE], sh[:, :, C_DST]).then_inc(s["rec_split"], 1)
                v.tensor_copy(own_f[:, i * SHARE:(i + 1) * SHARE], sh[:, :, C_OWN]).then_inc(s["rec_split"], 1)
            dve.wait_ge(s["rec_split"], 4)
            v.tensor_copy(dst_idx[:, :], dst_f[:, :]).then_inc(s["rec_split"], 1)
            dve.wait_ge(s["prep"], 1)
            w_lo(Ws, 1)
            dve.wait_ge(s["g_ready"], NB)

            def one_hots(g):
                for k in range(GT):
                    t = g * GT + k
                    atleast(dve, s["tile_summed"], t - 3)
                    v.tensor_scalar(oh_dst[:, k % 4, :], iota_n[:, :], dst_f[:, bass.ds(t, 1)], None,
                                    ALU.is_equal).then_inc(s["one_hots"], 1)
                    v.tensor_scalar(oh_own[:, k % 4, :], iota_n[:, 0:P], own_f[:, bass.ds(t, 1)], None,
                                    ALU.is_equal).then_inc(s["one_hots"], 1)

            def add_block(g, h):
                dve.wait_ge(s["tile_summed"], GT * (g + 1))
                atleast(dve, s["block_added"], g)
                b = v.value_load(group_block[0:1, bass.ds(g, 1)], min_val=0, max_val=NB - 1)
                a = AT[:, bass.ds(b * NP + NC, NP - NC)]
                v.tensor_tensor(a, a, psf[:, 1536 * h + NC:1536 * h + NP], ALU.add).then_inc(s["block_added"], 1)

            def count_group(g, h):
                one_hots(g)
                if not (isinstance(g, int) and g == 0):
                    add_block(g - 1, 1 - h)

            over_groups(v, G, count_group)
            add_block(G - 1, (G - 1) % 2)

            dve.wait_ge(s["block_added"], G)
            dve.wait_ge(s["counts_added"], G)
            v.tensor_reduce(deg_part, AT[:, :].rearrange("p (j n) -> p n j", j=NB), axis=AX.X, op=ALU.add
                            ).then_inc(s["deg_part"], 1)
            dve.wait_ge(s["deg_ready"], 1)
            step(v.tensor_scalar(small[:, 8, :], ps[:, 7, 0:NB], 1.0, None, ALU.max))
            v.reciprocal(inv_deg[:, :], small[:, 8, :]).then_inc(s["inv_ready"], 1)
            v.tensor_reduce(small[:, 9, 0:1], small[:, 8, :], axis=AX.X, op=ALU.max).then_inc(s["max_ready"], 1)
            dve.wait_ge(s["max_turned"], 1)
            step(v.tensor_reduce(degree_row[:, :], ps[0:1, 6, 0:P], axis=AX.X, op=ALU.max))
            v.tensor_scalar(many[:, :], degree_row[:, :], 4096.0, None, ALU.is_gt).then_inc(s["many_ready"], 1)
            dve.wait_ge(s["many_ready"], 1)
            too_many = v.value_load(many[0:1, 0:1], min_val=0, max_val=1)
            with v.If(too_many):
                dve.sem_inc(s["at_ready"], 1)
            with v.Else():
                v.tensor_copy(AT_r[:, :, :].rearrange("p j n -> p (j n)"), AT[:, :]).then_inc(s["at_ready"], 1)
            dve.wait_ge(s["inv_ready"], 1)

            def combine(l, b):
                dve.wait_ge(s["bias_loaded"], 16 * l + 16)
                dve.wait_ge(s["dense_ready"], l * NB + b + 1)
                pd = 4 + 2 * (b % 2)
                v.scalar_tensor_tensor(out=tmp[:, b % 2, 0, :], in0=ps[:, pd + 1, :], scalar=inv_deg[:, b:b + 1],
                                       in1=bias[:, :], op0=ALU.mult, op1=ALU.add).then_inc(s["dense_step"], 1)
                dve.wait_ge(s["dense_step"], l * (2 * NB) + 2 * b + 1)
                v.tensor_tensor(tmp[:, b % 2, 1, :], tmp[:, b % 2, 0, :], ps[:, pd, :], ALU.add).then_inc(s["dense_step"], 1)

            dve.wait_ge(s["weights_loaded"], 160)
            c = C ** -0.5
            v.tensor_scalar(WIN[:, :, :], WIN[:, :, :], c, None, ALU.mult).then_inc(s["prep"], 1)

            with v.Fori(0, LAYERS - 1, 1) as i:
                w_lo(Wn, 2 * i + 2)
                for b in range(NB):
                    dve.wait_ge(s["h_turned"], NB * i + NB + b - 1 if b >= 2 else NB * i + NB)
                    combine(i, b)
                    if b >= 1:
                        ht_lo(b - 1, (b - 1) % 2, NB * i + NB + b - 1)
                ht_lo(NB - 1, (NB - 1) % 2, NB * i + 2 * NB - 1)
                w_lo(Ws, 2 * i + 3)
                for b in range(NB):
                    g_lo(b, b % 2, NB * i + NB + b)

            dve.wait_ge(s["h_turned"], NB * LAYERS)
            for b in range(NB):
                combine(LAYERS - 1, b)
                dve.wait_ge(s["dense_step"], 2 * NB * (LAYERS - 1) + 2 * b + 2)
                load = NB + b
                dve.wait_ge(s[f"x_loaded_{load % 4}"], 16 * (load // 4 + 1))
                v.tensor_tensor(X[:, b, :], x_in[:, load % 4, :], tmp[:, b % 2, 1, :], ALU.add).then_inc(s["z_ready"], 1)
                dve.wait_ge(s["z_ready"], b + 1)
                step(v.bn_stats(stats[:, b, :], X[:, b, :]))
                step(v.bn_aggr(mv[:, b, :], stats[:, b, :]))
            v.tensor_scalar(rstd[:, 0, :], mv[:, :, 1], LN_EPS, None, ALU.add).then_inc(s["var_ready"], 1)
            dve.wait_ge(s["std_ready"], 1)
            step(v.reciprocal(rstd[:, 2, :], rstd[:, 1, :]))
            for b in range(NB):
                v.tensor_scalar(X[:, b, :], X[:, b, :], mv[:, b, 0:1], rstd[:, 2, b:b + 1], ALU.subtract, ALU.mult
                                ).then_inc(s["x1_ready"], 1)
            v.memset(rec_f[:, :, :, :], 0.0).then_inc(s["filter_prep"], 1)
            v.tensor_copy(wf1_part[:, 0, :], wf1_raw[:, :]).then_inc(s["filter_prep"], 1)
            dve.wait_ge(s["filter_prep"], 2)
            v.tensor_tensor(wf1_part[:, 1, :], wf1_raw[:, :], wf1_part[:, 0, :].bitcast(F32), ALU.subtract
                            ).then_inc(s["filter_prep"], 1)
            dve.wait_ge(s["filter_prep"], 3)
            for q in range(4):
                v.tensor_copy(WF1[32 * q:32 * q + 32, :], wf1_part[32 * q:32 * q + 32, q % 2, :].bitcast(F32)
                              ).then_inc(s["filter_prep"], 1)
            dve.wait_ge(s["edge_weights_loaded"], 16 * 7)
            pair = lambda a, lo: a[:, lo:lo + 2 * P].rearrange("p (f u) -> p u f", u=2)
            k3 = 3.0 ** -0.5
            for j, (lo, u, scale) in enumerate(((2 * P, 0, Y1), (0, 0, Y0), (0, 1, Y1 * k3), (2 * P, 1, Y0))):
                v.tensor_scalar(wf2[:, j, :], pair(wf2_raw, lo)[:, u, :], scale, None, ALU.mult).then_inc(s["prep"], 1)
                step(v.tensor_scalar(bf_perm[:, j, :], pair(bf_raw, lo)[:, u, :], scale, None, ALU.mult))
            bfp = bf_perm.rearrange("p j f -> p (j f)")
            step(v.tensor_copy(bf_part[:, 0, :], bfp))
            step(v.tensor_tensor(bf_rest[:, 0, :], bfp, bf_part[:, 0, :], ALU.subtract))
            step(v.tensor_copy(bf_part[:, 1, :], bf_rest[:, 0, :]))
            step(v.tensor_tensor(bf_rest[:, 1, :], bf_rest[:, 0, :], bf_part[:, 1, :], ALU.subtract))
            step(v.tensor_scalar(bfp, bf_part[:, 0, :], sel3[:, 0:1], None, ALU.mult))
            step(v.scalar_tensor_tensor(out=bf_rest[:, 0, :], in0=bf_part[:, 1, :], scalar=sel3[:, 1:2], in1=bfp,
                                        op0=ALU.mult, op1=ALU.add))
            v.scalar_tensor_tensor(out=bf3[:, :], in0=bf_rest[:, 1, :], scalar=sel3[:, 2:3], in1=bf_rest[:, 0, :],
                                   op0=ALU.mult, op1=ALU.add).then_inc(s["prep"], 1)
            for wt, scale in ((W1[:, :, :, :], (2 * C) ** -0.5), (W2[:, :, :], c)):
                v.tensor_scalar(wt, wt, scale, None, ALU.mult).then_inc(s["prep"], 1)
            dve.wait_ge(s["prep"], 9)
            v.tensor_copy(WF[:, 0, :, :], wf2[:, :, :]).then_inc(s["prep"], 1)
            dve.wait_ge(s["prep"], 10)
            v.tensor_tensor(WF[:, 1, :, :], wf2[:, :, :], WF[:, 0, :, :].bitcast(F32), ALU.subtract).then_inc(s["prep"], 1)
            def finish_hidden(g):
                dve.wait_ge(s["hid_ln"], g + 1)
                atleast(dve, s["hid_hi"], g)
                atleast(dve, s["hid_done"], g)
                v.scalar_tensor_tensor(out=h_full, in0=ps[:, 1, :], scalar=0.0, in1=h_ln,
                                       op0=ALU.max, op1=ALU.add).then_inc(s["hid_full"], 1)

            finish_hidden(0)
            dve.wait_ge(s["table_written"], 16 * NB)
            v.memset(agg[:, half_agg:], 0.0).then_inc(s["agg_zeroed"], 1)
            dve.wait_ge(s["agg_zeroed"], 2)
            dve.wait_ge(s["x1_ready"], NB)

            def messages(g, h, k):
                n = g * GT + k
                dve.wait_ge(s["w_ready"], n + 1)
                dve.wait_ge(gathered[h][k], 16 * (g // 2 + 1) if isinstance(g, int) else 8 * g + (16 if h == 0 else 8))
                atleast(dve, s["edges_summed"], n - 3)
                atleast(dve, s["va_ready"], 3 * (n - 3))
                atleast(dve, s["vb_lo"], n - 3)
                w = ps[:, 2 + k % 2, :].rearrange("p (m f) -> p m f", m=4)
                r = rows[:, h, k, :].rearrange("p (m f) -> p m f", m=4)
                y = lambda i: rec[:, bass.ds(n * REC + C_DIR + i, 1)]
                cutoff = rec[:, bass.ds(n * REC + C_CUT, 1)]
                v.scalar_tensor_tensor(out=msg[:, k, M_SCALED:M_SA + 1, :], in0=w[:, 0:2, :], scalar=cutoff,
                                       in1=r[:, 0:1, :].to_broadcast([P, 2, P]), op0=ALU.mult, op1=ALU.mult
                                       ).then_inc(s["msg_ready"], 1)
                dve.wait_ge(s["dot_begun"], n + 1)
                v.scalar_tensor_tensor(out=dots[:, k, 1, :], in0=r[:, 2, :], scalar=y(1), in1=dots[:, k, 0, :],
                                       op0=ALU.mult, op1=ALU.add).then_inc(s["dot_step"], 1)
                v.scalar_tensor_tensor(out=vb[:, k, :, :], in0=w[:, 3:4, :].to_broadcast([P, 3, P]), scalar=cutoff,
                                       in1=r[:, 1:4, :], op0=ALU.mult, op1=ALU.mult).then_inc(s["msg_ready"], 1)
                dve.wait_ge(s["dot_step"], 2 * n + 1)
                v.scalar_tensor_tensor(out=dots[:, k, 2, :], in0=r[:, 3, :], scalar=y(2), in1=dots[:, k, 1, :],
                                       op0=ALU.mult, op1=ALU.add).then_inc(s["dot_step"], 1)
                v.tensor_scalar(hot[:, k, :], iota_n[:, 0:P], rec[:, bass.ds(n * REC + C_OWN, 1)], None,
                                ALU.is_equal).then_inc(s["msg_ready"], 1)
                dve.wait_ge(s["dot_step"], 2 * n + 2)
                v.scalar_tensor_tensor(out=msg[:, k, M_SB, :], in0=dots[:, k, 2, :], scalar=cutoff, in1=w[:, 2, :],
                                       op0=ALU.mult, op1=ALU.mult).then_inc(s["msg_ready"], 1)

            two = {}

            def add_sums(g, h):
                dve.wait_ge(s["edges_summed"], GT * (g + 1))
                atleast(dve, s["agg_added"], g)
                if isinstance(g, int):
                    b = v.value_load(group_block[0:1, g:g + 1], min_val=0, max_val=NB - 1)
                elif h == 1:
                    two["blocks"] = v.value_load(pair_block[0:1, bass.ds(g, 1)], min_val=0, max_val=17 * (NB - 1))
                    b = (two["blocks"] & 15).with_bounds(min_val=0, max_val=NB - 1)
                else:
                    b = (two["blocks"] >> 4).with_bounds(min_val=0, max_val=NB - 1)
                a = agg[:, bass.ds(b * NA, NA)]
                v.tensor_tensor(a, a, psf[:, (4 + 2 * h) * 512:(6 + 2 * h) * 512], ALU.add).then_inc(s["agg_added"], 1)

            def edge_group(g, h):
                is_first = isinstance(g, int) and g == 0
                is_last = isinstance(g, int) and g == G - 1
                messages(g, h, 0)
                messages(g, h, 1)
                if not is_last:
                    finish_hidden(g + 1)
                messages(g, h, 2)
                if not is_first:
                    add_sums(g - 1, 1 - h)
                messages(g, h, 3)

            over_groups(v, G, edge_group)
            add_sums(G - 1, (G - 1) % 2)

            def softplus(b):
                dve.wait_ge(s["s_step"], 3 * b + 3)
                dve.wait_ge(s["v_copied"], b + 1)
                if b >= 2:
                    dve.wait_ge(s["o_ready"], b - 1)
                v.scalar_tensor_tensor(out=sv[:, b % 2, 0, :], in0=ps[:, 2 + b % 2, 0:P], scalar=0.0,
                                       in1=s_tmp[:, b % 2, 2, :], op0=ALU.max, op1=ALU.add).then_inc(s["sv_ready"], 1)

            def residual(b):
                dve.wait_ge(s["o_ready"], b + 1)
                po = ps[:, 4 + b % 2, :]
                n = b * 4
                v.tensor_tensor(X[:, b, 0:P], X[:, b, 0:P], po[:, 0:P], ALU.add).then_inc(s["z_step"], 1)
                xv = X[:, b, P:].rearrange("p (f i) -> p i f", i=3)
                v.tensor_tensor(xv, xv, po[:, P:].rearrange("p (i f) -> p i f", i=3), ALU.add).then_inc(s["z_step"], 1)
                dve.wait_ge(s["z_step"], n + 2)
                v.bn_stats(stats[:, b, :], X[:, b, :]).then_inc(s["z_step"], 1)
                dve.wait_ge(s["z_step"], n + 3)
                v.bn_aggr(mv[:, b, :], stats[:, b, :]).then_inc(s["z_step"], 1)

            for b in range(NB + 1):
                if b < NB:
                    softplus(b)
                if b >= 1:
                    residual(b - 1)
            dve.wait_ge(s["z_step"], 4 * NB)
            v.tensor_scalar(rstd[:, 0, :], mv[:, :, 1], LN_EPS, None, ALU.add).then_inc(s["var_ready"], 1)
            dve.wait_ge(s["std_ready"], 2)
            step(v.reciprocal(rstd[:, 2, :], rstd[:, 1, :]))
            for b in range(NB):
                v.tensor_scalar(X[:, b, :], X[:, b, :], mv[:, b, 0:1], rstd[:, 2, b:b + 1], ALU.subtract, ALU.mult
                                ).then_inc(s["out_ready"], 1)

        @block.tensor
        def _(pe):
            mm = nc.tensor.matmul
            pe.wait_ge(s["consts_made"], 7)
            pe.wait_ge(s["zeroed"], 6)
            pe.wait_ge(s["counts_ready"], 1)
            counts = small[0:EP, 0, :]
            mm(ps[0:EP, 7, 0:NB], lower[0:EP, 0:EP], counts, start=True, stop=True)
            mm(ps[:, 7, 16:16 + NB], ones[0:EP, :], counts, start=True, stop=True).then_inc(s["totals_ready"], 1)

            def turn(source, b, ready):
                for f, a in enumerate(source):
                    last = nc.tensor.transpose(ps[:, b % 2, f * P:(f + 1) * P], a, ident[:, :])
                last.then_inc(s[ready], 1)

            split = ((0, 0), (0, 1), (1, 0))

            def rows_times(bank, b, w):
                for j, (x_part, w_part) in enumerate(split):
                    for f in range(K):
                        last = mm(ps[:, bank, :], HT[:, x_part, f, b * P:(b + 1) * P], w[:, w_part, f, :],
                                  start=(j == 0 and f == 0), stop=(j == 2 and f == K - 1))
                return last

            def times_neighbours(b, done):
                pe.wait_ge(s["ht_done"], done + 1)
                atleast(pe, s["g_done"], done - 1)
                rows_times(2 + b % 2, b, Wn).then_inc(s["g_ready"], 1)

            pe.wait_ge(s["w_split"], 1)
            for b in range(NB + 1):
                if b < NB:
                    pe.wait_ge(s[f"x_loaded_{b % 4}"], 16 * (b // 4 + 1))
                    atleast(pe, s["ht_done"], b - 1)
                    turn([x_in[:, b % 4, f * P:(f + 1) * P] for f in range(K)], b, "h_turned")
                if b >= 1:
                    times_neighbours(b - 1, b - 1)

            pe.wait_ge(s["g_done"], NB)

            def count_group(g, h):
                atleast(pe, s["block_added"], g - 1)
                atleast(pe, s["counts_copied"], g - 1)
                for k in range(GT):
                    pe.wait_ge(s["one_hots"], 2 * GT * g + 2 * k + 2)
                    for a, z in SLICES:
                        last = mm(psf[:, 1536 * h + a:1536 * h + z], oh_own[:, k % 4, :], oh_dst[:, k % 4, a:z],
                                  start=(k == 0), stop=(k == GT - 1))
                    last.then_inc(s["tile_summed"], 1)

            over_groups(pe, G, count_group)

            pe.wait_ge(s["deg_part"], 1)
            for b in range(NB):
                last = mm(ps[:, 7, b:b + 1], deg_part[:, b * P:(b + 1) * P], ones[:, 0:1], start=True, stop=True)
            last.then_inc(s["deg_ready"], 1)
            pe.wait_ge(s["max_ready"], 1)
            nc.tensor.transpose(ps[0:1, 6, 0:P], small[:, 9, 0:1], ident[:, :]).then_inc(s["max_turned"], 1)
            pe.wait_ge(s["many_ready"], 1)
            pe.wait_ge(s["at_ready"], 1)
            pe.wait_ge(s["inv_ready"], 1)
            too_many = nc.tensor.value_load(many[0:1, 0:1], min_val=0, max_val=1)
            a_t = AT[:, :].rearrange("p (j n) -> p j n", j=NB)

            def mean_block(bank, b):
                with nc.tensor.If(too_many):
                    for part in range(2):
                        for j in range(NB):
                            mm(ps[:, bank, :], a_t[:, j, b * P:(b + 1) * P], GN[:, part, j, :].bitcast(F32),
                               start=(part == 0 and j == 0), stop=(part == 1 and j == NB - 1))
                with nc.tensor.Else():
                    for part in range(2):
                        for j in range(NB):
                            mm(ps[:, bank, :], AT_r[:, j, b * P:(b + 1) * P], GN[:, part, j, :],
                               start=(part == 0 and j == 0), stop=(part == 1 and j == NB - 1))

            def dense_block(l, b):
                pe.wait_ge(s["dense_step"], l * (2 * NB) + (2 * b - 2 if b >= 2 else 0))
                mean_block(5 + 2 * (b % 2), b)
                rows_times(4 + 2 * (b % 2), b, Ws).then_inc(s["dense_ready"], 1)

            pe.wait_ge(s["w_split"], 2)
            with pe.Fori(0, LAYERS - 1, 1) as i:
                def turn_relu(b):
                    pe.wait_ge(s["h_ready"], NB * i + b + 1)
                    pe.wait_ge(s["ht_done"], NB * i + NB + b - 1)
                    turn([tmp[:, b % 2, 0, f * P:(f + 1) * P] for f in range(K)], b, "h_turned")

                pe.wait_ge(s["g_done"], NB * i + NB)
                pe.wait_ge(s["w_split"], 2 * i + 2)
                for b in range(NB):
                    dense_block(i, b)
                    if b >= 1:
                        turn_relu(b - 1)
                turn_relu(NB - 1)
                pe.wait_ge(s["w_split"], 2 * i + 3)
                for b in range(NB):
                    times_neighbours(b, NB * i + NB + b)
            pe.wait_ge(s["g_done"], NB * LAYERS)
            pe.wait_ge(s["w_split"], 2 * LAYERS)
            for b in range(NB):
                dense_block(LAYERS - 1, b)

            pe.wait_ge(s["prep"], 2)
            for b in range(NB + 1):
                if b < NB:
                    pe.wait_ge(s["x1_ready"], b + 1)
                    atleast(pe, s["xt_copied"], b - 1)
                    turn([X[:, b, 0:P]] + [X[:, b, P + i:D:3] for i in range(3)], b, "x_turned")
                if b >= 1:
                    q = b - 1
                    pe.wait_ge(s["xt_copied"], q + 1)
                    atleast(pe, s["table_copied"], q - 1)
                    for f in range(K):
                        last = mm(ps[:, 2 + q % 2, f * P:(f + 1) * P], XT[:, f, q * P:(q + 1) * P],
                                  WIN[:, min(f, 1), :], start=True, stop=True)
                    last.then_inc(s["table_ready"], 1)

            def turn_features(g):
                pe.wait_ge(s["rec_hi"], 2 * g + 2)
                pe.wait_ge(s["staged_f"], g + 1)
                atleast(pe, s["ft_copied"], g)
                for k in range(GT):
                    last = nc.tensor.transpose(ps[:, 0, k * P:(k + 1) * P],
                                               rec_f[:, k, :, :].rearrange("p u c -> p (u c)"), ident[:, :])
                last.then_inc(s["f_turned"], 1)

            def hidden(g):
                pe.wait_ge(s["ft_copied"], g + 1)
                atleast(pe, s["hid_full"], g)
                mm(ps[:, 1, :], WF1[:, :], f_t, start=True, stop=True).then_inc(s["hid_ready"], 1)

            def weights(g, h, k):
                if k == 0:
                    pe.wait_ge(s["hid_done"], g + 1)
                mm(ps[:, 2 + k % 2, :], ones3[:, :], bf3[:, :], start=True, stop=False)
                for j, (h_part, w_part) in enumerate(split):
                    last = mm(ps[:, 2 + k % 2, :], hid[:, h, h_part, k * P:(k + 1) * P], WF[:, w_part, :, :],
                              start=False, stop=(j == 2))
                last.then_inc(s["w_ready"], 1)

            def sums(g, h, k):
                n = g * GT + k
                pe.wait_ge(s["va_ready"], 3 * n + 3)
                if k == 0:
                    atleast(pe, s["agg_added"], g - 1)
                first, last_k = k == 0, k == GT - 1
                bank = 4 + 2 * h
                own = hot[:, k, :]
                mm(ps[:, bank, :], own.bitcast(F32), msg[:, k, 1:5, :], start=first, stop=last_k)
                mm(ps[:, bank + 1, 0:P], own.bitcast(F32), msg[:, k, 5, :], start=first, stop=last_k,
                   skip_group_check=True)
                mm(ps[:, bank + 1, P:], own, vb_hi[:, k, :, :], start=False, stop=False, skip_group_check=True)
                pe.wait_ge(s["vb_lo"], n + 1)
                mm(ps[:, bank + 1, P:], own, vb_lo[:, k, :, :], start=False, stop=last_k,
                   skip_group_check=True).then_inc(s["edges_summed"], 1)

            def edge_group(g, h):
                left = G - 1 - g if isinstance(g, int) else G
                for k in range(GT):
                    if k == 2 and left >= 2:
                        turn_features(g + 2)
                    if k == 3 and left >= 2:
                        hidden(g + 2)
                    pe.wait_ge(s["msg_ready"], 4 * (g * GT + k) + 4)
                    if k + 2 < GT:
                        weights(g, h, k + 2)
                    elif left >= 1:
                        weights(g + 1, 1 - h, k + 2 - GT)
                    if k >= 1:
                        sums(g, h, k - 1)
                    elif not (isinstance(g, int) and g == 0):
                        sums(g - 1, 1 - h, GT - 1)

            pe.wait_ge(s["table_copied"], NB)
            pe.wait_ge(s["filter_prep"], 7)
            turn_features(0)
            hidden(0)
            turn_features(1)
            hidden(1)
            pe.wait_ge(s["prep"], PREPARED)
            weights(0, 0, 0)
            weights(0, 0, 1)
            over_groups(pe, G, edge_group)
            sums(G - 1, (G - 1) % 2, GT - 1)

            pe.wait_ge(s["agg_added"], G)
            ag = agg[:, :].rearrange("p (b m f) -> p b m f", b=NB, m=8)

            def turn_agg(b):
                if b >= 1:
                    pe.wait_ge(s["agg_copied"], 2 * b)
                for m in range(8):
                    last = nc.tensor.transpose(ps[:, m // 4, (m % 4) * P:(m % 4 + 1) * P], ag[:, b, m, :], ident[:, :])
                last.then_inc(s["agg_turned"], 1)

            def mix(b):
                pe.wait_ge(s["agg_copied"], 2 * b + 2)
                if b >= 2:
                    pe.wait_ge(s["sv_ready"], b - 1)
                a = agg_t[:, b % 2, :, :]
                pb = ps[:, 2 + b % 2, :]
                mm(pb[:, 0:P], W1[:, 0, 0, :], a[:, 0, :], start=True, stop=False)
                mm(pb[:, 0:P], W1[:, 0, 1, :], a[:, 1, :], start=False, stop=True)
                mm(pb[:, P:], W1[:, 1, 0, :], a[:, 2:5, :], start=True, stop=False)
                mm(pb[:, P:], W1[:, 1, 1, :], a[:, 5:8, :], start=False, stop=True).then_inc(s["s_ready"], 1)

            def project(b):
                pe.wait_ge(s["sv_ready"], b + 1)
                if b >= 2:
                    pe.wait_ge(s["z_step"], 4 * (b - 1))
                for m in range(4):
                    last = mm(ps[:, 4 + b % 2, m * P:(m + 1) * P], sv[:, b % 2, m, :], W2[:, min(m, 1), :],
                              start=True, stop=True)
                last.then_inc(s["o_ready"], 1)

            turn_agg(0)
            for b in range(NB + 1):
                if b + 1 < NB:
                    turn_agg(b + 1)
                if b < NB:
                    mix(b)
                if b >= 1:
                    project(b - 1)


INS = ("x", "src", "dst", "edge_attr_20", "edge_attr_3", "edge_weight",
       "L0_gnn_Ws_self", "L0_gnn_Ws_neigh", "L0_gnn_bs",
       "L1_gnn_W_in2f_s", "L1_gnn_W_in2f_v", "L1_gnn_Wf1", "L1_gnn_bf1", "L1_gnn_Wf2", "L1_gnn_bf2",
       "L1_gnn_W1_s", "L1_gnn_W1_v", "L1_gnn_W2_s", "L1_gnn_W2_v")


def kernel(**inputs):
    import numpy as np
    import concourse.bacc as bacc
    from concourse.bass_utils import run_bass_kernel_spmd

    nc = bacc.Bacc("TRN2", target_bir_lowering=False, num_devices=1)
    arrays, args = {}, []
    for name in INS:
        a = np.ascontiguousarray(inputs[name])
        arrays[f"in_{name}"] = a
        args.append(nc.dram_tensor(f"in_{name}", a.shape, mybir.dt.from_np(a.dtype), kind="ExternalInput").ap())
    shape = inputs["x"].shape
    out = nc.dram_tensor("out", shape, F32, kind="ExternalOutput").ap()
    gnn_resnorm(nc, *args, out)
    result = run_bass_kernel_spmd(nc, [arrays], core_ids=[0])
    return result.results[0]["out"]
```

```python
from contextlib import ExitStack

import concourse.bass as bass
from concourse import mybir

F32 = mybir.dt.float32
F32R = mybir.dt.float32r
BF16 = mybir.dt.bfloat16
I32 = mybir.dt.int32
I16 = mybir.dt.int16
ALU = mybir.AluOpType
ACT = mybir.ActivationFunctionType
AX = mybir.AxisListType

P = 128
LN_EPS = 1e-5
PI = 3.141592653589793
Y0 = (1.0 / (4.0 * PI)) ** 0.5
Y1 = (3.0 / (4.0 * PI)) ** 0.5

REC = 32
C_ONE, C_CUT, C_DIR, C_DST, C_OWN = 20, 21, 22, 25, 26
NF = C_ONE + 1

M_SCALED, M_SA, M_SB, M_VA, M_ALL = 0, 1, 2, 3, 6
N_SUMS = 8


def plan(n_nodes, n_edges):
    nb = -(-n_nodes // P)
    gt = 4
    gsz = gt * P
    groups = (n_edges + nb * (gsz - 1)) // gsz
    groups += 1 - groups % 2
    ep = max(k for k in range(1, P + 1) if n_edges % k == 0)
    return nb, gt, gsz, groups, ep, n_edges // ep


def over_groups(engine, groups, body):
    body(0, 0)
    body(1, 1)
    with engine.Fori(0, (groups - 5) // 2, 1) as i:
        body(2 * i + 2, 0)
        body(2 * i + 3, 1)
    body(groups - 3, 0)
    body(groups - 2, 1)
    body(groups - 1, 0)


def gnn_resnorm(nc, x, src, dst, edge_f, edge_r, edge_w, ws_self, ws_neigh, bs,
                w_in_s, w_in_v, wf1, bf1, w_f2, bf2, w1_s, w1_v, w2_s, w2_v, out):
    N, D = x.shape
    E = src.shape[0]
    LAYERS = ws_self.shape[0]
    C = w_in_s.shape[0]
    K = D // P
    NB, GT, GSZ, G, EP, ET = plan(N, E)
    T = G * GT
    NP = NB * P
    TAIL = N - (NB - 1) * P
    SH = GSZ.bit_length() - 1
    SLICES = [(s, min(s + 512, NP)) for s in range(0, NP, 512)]
    ST = 5
    assert C == P and D == 4 * P and ET % (2 * ST) == 0 and GSZ == 1 << SH and LAYERS == 3

    slots = nc.dram_tensor("edge_slots", (P * T, REC), F32, kind="Internal").ap()
    table = nc.dram_tensor("node_rows", (NP, D), F32, kind="Internal").ap()

    with ExitStack() as ctx:
        def sb(name, shape, dt=F32):
            return ctx.enter_context(nc.sbuf_tensor(name, shape, dt))

        def sem(name):
            return ctx.enter_context(nc.semaphore(name))

        def at(offset, name, shape, dt=F32):
            return nc.alloc_sbuf_tensor_at(name, shape, dt, offset=offset)

        ps = ctx.enter_context(nc.psum_tensor("ps", [P, 8, 512], F32))
        psf = ps[:, :, :].rearrange("p b n -> p (b n)")

        bias = sb("bias", [P, D])
        WIN = sb("WIN", [P, 2, P])
        WF1 = sb("WF1", [P, P], F32R)
        wf1_raw = sb("wf1_raw", [P, P])
        x_in = sb("x_in", [P, 4, D])
        tmp = sb("tmp", [P, 2, 2, D])
        bf_raw = tmp[0:3, 0, 0, :]
        bf_perm = tmp[0:3, 0, 1, :].rearrange("p (j f) -> p j f", j=4)
        bf_rest = tmp[0:3, 1, :, :]
        ones3 = sb("ones3", [3, P], BF16)
        sel3 = sb("sel3", [3, 3])
        ident = sb("ident", [P, P])
        lower = sb("lower", [P, P])
        ones = sb("ones", [P, P])
        ones_bf = sb("ones_bf", [P, 1], BF16)
        half = sb("half", [P, 1])
        iota_n = sb("iota_n", [P, NP], I16)
        iota_g = sb("iota_g", [1, G, NB])
        dst_f = sb("dst_f", [P, T])
        own_f = sb("own_f", [P, T])
        dst_idx = sb("dst_idx", [P, T], I32)
        blocks_before = sb("blocks_before", [1, G])
        group_block = sb("group_block", [1, G], I32)
        pair_block = sb("pair_block", [1, G], I32)
        inv_deg = sb("inv_deg", [P, NB])
        stats = sb("stats", [P, NB, 6])
        mv = sb("mv", [P, NB, 2])
        rstd = sb("rstd", [P, 3, NB])
        gather_idx = sb("gather_idx", [P, 2, GT], I32)
        small = sb("small", [P, 10, NB])
        degree_row = sb("degree_row", [1, 1])
        many = sb("many", [1, 1], I32)
        stage = sb("stage", [EP, 2, ST, REC])
        stage_idx = sb("stage_idx", [EP, 2, ST], I32)
        bucket_end = sb("bucket_end", [EP, NB + 1])

        R_AT = -(-nc.sbuf_base // 64) * 64
        R_HT = R_AT + 4 * NB * NP
        R_G = R_HT + 8 * K * NP
        R_WS = R_G + 8 * NB * D
        R_WN = R_WS + 8 * K * D
        R_RAW = R_WN + 8 * K * D
        assert R_RAW + 4 * K * D + 4 * ET <= nc.sbuf_usable_end, (R_RAW + 4 * K * D + 4 * ET, nc.sbuf_usable_end)

        AT = at(R_AT, "AT", [P, NB * NP])
        AT_r = at(R_AT, "AT_r", [P, NB, NP], F32R)
        AT_rounded = AT_r[:, :, :].rearrange("p j n -> p (j n)")
        HT = at(R_HT, "HT", [P, 2, K, NP], F32R)
        S0 = at(R_HT + 4 * K * NP, "S0", [P, K, NP])
        GN = at(R_G, "GN", [P, 2, NB, D], F32R)
        Ws = at(R_WS, "Ws", [P, 2, K, D], F32R)
        Wn = at(R_WN, "Wn", [P, 2, K, D], F32R)
        raw = at(R_RAW, "raw", [P, K, D])

        pads = at(R_WS, "pads", [P, T // 4 * REC])
        n_buckets = NB * ET
        srt = at(R_AT, "srt", [EP, 4 * n_buckets + ET * REC])
        bucket = srt[:, 0:n_buckets]
        in_bucket = srt[:, n_buckets:2 * n_buckets]
        running = srt[:, 2 * n_buckets:3 * n_buckets]
        all_ones = srt[:, 3 * n_buckets:4 * n_buckets]
        E_rec = srt[:, 4 * n_buckets:4 * n_buckets + ET * REC]
        lists = at(R_G, "lists", [EP, 38 * ET])
        f_raw = lists[:, 18 * ET:38 * ET]
        ht = lists[:, 0:18 * ET]
        row_i = at(R_RAW + 4 * K * D, "row_i", [EP, ET], I32)[:, :]
        r_raw = ht[:, 0:3 * ET]
        r_sq = ht[:, 3 * ET:6 * ET]
        dst_i = ht[:, 6 * ET:7 * ET].bitcast(I32)
        src_i = ht[:, 7 * ET:8 * ET].bitcast(I32)
        w_raw = ht[:, 8 * ET:9 * ET]
        blk_i = ht[:, 9 * ET:10 * ET].bitcast(I32)
        blk_f = ht[:, 10 * ET:11 * ET]
        place_f = ht[:, 11 * ET:12 * ET]
        place_i = ht[:, 12 * ET:13 * ET].bitcast(I32)
        place_lo = ht[:, 13 * ET:14 * ET].bitcast(I32)
        place_hi = ht[:, 14 * ET:15 * ET].bitcast(I32)
        norm = ht[:, 15 * ET:18 * ET]

        SHARE = T // 4
        shares = (x_in[:, :, :].rearrange("p u n -> p (u n)")[:, 0:SHARE * REC],
                  raw[:, :, :].rearrange("p k n -> p (k n)")[:, 0:SHARE * REC],
                  tmp[:, :, :, :].rearrange("p a b n -> p (a b n)")[:, 0:SHARE * REC])
        oh_dst = at(R_WN, "oh_dst", [P, 4, NP], BF16)
        oh_own = at(R_WN + 8 * NP, "oh_own", [P, 2, GT, P], BF16)
        own_distance = at(R_WN + 8 * NP + 4 * GT * P, "own_distance", [P, GT - 1, P], BF16)
        DH = 5
        deg_hots = at(R_WN, "deg_hots", [EP, DH, NP], BF16)
        degrees = tmp[0:1, :, :, :].rearrange("p a b d -> p (a b d)")[:, 0:NP]

        NC = NP - 512
        COUNT_SLICES = ((0, 512, 0), (512, NC, 512), (NC, NP, 1024))
        counts_sb = x_in[:, :, :].rearrange("p u n -> p (u n)")

        X = at(R_WN, "X", [P, NB, D])
        XT = at(R_HT + 4 * K * NP, "XT", [P, K, NP])
        TAB = at(R_AT + 4 * K * NP, "TAB", [P, K, NP])

        NA = N_SUMS * P
        agg = at(R_AT, "agg", [P, NB * NA])
        o = R_AT + 4 * NB * NA
        WF = at(o, "WF", [P, 2, 4, P], F32R)
        W1 = at(o + 4096, "W1", [P, 2, 2, P])
        W2 = at(o + 6144, "W2", [P, 2, P])
        bf3 = at(o + 7168, "bf3", [3, 4 * P], BF16)
        bf_part = at(o + 8192, "bf_part", [3, 2, 4 * P], BF16)
        rec = at(R_G, "rec", [P, T * REC])
        o = R_G + 4 * T * REC
        wf2_raw = at(o, "wf2_raw", [P, 6 * P])
        wf2 = at(o + 3072, "wf2_scaled", [P, 4, P])
        wf1_part = at(o + 5120, "wf1_part", [P, 2, P], F32R)
        rows = at(R_WS, "rows", [P, 2, GT, D])
        o = R_HT
        hid = at(o, "hid", [P, 2, 2, GSZ], F32R)
        o += 16 * GSZ
        h_full = at(o, "h_full", [P, GSZ])[:, :]
        o += 4 * GSZ
        f_t = at(o, "f_t", [P, GSZ], F32R)[:, :]
        o += 4 * GSZ
        h_exp, h_ln = (at(o + 4 * GSZ * i, f"hid_{i}", [P, GSZ])[:, :] for i in range(2))
        o += 8 * GSZ
        h_abs = x_in[:, :, 3 * P:]
        rec_f = at(o, "rec_f", [P, GT, 4, 32])
        o += 4 * GT * P
        rec_hi = at(o, "rec_hi", [P, GT, NF], F32R)
        o += -(-4 * GT * NF // 64) * 64
        assert o <= R_HT + 4 * K * NP
        vb = at(o, "vb", [P, 4, 3, P])
        vb_hi = at(o + 48 * P, "vb_hi", [P, 4, 3, P], F32R)
        vb_lo = at(o + 96 * P, "vb_lo", [P, 4, 3, P], F32R)
        o += 144 * P
        hot = at(o, "hot", [P, 4, P], F32R)
        o += 16 * P
        dots = x_in[:, :, 0:3 * P].rearrange("p u (i f) -> p u i f", i=3)
        msg = at(R_G + 4 * T * REC, "msg", [P, 4, M_ALL, P])
        assert 4 * T * REC + 16 * M_ALL * P <= 8 * NB * D
        assert o <= R_G

        half_agg = NB * NA // 2
        assert half_agg == K * NP

        agg_t = at(R_HT, "agg_t", [P, 2, 8, P])
        sv = at(R_HT + 8192, "sv", [P, 2, 4, P])
        s_tmp = at(R_HT + 12288, "s_tmp", [P, 2, 3, P])

        s = {name: sem(name) for name in (
            "edges_loaded", "x_loaded_0", "x_loaded_1", "x_loaded_2", "x_loaded_3", "weights_loaded",
            "edge_weights_loaded", "raw_loaded", "bias_loaded", "w_hi", "w_split", "pads_written",
            "consts_made", "zeroed", "sort_step", "counts_ready", "blocks_known", "totals_ready", "edge_copied",
            "norm_sq", "norm_ready", "staged", "scattered_0", "scattered_1", "rec_loaded_0", "rec_loaded_1",
            "rec_loaded_2", "rec_split", "one_hots", "own_abs", "own_hots", "tile_summed", "block_added",
            "counts_copied", "counts_added", "deg_hots", "deg_summed", "deg_copied", "deg_ready", "inv_ready",
            "max_ready", "max_turned", "many_ready", "h_turned", "ht_hi", "ht_done", "g_ready", "g_hi",
            "g_done", "own_ready", "own_copied", "dense_ready", "mean_ready", "dense_step", "h_ready",
            "z_ready", "x_turned", "xt_copied", "var_ready", "std_ready", "x1_ready", "table_ready",
            "table_copied", "table_written", "prep", "staged_f", "f_turned", "ft_copied", "hid_ready",
            "hid_abs", "hid_exp", "hid_ln", "hid_done", "w_ready", "msg_ready", "dot_step", "dot_begun",
            "act_turns", "hid_full", "hid_hi", "vb_hi", "vb_lo", "rec_hi", "va_ready", "edges_summed",
            "agg_added", "agg_zeroed", "at_zeroed", "filter_prep", "idx_copied", "turns", "agg_turned",
            "agg_copied", "s_ready", "s_step", "v_copied", "sv_ready", "o_ready", "z_step", "out_ready",
            "written")}

        gathered = [[sem(f"gathered_{h}_{k}") for k in range(GT)] for h in range(2)]

        block = ctx.enter_context(nc.Block())

        def at_columns(counts, a, z):
            return counts.rearrange("p (j n) -> p j n", j=NB)[:, :, a:z]

        def atleast(eng, semaphore, value):
            if not isinstance(value, int) or value > 0:
                eng.wait_ge(semaphore, value)

        def block_of(eng, loaded, g, is_first):
            if isinstance(g, int):
                return eng.value_load(group_block[0:1, g:g + 1], min_val=0, max_val=NB - 1)
            if is_first:
                loaded["two"] = eng.value_load(pair_block[0:1, bass.ds(g, 1)], min_val=0, max_val=17 * (NB - 1))
                b = loaded["two"] & 15
            else:
                b = loaded["two"] >> 4
            return b.with_bounds(min_val=0, max_val=NB - 1)

        class Chain:

            def __init__(self, eng, semaphore):
                self.eng, self.semaphore, self.n = eng, semaphore, 0

            def __call__(self, instruction):
                instruction.then_inc(self.semaphore, 1)
                self.n += 1
                self.eng.wait_ge(self.semaphore, self.n)

        PREPARED = 11
        SORTED = 24
        HALVES = ET // ST

        @block.sync
        def _(sp):
            sp.dma_start(dst_i, dst.rearrange("(p t) -> p t", p=EP)).then_inc(s["edges_loaded"], 16)
            sp.dma_start(src_i, src.rearrange("(p t) -> p t", p=EP)).then_inc(s["edges_loaded"], 16)
            sp.dma_start(r_raw, edge_r.rearrange("(p t) c -> p (t c)", p=EP)).then_inc(s["edges_loaded"], 16)
            sp.dma_start(w_raw, edge_w.rearrange("(p t) -> p t", p=EP)).then_inc(s["edges_loaded"], 16)
            sp.dma_start(f_raw, edge_f.rearrange("(p t) c -> p (t c)", p=EP)).then_inc(s["edges_loaded"], 16)
            sp.dma_start(raw[:, :, :], ws_neigh[0, :, :].rearrange("(k p) n -> p k n", p=P)).then_inc(s["raw_loaded"], 16)

            def load_x(b, load):
                n = P if b < NB - 1 else TAIL
                sp.dma_start(x_in[0:n, load % 4, :], x[b * P:b * P + n, :]).then_inc(s[f"x_loaded_{load % 4}"], 16)

            for b in range(4):
                load_x(b, b)
            sp.wait_ge(s["zeroed"], 2)
            slot_rows = slots.rearrange("(p t) c -> p (t c)", p=P)
            n = T // 4 * REC
            for i in range(4):
                sp.dma_start(slot_rows[:, i * n:(i + 1) * n], pads[:, :]).then_inc(s["pads_written"], 16)
            sp.wait_ge(s["zeroed"], 3)
            for buf, w in ((WIN[:, 0, :], w_in_s), (WIN[:, 1, :], w_in_v),
                           *((wf1_raw[q:q + NF - 1, :], wf1) for q in range(0, P, 32)),
                           *((wf1_raw[q + NF - 1:q + NF, :], bf1.rearrange("(a f) -> a f", a=1))
                             for q in range(0, P, 32))):
                sp.dma_start(buf, w).then_inc(s["weights_loaded"], 16)
            sp.dma_start(bias[:, :], bs[0:1, :].to_broadcast([P, D])).then_inc(s["bias_loaded"], 16)
            sp.wait_ge(s["w_split"], 1)
            sp.dma_start(raw[:, :, :], ws_self[0, :, :].rearrange("(k p) n -> p k n", p=P)).then_inc(s["raw_loaded"], 16)
            for b in range(4, NB):
                sp.wait_ge(s["h_turned"], b - 3)
                load_x(b, b)
            sp.wait_ge(s["scattered_0"], 16 * ST * (HALVES // 2))
            sp.wait_ge(s["scattered_1"], 16 * ST * (HALVES // 2))
            sp.wait_ge(s["h_turned"], NB)
            sp.wait_ge(s["w_split"], 2)
            for i in range(4):
                if i == 2:
                    sp.wait_ge(s["deg_ready"], 1)
                if i == 3:
                    sp.wait_ge(s["rec_split"], 2)
                sp.dma_start(shares[i % 3], slot_rows[:, i * SHARE * REC:(i + 1) * SHARE * REC]).then_inc(s[f"rec_loaded_{i % 3}"], 16)
            sp.wait_ge(s["rec_split"], 4)
            with sp.Fori(0, LAYERS - 1, 1) as i:
                for u, w in ((0, ws_neigh), (1, ws_self)):
                    sp.wait_ge(s["w_split"], 2 * i + 2 + u)
                    sp.dma_start(raw[:, :, :], w[bass.ds(i + 1, 1), :, :].rearrange("a (k p) n -> p (a k) n", p=P)
                                 ).then_inc(s["raw_loaded"], 16)
                sp.wait_ge(s["dense_step"], 2 * NB * i + 2 * NB)
                sp.dma_start(bias[:, :], bs[bass.ds(i + 1, 1), :].to_broadcast([P, D])).then_inc(s["bias_loaded"], 16)
            for b in range(4):
                load_x(b, NB + b)
            for b in range(4, NB):
                sp.wait_ge(s["z_ready"], b - 3)
                load_x(b, NB + b)
            sp.wait_ge(s["dense_ready"], LAYERS * NB)
            for buf, w in ((rec[:, :], slot_rows), (wf2_raw[:, :], w_f2),
                           (W1[:, 0, :, :], w1_s.rearrange("(f u) c -> f u c", u=2)),
                           (W1[:, 1, :, :], w1_v.rearrange("(f u) c -> f u c", u=2)),
                           (W2[:, 0, :], w2_s), (W2[:, 1, :], w2_v)):
                sp.dma_start(buf, w).then_inc(s["edge_weights_loaded"], 16)
            sp.wait_ge(s["z_ready"], NB)
            sp.dma_start(bf_raw, bf2[0:4 * P].rearrange("(a f) -> a f", a=1).to_broadcast([3, 4 * P])
                         ).then_inc(s["edge_weights_loaded"], 16)
            for b in range(NB):
                sp.wait_ge(s["table_copied"], b + 1)
                sp.dma_start(table[b * P:(b + 1) * P, :],
                             TAB[:, :, b * P:(b + 1) * P]).then_inc(s["table_written"], 16)
            for b in range(NB):
                n = P if b < NB - 1 else TAIL
                sp.wait_ge(s["out_ready"], b + 1)
                sp.dma_start(out[b * P:b * P + n, :], X[0:n, b, :]).then_inc(s["written"], 16)
            sp.wait_ge(s["written"], 16 * NB)

        @block.gpsimd
        def _(pool):
            bk = bucket.rearrange("p (b t) -> p b t", b=NB)
            pool.iota(bk, pattern=[[1, NB], [0, ET]], base=0, channel_multiplier=0,
                      allow_small_or_imprecise_dtypes=True).then_inc(s["consts_made"], 1)
            pool.memset(ident[:, :], 0.0).then_inc(s["consts_made"], 1)
            pool.memset(lower[:, :], 1.0).then_inc(s["consts_made"], 1)
            pool.memset(sel3[:, :], 0.0).then_inc(s["consts_made"], 1)
            pool.wait_ge(s["consts_made"], 4)
            pool.affine_select(out=ident[:, :], in_=ident[:, :], compare_op=ALU.not_equal, fill=1.0, base=0,
                               pattern=[[-1, P]], channel_multiplier=1).then_inc(s["consts_made"], 1)
            pool.affine_select(out=lower[:, :], in_=lower[:, :], compare_op=ALU.is_gt, fill=0.0, base=0,
                               pattern=[[1, P]], channel_multiplier=-1).then_inc(s["consts_made"], 1)
            pool.affine_select(out=sel3[:, :], in_=sel3[:, :], compare_op=ALU.not_equal, fill=1.0, base=0,
                               pattern=[[-1, 3]], channel_multiplier=1).then_inc(s["consts_made"], 1)
            pool.iota(iota_g[:, :, :], pattern=[[1, G], [0, NB]], base=0, channel_multiplier=0,
                      allow_small_or_imprecise_dtypes=True).then_inc(s["consts_made"], 1)
            pool.iota(iota_n[:, :], pattern=[[1, NP]], base=0, channel_multiplier=0).then_inc(s["consts_made"], 1)

            pool.wait_ge(s["pads_written"], 64)
            with pool.Fori(0, HALVES // 2, 1) as i:
                for h in range(2):
                    pool.wait_ge(s["staged"], 4 * i + 2 * h + 2)
                    pool.sem_inc(s["turns"], 1)
                    for k in range(ST):
                        pool.indirect_dma_start(
                            out=slots[:, :], out_offset=bass.IndirectOffsetOnAxis(ap=stage_idx[:, h, k:k + 1], axis=0),
                            in_=stage[:, h, k, :], in_offset=None).then_inc(s[f"scattered_{h}"], 16)

            pool.wait_ge(s["many_ready"], 1)
            pool.wait_ge(s["blocks_known"], 2)

            loaded = {}

            def add_counts(g, h, counts):
                pool.wait_ge(s["counts_copied"], g + 1)
                atleast(pool, s["counts_added"], g)
                pool.sem_inc(s["turns"], 1)
                b = block_of(nc.gpsimd, loaded, g, h == 0)
                a = counts[:, bass.ds(b * NP, NC)]
                pool.tensor_tensor(a, a.bitcast(F32), counts_sb[:, h * NC:(h + 1) * NC], ALU.add).then_inc(s["counts_added"], 1)

            too_many = nc.gpsimd.value_load(many[0:1, 0:1], min_val=0, max_val=1)
            with pool.If(too_many):
                pool.memset(at_columns(AT[:, :], 0, NC), 0.0).then_inc(s["at_zeroed"], 1)
                pool.wait_ge(s["at_zeroed"], 1)
                over_groups(pool, G, lambda g, h: add_counts(g, h, AT))
            with pool.Else():
                pool.memset(at_columns(AT_rounded, 0, NC).bitcast(F32), 0.0).then_inc(s["at_zeroed"], 1)
                pool.wait_ge(s["at_zeroed"], 1)
                over_groups(pool, G, lambda g, h: add_counts(g, h, AT_rounded))

            pool.wait_ge(s["rec_split"], 9)

            def copy_index(g, h):
                atleast(pool, s["msg_ready"], 16 * (g - 1))
                pool.tensor_copy(gather_idx[:, h, :], dst_idx[:, bass.ds(g * GT, GT)]).then_inc(s["idx_copied"], 1)
                pool.wait_ge(s["idx_copied"], g + 1)
                pool.sem_inc(s["turns"], 1)

            def gather(h, k):
                pool.indirect_dma_start(
                    out=rows[:, h, k, :], out_offset=None, in_=table[:, :],
                    in_offset=bass.IndirectOffsetOnAxis(ap=gather_idx[:, h, k:k + 1], axis=0),
                ).then_inc(gathered[h][k], 16)

            def edge_group(g, h):
                left = G - 1 - g if isinstance(g, int) else G
                if left >= 1:
                    copy_index(g + 1, 1 - h)
                for k in range(GT):
                    n = g * GT + k
                    if left >= 1:
                        gather(1 - h, k)
                    if k == 1 and left >= 2:
                        pool.wait_ge(s["rec_hi"], 2 * (g + 2) + 1)
                        split_features(g + 2)
                    pool.wait_ge(s["vb_hi"], n + 1)
                    atleast(pool, s["edges_summed"], n - 3)
                    pool.tensor_tensor(vb_lo[:, k, :, :], vb[:, k, :, :], vb_hi[:, k, :, :].bitcast(F32),
                                       ALU.subtract).then_inc(s["vb_lo"], 1)
                    if k == 1 and left >= 1:
                        split_hidden(g + 1, 1 - h)

            def split_features(g):
                pool.tensor_tensor(rec_f[:, :, 2:4, 0:NF],
                                   rec[:, bass.ds(g * GT * REC, GT * REC)].rearrange("p (k u c) -> p k u c", u=1, c=REC)
                                   [:, :, :, 0:NF].to_broadcast([P, GT, 2, NF]),
                                   rec_hi[:, :, :].rearrange("p k (u c) -> p k u c", u=1).bitcast(F32)
                                   .to_broadcast([P, GT, 2, NF]), ALU.subtract).then_inc(s["staged_f"], 1)

            def split_hidden(g, h):
                pool.wait_ge(s["hid_hi"], g + 1)
                pool.tensor_tensor(hid[:, h, 1, :], h_full, hid[:, h, 0, :].bitcast(F32), ALU.subtract
                                   ).then_inc(s["hid_done"], 1)

            pool.wait_ge(s["dense_ready"], LAYERS * NB)
            pool.memset(agg[:, 0:half_agg], 0.0).then_inc(s["agg_zeroed"], 1)
            pool.wait_ge(s["rec_hi"], 1)
            split_features(0)
            copy_index(0, 0)
            pool.wait_ge(s["table_written"], 16 * NB)
            for k in range(GT):
                gather(0, k)
                if k == 1:
                    pool.wait_ge(s["rec_hi"], 3)
                    split_features(1)
            split_hidden(0, 0)
            over_groups(pool, G, edge_group)

        @block.scalar
        def _(act):
            act.preload_act_table_set("natural_log_exp_and_others")
            er = E_rec.rearrange("p (t c) -> p t c", c=REC)
            act.wait_ge(s["edges_loaded"], 80)
            act.activation(er[:, :, C_DST], dst_i, ACT.Copy).then_inc(s["edge_copied"], 1)
            act.activation(er[:, :, C_CUT], w_raw, ACT.Copy).then_inc(s["edge_copied"], 1)
            act.activation(er[:, :, 0:20], f_raw.rearrange("p (t c) -> p t c", c=20), ACT.Copy).then_inc(s["edge_copied"], 1)
            act.wait_ge(s["norm_sq"], 1)
            act.activation(norm[:, 0:ET], norm[:, ET:2 * ET], ACT.Sqrt).then_inc(s["norm_ready"], 1)
            act.preload_act_table_set("natural_log_exp_and_others")

            def w_hi(w, n):
                act.wait_ge(s["raw_loaded"], 16 * (n + 1))
                act.activation(w[:, 0, :, :], raw[:, :, :], ACT.Copy).then_inc(s["w_hi"], 1)

            def ht_hi(b, done):
                act.wait_ge(s["h_turned"], done + 1)
                act.activation(HT[:, 0, :, b * P:(b + 1) * P], ps[:, b % 2, :].rearrange("p (k n) -> p k n", k=K),
                               ACT.Copy).then_inc(s["ht_hi"], 1)

            def g_hi(b, done):
                act.wait_ge(s["g_ready"], done + 1)
                act.activation(GN[:, 0, b, :], ps[:, 2 + b % 2, :], ACT.Copy).then_inc(s["g_hi"], 1)

            w_hi(Wn, 0)
            act.wait_ge(s["sort_step"], SORTED)
            def copy_own(b):
                act.wait_ge(s["own_ready"], b + 1)
                act.activation(S0[:, :, b * P:(b + 1) * P], ps[:, 2 + b % 2, :].rearrange("p (k n) -> p k n", k=K),
                               ACT.Copy).then_inc(s["own_copied"], 1)

            for b in range(NB):
                ht_hi(b, b)
                g_hi(b, b)
            act.wait_ge(s["pads_written"], 64)
            w_hi(Ws, 1)
            for b in range(NB):
                copy_own(b)
            act.wait_ge(s["deg_summed"], ET)
            act.activation(degrees, psf[0:1, 2048:2048 + NP], ACT.Copy).then_inc(s["deg_copied"], 1)

            def copy_counts(g, h):
                act.wait_ge(s["tile_summed"], GT * (g + 1))
                atleast(act, s["counts_added"], g - 1)
                act.activation(counts_sb[:, h * NC:(h + 1) * NC], psf[:, 1536 * h:1536 * h + NC], ACT.Copy
                               ).then_inc(s["counts_copied"], 1)

            act.wait_ge(s["rec_split"], 9)
            def own_rows(g, h):
                atleast(act, s["own_hots"], g)
                for k in range(1, GT):
                    act.activation(own_distance[:, k - 1, :], iota_n[:, 0:P], ACT.Abs,
                                   bias=own_f[:, bass.ds(g * GT + k, 1)], scale=-1.0).then_inc(s["own_abs"], 1)
                atleast(act, s["tile_summed"], GT * (g - 1))
                act.wait_ge(s["own_abs"], (GT - 1) * (g + 1))
                act.activation(oh_own[:, h, 1:GT, :], own_distance[:, :, :], ACT.Relu, bias=ones[:, 0:1], scale=-1.0
                               ).then_inc(s["own_hots"], 1)

            def counts_group(g, h):
                left = G - 1 - g if isinstance(g, int) else G
                if left >= 1:
                    own_rows(g + 1, 1 - h)
                copy_counts(g, h)

            own_rows(0, 0)
            over_groups(act, G, counts_group)
            act.wait_ge(s["tile_summed"], T)

            with act.Fori(0, LAYERS - 1, 1) as i:
                w_hi(Wn, 2 * i + 2)
                for b in range(NB):
                    act.wait_ge(s["dense_step"], 2 * NB * i + 2 * b + 2)
                    act.activation(tmp[:, b % 2, 0, :], tmp[:, b % 2, 1, :], ACT.Relu).then_inc(s["h_ready"], 1)
                    if b >= 1:
                        ht_hi(b - 1, NB * i + NB + b - 1)
                ht_hi(NB - 1, NB * i + 2 * NB - 1)
                w_hi(Ws, 2 * i + 3)
                for b in range(NB):
                    g_hi(b, NB * i + NB + b)

            act.wait_ge(s["var_ready"], 1)
            act.activation(rstd[:, 1, :], rstd[:, 0, :], ACT.Sqrt).then_inc(s["std_ready"], 1)
            act.preload_act_table_set("natural_log_exp_and_others")
            def stage_features(g):
                atleast(act, s["f_turned"], g)
                atleast(act, s["staged_f"], g)
                act.activation(rec_hi[:, :, :],
                               rec[:, bass.ds(g * GT * REC, GT * REC)].rearrange("p (k c) -> p k c", c=REC)[:, :, 0:NF],
                               ACT.Copy).then_inc(s["rec_hi"], 1)
                act.wait_ge(s["rec_hi"], 2 * g + 1)
                act.activation(rec_f[:, :, 0:2, 0:NF], rec_hi[:, :, :].rearrange("p k (u c) -> p k u c", u=1)
                               .bitcast(F32).to_broadcast([P, GT, 2, NF]), ACT.Copy).then_inc(s["rec_hi"], 1)

            for b in range(NB + 1):
                if b < NB:
                    act.wait_ge(s["x_turned"], b + 1)
                    act.activation(XT[:, :, b * P:(b + 1) * P], ps[:, b % 2, :].rearrange("p (k n) -> p k n", k=K),
                                   ACT.Copy).then_inc(s["xt_copied"], 1)
                if b == NB:
                    act.wait_ge(s["edge_weights_loaded"], 16 * 7)
                    act.wait_ge(s["filter_prep"], 7)
                    stage_features(0)
                if b >= 1:
                    act.wait_ge(s["table_ready"], b)
                    act.activation(TAB[:, :, (b - 1) * P:b * P],
                                   ps[:, 2 + (b - 1) % 2, :].rearrange("p (k n) -> p k n", k=K), ACT.Copy
                                   ).then_inc(s["table_copied"], 1)

            def copy_features(g):
                act.wait_ge(s["f_turned"], g + 1)
                atleast(act, s["hid_ready"], g)
                act.activation(f_t, ps[:, 0, :], ACT.Copy).then_inc(s["ft_copied"], 1)

            def hid_1(g):
                act.wait_ge(s["hid_ready"], g + 1)
                act.activation(h_abs, ps[:, 1, :].rearrange("p (u f) -> p u f", f=P), ACT.Abs).then_inc(s["hid_abs"], 1)
                act.wait_ge(s["hid_abs"], g + 1)
                act.activation(h_exp.rearrange("p (u f) -> p u f", f=P), h_abs, ACT.Exp, scale=-1.0).then_inc(s["hid_exp"], 1)

            def hid_2(g):
                act.wait_ge(s["hid_exp"], g + 1)
                act.activation(h_ln, h_exp, ACT.Ln, bias=half[:, :], scale=0.5).then_inc(s["hid_ln"], 1)

            def hid_hi(g, h):
                act.wait_ge(s["hid_full"], g + 1)
                atleast(act, s["w_ready"], GT * (g - 1))
                act.activation(hid[:, h, 0, :], h_full, ACT.Copy).then_inc(s["hid_hi"], 1)

            def gathered_all(g, h):
                return 16 * (g // 2 + 1) if isinstance(g, int) else 8 * g + (16 if h == 0 else 8)

            def begin_dot(g, h, k):
                n = g * GT + k
                act.wait_ge(gathered[h][k], gathered_all(g, h))
                act.sem_inc(s["act_turns"], 1)
                act.activation(dots[:, k, 0, :], rows[:, h, k, P:2 * P], ACT.Copy,
                               scale=rec[:, bass.ds(n * REC + C_DIR, 1)]).then_inc(s["dot_begun"], 1)

            def direct(g, h, k):
                n = g * GT + k
                act.wait_ge(s["msg_ready"], 4 * n + 2)
                act.activation(vb_hi[:, k, :, :], vb[:, k, :, :], ACT.Copy).then_inc(s["vb_hi"], 1)
                for i in range(3):
                    act.activation(msg[:, k, M_VA + i, :], msg[:, k, M_SCALED, :], ACT.Copy,
                                   scale=rec[:, bass.ds(n * REC + C_DIR + i, 1)]).then_inc(s["va_ready"], 1)

            def group(g, h):
                left = G - 1 - g if isinstance(g, int) else G
                if left >= 1:
                    hid_2(g + 1)
                direct(g, h, 0)
                if left >= 2:
                    stage_features(g + 2)
                begin_dot(g, h, 2)
                direct(g, h, 1)
                if left >= 1:
                    hid_hi(g + 1, 1 - h)
                begin_dot(g, h, 3)
                direct(g, h, 2)
                if left >= 2:
                    copy_features(g + 2)
                if left >= 1:
                    begin_dot(g + 1, 1 - h, 0)
                direct(g, h, 3)
                if left >= 1:
                    begin_dot(g + 1, 1 - h, 1)
                if left >= 2:
                    hid_1(g + 2)

            copy_features(0)
            stage_features(1)
            hid_1(0)
            hid_2(0)
            hid_hi(0, 0)
            copy_features(1)
            begin_dot(0, 0, 0)
            begin_dot(0, 0, 1)
            hid_1(1)
            over_groups(act, G, group)

            def copy_agg(b):
                act.wait_ge(s["agg_turned"], b + 1)
                if b >= 2:
                    act.wait_ge(s["s_ready"], b - 1)
                for u in range(2):
                    act.activation(agg_t[:, b % 2, 4 * u:4 * u + 4, :],
                                   ps[:, u, :].rearrange("p (m n) -> p m n", m=4), ACT.Copy).then_inc(s["agg_copied"], 1)

            copy_agg(0)
            for b in range(NB):
                if b + 1 < NB:
                    copy_agg(b + 1)
                act.wait_ge(s["s_ready"], b + 1)
                if b >= 2:
                    act.wait_ge(s["o_ready"], b - 1)
                    act.wait_ge(s["sv_ready"], b - 1)
                pb = ps[:, 2 + b % 2, :].rearrange("p (m n) -> p m n", m=4)
                act.activation(s_tmp[:, b % 2, 0, :], pb[:, 0, :], ACT.Abs).then_inc(s["s_step"], 1)
                act.activation(sv[:, b % 2, 1:4, :], pb[:, 1:4, :], ACT.Copy).then_inc(s["v_copied"], 1)
                act.wait_ge(s["s_step"], 3 * b + 1)
                act.activation(s_tmp[:, b % 2, 1, :], s_tmp[:, b % 2, 0, :], ACT.Exp, scale=-1.0).then_inc(s["s_step"], 1)
                act.wait_ge(s["s_step"], 3 * b + 2)
                act.activation(s_tmp[:, b % 2, 2, :], s_tmp[:, b % 2, 1, :], ACT.Ln, bias=half[:, :], scale=0.5
                               ).then_inc(s["s_step"], 1)
            act.wait_ge(s["var_ready"], 2)
            act.activation(rstd[:, 1, :], rstd[:, 0, :], ACT.Sqrt).then_inc(s["std_ready"], 1)

        @block.vector
        def _(dve):
            v = nc.vector
            v.memset(pads[:, :], 0.0).then_inc(s["zeroed"], 1)
            dve.wait_ge(s["zeroed"], 1)
            v.memset(pads[:, :].rearrange("p (t c) -> p t c", c=REC)[:, :, C_OWN], -1.0).then_inc(s["zeroed"], 1)
            v.memset(wf1_raw[:, :], 0.0).then_inc(s["zeroed"], 1)
            v.memset(ones[:, :], 1.0).then_inc(s["zeroed"], 1)
            v.memset(ones_bf[:, :], 1.0).then_inc(s["zeroed"], 1)
            v.memset(half[:, :], 0.5).then_inc(s["zeroed"], 1)
            v.memset(ones3[:, :], 1.0).then_inc(s["zeroed"], 1)
            v.memset(bucket_end[:, 0:1], 0.0).then_inc(s["zeroed"], 1)
            er = E_rec.rearrange("p (t c) -> p t c", c=REC)
            v.memset(er[:, :, C_ONE], 1.0).then_inc(s["zeroed"], 1)
            v.memset(er[:, :, C_OWN + 1:REC], 0.0).then_inc(s["zeroed"], 1)

            step = Chain(dve, s["sort_step"])
            step(v.memset(all_ones, 1.0))
            dve.wait_ge(s["edges_loaded"], 80)
            dve.wait_ge(s["consts_made"], 1)
            step(v.tensor_scalar(blk_i, src_i, 7, None, ALU.arith_shift_right))
            step(v.tensor_copy(blk_f, blk_i))
            step(v.scalar_tensor_tensor(out=er[:, :, C_OWN], in0=blk_f, scalar=-float(P), in1=src_i,
                                        op0=ALU.mult, op1=ALU.add))
            pbt = lambda a: a.rearrange("p (b t) -> p b t", b=NB)
            step(v.tensor_tensor(pbt(in_bucket), blk_f.rearrange("p (a t) -> p a t", a=1).to_broadcast([EP, NB, ET]),
                                 pbt(bucket), ALU.is_equal))
            step(v.tensor_tensor_scan(running, all_ones, in_bucket, 0.0, ALU.mult, ALU.add))
            dve.wait_ge(s["zeroed"], 8)
            step(v.tensor_copy(bucket_end[:, 1:NB + 1], pbt(running)[:, :, ET - 1]))
            counts = small[0:EP, 0, :]
            v.tensor_tensor(counts, bucket_end[:, 1:NB + 1], bucket_end[:, 0:NB], ALU.subtract).then_inc(s["counts_ready"], 1)
            r3 = lambda a: a.rearrange("p (t c) -> p t c", c=3)
            step(v.tensor_tensor(r_sq, r_raw, r_raw, ALU.mult))
            v.tensor_reduce(norm[:, ET:2 * ET], r3(r_sq), axis=AX.X, op=ALU.add).then_inc(s["norm_sq"], 1)
            dve.wait_ge(s["totals_ready"], 1)
            g_i, g_s = small[:, 1, :].bitcast(I32), small[:, 2, :].bitcast(I32)
            g_f, g_end, g_start = small[:, 3, :], small[:, 4, :], small[:, 5, :]
            first, base = small[0:EP, 6, :], small[0:EP, 7, :]
            step(v.tensor_scalar(g_i, ps[:, 7, 16:16 + NB], float(GSZ - 1), None, ALU.add))
            step(v.tensor_scalar(g_s, g_i, SH, None, ALU.arith_shift_right))
            step(v.tensor_copy(g_f, g_s))
            step(v.tensor_tensor_scan(g_end, ones[:, 0:NB], g_f, 0.0, ALU.mult, ALU.add))
            step(v.tensor_tensor(g_start, g_end, g_f, ALU.subtract))
            step(v.scalar_tensor_tensor(out=first, in0=g_start[0:EP, :], scalar=float(GSZ), in1=ps[0:EP, 7, 0:NB],
                                        op0=ALU.mult, op1=ALU.add))
            step(v.scalar_tensor_tensor(out=base, in0=first, scalar=-1.0, in1=bucket_end[:, 0:NB],
                                        op0=ALU.add, op1=ALU.subtract))
            step(v.tensor_tensor(pbt(running), pbt(running),
                                 base.rearrange("p (b a) -> p b a", a=1).to_broadcast([EP, NB, ET]), ALU.add))
            step(v.tensor_tensor(running, running, in_bucket, ALU.mult))
            step(v.tensor_reduce(place_f, running.rearrange("p (b t) -> p t b", b=NB), axis=AX.X, op=ALU.add))
            step(v.tensor_copy(place_i, place_f))
            step(v.tensor_scalar(place_lo, place_i, P - 1, None, ALU.bitwise_and))
            step(v.tensor_scalar(place_hi, place_i, 7, None, ALU.arith_shift_right))
            step(v.scalar_tensor_tensor(out=row_i, in0=place_lo, scalar=float(T), in1=place_hi,
                                        op0=ALU.mult, op1=ALU.add))
            dve.wait_ge(s["norm_ready"], 1)
            step(v.reciprocal(norm[:, 2 * ET:3 * ET], norm[:, 0:ET]))
            step(v.tensor_tensor(er[:, :, C_DIR:C_DIR + 3], r3(r_raw),
                                 norm[:, 2 * ET:3 * ET].rearrange("p (t a) -> p t a", a=1).to_broadcast([EP, ET, 3]), ALU.mult))
            dve.wait_ge(s["edge_copied"], 3)
            dve.wait_ge(s["zeroed"], 10)
            assert step.n == SORTED

            def w_lo(w, n):
                dve.wait_ge(s["w_hi"], n + 1)
                v.tensor_tensor(w[:, 1, :, :], raw[:, :, :], w[:, 0, :, :].bitcast(F32), ALU.subtract).then_inc(s["w_split"], 1)

            def ht_lo(b, u, done):
                dve.wait_ge(s["ht_hi"], done + 1)
                v.tensor_tensor(HT[:, 1, :, bass.ds(b * P, P)], ps[:, u, :].rearrange("p (k n) -> p k n", k=K),
                                HT[:, 0, :, bass.ds(b * P, P)].bitcast(F32), ALU.subtract).then_inc(s["ht_done"], 1)

            def g_lo(b, u, done):
                dve.wait_ge(s["g_hi"], done + 1)
                v.tensor_tensor(GN[:, 1, bass.ds(b, 1), :], ps[:, 2 + u:3 + u, :],
                                GN[:, 0, bass.ds(b, 1), :].bitcast(F32), ALU.subtract).then_inc(s["g_done"], 1)

            def stage_edges(i, h):
                atleast(dve, s[f"scattered_{h}"], 16 * ST * i)
                v.tensor_copy(stage[:, h, :, :].rearrange("p k c -> p (k c)"),
                              E_rec[:, bass.ds((i * 2 + h) * (ST * REC), ST * REC)]).then_inc(s["staged"], 1)
                v.tensor_copy(stage_idx[:, h, :], row_i[:, bass.ds((i * 2 + h) * ST, ST)]).then_inc(s["staged"], 1)

            stage_edges(0, 0)
            stage_edges(0, 1)
            w_lo(Wn, 0)
            with v.Fori(0, NB // 2, 1) as i:
                for h in range(2):
                    stage_edges(i + 1, h)
                    ht_lo(2 * i + h, h, 2 * i + h)
                    g_lo(2 * i + h, h, 2 * i + h)
            dve.wait_ge(s["g_ready"], NB)
            dve.wait_ge(s["consts_made"], 9)
            left = HALVES // 2 - NB // 2 - 1
            PER = ET // left // DH * DH

            def degree_hots(t, k):
                atleast(dve, s["deg_summed"], t - DH + 1)
                v.tensor_scalar(deg_hots[:, k % DH, :], iota_n[0:EP, :], E_rec[:, bass.ds(t * REC + C_DST, 1)], None,
                                ALU.is_equal).then_inc(s["deg_hots"], 1)

            stage_edges(NB // 2 + 1, 0)
            stage_edges(NB // 2 + 1, 1)
            w_lo(Ws, 1)
            for k in range(PER):
                degree_hots(k, k)
            with v.Fori(1, left, 1) as i:
                for h in range(2):
                    stage_edges(i + NB // 2 + 1, h)
                    for k in range(h * (PER // 2), PER // 2 if h == 0 else PER):
                        degree_hots(i * PER + k, k)
            for k in range(left * PER, ET):
                degree_hots(k, k)

            dve.wait_ge(s["deg_ready"], 1)
            step(v.tensor_scalar(small[:, 8, :], ps[:, 7, 0:NB], 1.0, None, ALU.max))
            v.reciprocal(inv_deg[:, :], small[:, 8, :]).then_inc(s["inv_ready"], 1)
            v.tensor_reduce(small[:, 9, 0:1], small[:, 8, :], axis=AX.X, op=ALU.max).then_inc(s["max_ready"], 1)
            dve.wait_ge(s["max_turned"], 1)
            step(v.tensor_reduce(degree_row[:, :], ps[0:1, 6, 0:P], axis=AX.X, op=ALU.max))
            v.tensor_scalar(many[:, :], degree_row[:, :], 4096.0, None, ALU.is_gt).then_inc(s["many_ready"], 1)

            step(v.tensor_tensor(iota_g[:, :, :], iota_g[:, :, :],
                                 g_end[0:1, :].rearrange("p (a b) -> p a b", a=1).to_broadcast([1, G, NB]), ALU.is_ge))
            step(v.tensor_reduce(blocks_before[:, :], iota_g[:, :, :], axis=AX.X, op=ALU.add))
            v.tensor_scalar(group_block[:, :], blocks_before[:, :], float(NB - 1), None, ALU.min).then_inc(s["blocks_known"], 1)
            dve.wait_ge(s["blocks_known"], 1)
            assert NB <= 16
            v.scalar_tensor_tensor(out=pair_block[:, 0:G - 1], in0=group_block[:, 1:G], scalar=16.0,
                                   in1=group_block[:, 0:G - 1], op0=ALU.mult, op1=ALU.add
                                   ).then_inc(s["blocks_known"], 1)
            dve.wait_ge(s["blocks_known"], 2)

            dve.wait_ge(s["many_ready"], 1)
            too_many = v.value_load(many[0:1, 0:1], min_val=0, max_val=1)
            with v.If(too_many):
                v.memset(at_columns(AT[:, :], NC, NP), 0.0).then_inc(s["prep"], 1)
            with v.Else():
                v.memset(at_columns(AT_rounded, NC, NP).bitcast(F32), 0.0).then_inc(s["prep"], 1)
            dve.wait_ge(s["scattered_0"], 16 * ST * (HALVES // 2))
            dve.wait_ge(s["scattered_1"], 16 * ST * (HALVES // 2))
            for i in range(4):
                sh = shares[i % 3].rearrange("p (t c) -> p t c", c=REC)
                dve.wait_ge(s[f"rec_loaded_{i % 3}"], 16 * (i // 3 + 1))
                v.tensor_copy(dst_f[:, i * SHARE:(i + 1) * SHARE], sh[:, :, C_DST]).then_inc(s["rec_split"], 1)
                v.tensor_copy(own_f[:, i * SHARE:(i + 1) * SHARE], sh[:, :, C_OWN]).then_inc(s["rec_split"], 1)
            dve.wait_ge(s["rec_split"], 8)
            v.tensor_copy(dst_idx[:, :], dst_f[:, :]).then_inc(s["rec_split"], 1)
            dve.wait_ge(s["prep"], 1)
            dve.wait_ge(s["g_ready"], NB)

            def one_hots(g, h):
                for k in range(GT):
                    t = g * GT + k
                    atleast(dve, s["tile_summed"], t - 3)
                    v.tensor_scalar(oh_dst[:, k % 4, :], iota_n[:, :], dst_f[:, bass.ds(t, 1)], None,
                                    ALU.is_equal).then_inc(s["one_hots"], 1)
                    if k == 0:
                        v.tensor_scalar(oh_own[:, h, k, :], iota_n[:, 0:P], own_f[:, bass.ds(t, 1)], None,
                                        ALU.is_equal).then_inc(s["one_hots"], 1)

            two = {}

            def add_block(g, h, counts):
                dve.wait_ge(s["tile_summed"], GT * (g + 1))
                atleast(dve, s["block_added"], g)
                b = block_of(v, two, g, h == 1)
                a = counts[:, bass.ds(b * NP + NC, NP - NC)]
                v.tensor_tensor(a, a.bitcast(F32), psf[:, 1536 * h + 1024:1536 * h + 1536], ALU.add).then_inc(s["block_added"], 1)

            def count_group(g, h, counts):
                one_hots(g, h)
                if not (isinstance(g, int) and g == 0):
                    add_block(g - 1, 1 - h, counts)

            with v.If(too_many):
                over_groups(v, G, lambda g, h: count_group(g, h, AT))
                add_block(G - 1, (G - 1) % 2, AT)
            with v.Else():
                over_groups(v, G, lambda g, h: count_group(g, h, AT_rounded))
                add_block(G - 1, (G - 1) % 2, AT_rounded)

            dve.wait_ge(s["inv_ready"], 1)
            dve.wait_ge(s["own_copied"], NB)

            def combine(l, b):
                dve.wait_ge(s["bias_loaded"], 16 * l + 16)
                dve.wait_ge(s["dense_ready"], l * NB + b + 1)
                pd = 4 + 2 * (b % 2)
                v.scalar_tensor_tensor(out=tmp[:, b % 2, 0, :], in0=ps[:, pd + 1, :], scalar=inv_deg[:, b:b + 1],
                                       in1=bias[:, :], op0=ALU.mult, op1=ALU.add).then_inc(s["dense_step"], 1)
                dve.wait_ge(s["dense_step"], l * (2 * NB) + 2 * b + 1)
                blocks = lambda a: a.rearrange("p (k n) -> p k n", k=K)
                own = S0[:, :, b * P:(b + 1) * P] if isinstance(l, int) and l == 0 else blocks(ps[:, pd, :])
                v.tensor_tensor(blocks(tmp[:, b % 2, 1, :]), blocks(tmp[:, b % 2, 0, :]), own, ALU.add
                                ).then_inc(s["dense_step"], 1)

            dve.wait_ge(s["weights_loaded"], 160)
            c = C ** -0.5
            v.tensor_scalar(WIN[:, :, :], WIN[:, :, :], c, None, ALU.mult).then_inc(s["prep"], 1)

            for i in range(LAYERS - 1):
                w_lo(Wn, 2 * i + 2)
                for b in range(NB):
                    dve.wait_ge(s["h_turned"], NB * i + NB + b - 1 if b >= 2 else NB * i + NB)
                    combine(i, b)
                    if b >= 1:
                        ht_lo(b - 1, (b - 1) % 2, NB * i + NB + b - 1)
                ht_lo(NB - 1, (NB - 1) % 2, NB * i + 2 * NB - 1)
                w_lo(Ws, 2 * i + 3)
                for b in range(NB):
                    g_lo(b, b % 2, NB * i + NB + b)

            dve.wait_ge(s["h_turned"], NB * LAYERS)
            for b in range(NB):
                combine(LAYERS - 1, b)
                dve.wait_ge(s["dense_step"], 2 * NB * (LAYERS - 1) + 2 * b + 2)
                load = NB + b
                dve.wait_ge(s[f"x_loaded_{load % 4}"], 16 * (load // 4 + 1))
                v.tensor_tensor(X[:, b, :], x_in[:, load % 4, :], tmp[:, b % 2, 1, :], ALU.add).then_inc(s["z_ready"], 1)
                dve.wait_ge(s["z_ready"], b + 1)
                step(v.bn_stats(stats[:, b, :], X[:, b, :]))
                step(v.bn_aggr(mv[:, b, :], stats[:, b, :]))
            v.tensor_scalar(rstd[:, 0, :], mv[:, :, 1], LN_EPS, None, ALU.add).then_inc(s["var_ready"], 1)
            dve.wait_ge(s["std_ready"], 1)
            step(v.reciprocal(rstd[:, 2, :], rstd[:, 1, :]))
            for b in range(NB):
                v.tensor_scalar(X[:, b, :], X[:, b, :], mv[:, b, 0:1], rstd[:, 2, b:b + 1], ALU.subtract, ALU.mult
                                ).then_inc(s["x1_ready"], 1)
            v.memset(rec_f[:, :, :, :], 0.0).then_inc(s["filter_prep"], 1)
            v.tensor_copy(wf1_part[:, 0, :], wf1_raw[:, :]).then_inc(s["filter_prep"], 1)
            dve.wait_ge(s["filter_prep"], 2)
            v.tensor_tensor(wf1_part[:, 1, :], wf1_raw[:, :], wf1_part[:, 0, :].bitcast(F32), ALU.subtract
                            ).then_inc(s["filter_prep"], 1)
            dve.wait_ge(s["filter_prep"], 3)
            for q in range(4):
                v.tensor_copy(WF1[32 * q:32 * q + 32, :], wf1_part[32 * q:32 * q + 32, q % 2, :].bitcast(F32)
                              ).then_inc(s["filter_prep"], 1)
            dve.wait_ge(s["edge_weights_loaded"], 16 * 7)
            pair = lambda a, lo: a[:, lo:lo + 2 * P].rearrange("p (f u) -> p u f", u=2)
            k3 = 3.0 ** -0.5
            for j, (lo, u, scale) in enumerate(((2 * P, 0, Y1), (0, 0, Y0), (0, 1, Y1 * k3), (2 * P, 1, Y0))):
                v.tensor_scalar(wf2[:, j, :], pair(wf2_raw, lo)[:, u, :], scale, None, ALU.mult).then_inc(s["prep"], 1)
                step(v.tensor_scalar(bf_perm[:, j, :], pair(bf_raw, lo)[:, u, :], scale, None, ALU.mult))
            bfp = bf_perm.rearrange("p j f -> p (j f)")
            step(v.tensor_copy(bf_part[:, 0, :], bfp))
            step(v.tensor_tensor(bf_rest[:, 0, :], bfp, bf_part[:, 0, :], ALU.subtract))
            step(v.tensor_copy(bf_part[:, 1, :], bf_rest[:, 0, :]))
            step(v.tensor_tensor(bf_rest[:, 1, :], bf_rest[:, 0, :], bf_part[:, 1, :], ALU.subtract))
            step(v.tensor_scalar(bfp, bf_part[:, 0, :], sel3[:, 0:1], None, ALU.mult))
            step(v.scalar_tensor_tensor(out=bf_rest[:, 0, :], in0=bf_part[:, 1, :], scalar=sel3[:, 1:2], in1=bfp,
                                        op0=ALU.mult, op1=ALU.add))
            v.scalar_tensor_tensor(out=bf3[:, :], in0=bf_rest[:, 1, :], scalar=sel3[:, 2:3], in1=bf_rest[:, 0, :],
                                   op0=ALU.mult, op1=ALU.add).then_inc(s["prep"], 1)
            for wt, scale in ((W1[:, :, :, :], (2 * C) ** -0.5), (W2[:, :, :], c)):
                v.tensor_scalar(wt, wt, scale, None, ALU.mult).then_inc(s["prep"], 1)
            dve.wait_ge(s["prep"], 9)
            v.tensor_copy(WF[:, 0, :, :], wf2[:, :, :]).then_inc(s["prep"], 1)
            dve.wait_ge(s["prep"], 10)
            v.tensor_tensor(WF[:, 1, :, :], wf2[:, :, :], WF[:, 0, :, :].bitcast(F32), ALU.subtract).then_inc(s["prep"], 1)
            def finish_hidden(g):
                dve.wait_ge(s["hid_ln"], g + 1)
                atleast(dve, s["hid_hi"], g)
                atleast(dve, s["hid_done"], g)
                v.scalar_tensor_tensor(out=h_full, in0=ps[:, 1, :], scalar=0.0, in1=h_ln,
                                       op0=ALU.max, op1=ALU.add).then_inc(s["hid_full"], 1)

            finish_hidden(0)
            dve.wait_ge(s["table_written"], 16 * NB)
            v.memset(agg[:, half_agg:], 0.0).then_inc(s["agg_zeroed"], 1)
            dve.wait_ge(s["agg_zeroed"], 2)
            dve.wait_ge(s["x1_ready"], NB)

            def messages(g, h, k):
                n = g * GT + k
                dve.wait_ge(s["w_ready"], n + 1)
                dve.wait_ge(gathered[h][k], 16 * (g // 2 + 1) if isinstance(g, int) else 8 * g + (16 if h == 0 else 8))
                atleast(dve, s["edges_summed"], n - 3)
                atleast(dve, s["va_ready"], 3 * (n - 3))
                atleast(dve, s["vb_lo"], n - 3)
                w = ps[:, 2 + k % 2, :].rearrange("p (m f) -> p m f", m=4)
                r = rows[:, h, k, :].rearrange("p (m f) -> p m f", m=4)
                y = lambda i: rec[:, bass.ds(n * REC + C_DIR + i, 1)]
                cutoff = rec[:, bass.ds(n * REC + C_CUT, 1)]
                v.scalar_tensor_tensor(out=msg[:, k, M_SCALED:M_SA + 1, :], in0=w[:, 0:2, :], scalar=cutoff,
                                       in1=r[:, 0:1, :].to_broadcast([P, 2, P]), op0=ALU.mult, op1=ALU.mult
                                       ).then_inc(s["msg_ready"], 1)
                dve.wait_ge(s["dot_begun"], n + 1)
                v.scalar_tensor_tensor(out=dots[:, k, 1, :], in0=r[:, 2, :], scalar=y(1), in1=dots[:, k, 0, :],
                                       op0=ALU.mult, op1=ALU.add).then_inc(s["dot_step"], 1)
                v.scalar_tensor_tensor(out=vb[:, k, :, :], in0=w[:, 3:4, :].to_broadcast([P, 3, P]), scalar=cutoff,
                                       in1=r[:, 1:4, :], op0=ALU.mult, op1=ALU.mult).then_inc(s["msg_ready"], 1)
                dve.wait_ge(s["dot_step"], 2 * n + 1)
                v.scalar_tensor_tensor(out=dots[:, k, 2, :], in0=r[:, 3, :], scalar=y(2), in1=dots[:, k, 1, :],
                                       op0=ALU.mult, op1=ALU.add).then_inc(s["dot_step"], 1)
                v.tensor_scalar(hot[:, k, :], iota_n[:, 0:P], rec[:, bass.ds(n * REC + C_OWN, 1)], None,
                                ALU.is_equal).then_inc(s["msg_ready"], 1)
                dve.wait_ge(s["dot_step"], 2 * n + 2)
                v.scalar_tensor_tensor(out=msg[:, k, M_SB, :], in0=dots[:, k, 2, :], scalar=cutoff, in1=w[:, 2, :],
                                       op0=ALU.mult, op1=ALU.mult).then_inc(s["msg_ready"], 1)

            def add_sums(g, h):
                dve.wait_ge(s["edges_summed"], GT * (g + 1))
                atleast(dve, s["agg_added"], g)
                b = block_of(v, two, g, h == 1)
                a = agg[:, bass.ds(b * NA, NA)]
                v.tensor_tensor(a, a, psf[:, (4 + 2 * h) * 512:(6 + 2 * h) * 512], ALU.add).then_inc(s["agg_added"], 1)

            def edge_group(g, h):
                is_first = isinstance(g, int) and g == 0
                is_last = isinstance(g, int) and g == G - 1
                messages(g, h, 0)
                messages(g, h, 1)
                if not is_last:
                    finish_hidden(g + 1)
                messages(g, h, 2)
                messages(g, h, 3)
                if not is_first:
                    add_sums(g - 1, 1 - h)

            over_groups(v, G, edge_group)
            add_sums(G - 1, (G - 1) % 2)

            def softplus(b):
                dve.wait_ge(s["s_step"], 3 * b + 3)
                dve.wait_ge(s["v_copied"], b + 1)
                if b >= 2:
                    dve.wait_ge(s["o_ready"], b - 1)
                v.scalar_tensor_tensor(out=sv[:, b % 2, 0, :], in0=ps[:, 2 + b % 2, 0:P], scalar=0.0,
                                       in1=s_tmp[:, b % 2, 2, :], op0=ALU.max, op1=ALU.add).then_inc(s["sv_ready"], 1)

            def residual(b):
                dve.wait_ge(s["o_ready"], b + 1)
                po = ps[:, 4 + b % 2, :]
                n = b * 4
                v.tensor_tensor(X[:, b, 0:P], X[:, b, 0:P], po[:, 0:P], ALU.add).then_inc(s["z_step"], 1)
                xv = X[:, b, P:].rearrange("p (f i) -> p i f", i=3)
                v.tensor_tensor(xv, xv, po[:, P:].rearrange("p (i f) -> p i f", i=3), ALU.add).then_inc(s["z_step"], 1)
                dve.wait_ge(s["z_step"], n + 2)
                v.bn_stats(stats[:, b, :], X[:, b, :]).then_inc(s["z_step"], 1)
                dve.wait_ge(s["z_step"], n + 3)
                v.bn_aggr(mv[:, b, :], stats[:, b, :]).then_inc(s["z_step"], 1)

            for b in range(NB + 1):
                if b < NB:
                    softplus(b)
                if b >= 1:
                    residual(b - 1)
            dve.wait_ge(s["z_step"], 4 * NB)
            v.tensor_scalar(rstd[:, 0, :], mv[:, :, 1], LN_EPS, None, ALU.add).then_inc(s["var_ready"], 1)
            dve.wait_ge(s["std_ready"], 2)
            step(v.reciprocal(rstd[:, 2, :], rstd[:, 1, :]))
            for b in range(NB):
                v.tensor_scalar(X[:, b, :], X[:, b, :], mv[:, b, 0:1], rstd[:, 2, b:b + 1], ALU.subtract, ALU.mult
                                ).then_inc(s["out_ready"], 1)

        @block.tensor
        def _(pe):
            mm = nc.tensor.matmul
            pe.wait_ge(s["consts_made"], 7)
            pe.wait_ge(s["zeroed"], 7)
            pe.wait_ge(s["counts_ready"], 1)
            counts = small[0:EP, 0, :]
            mm(ps[0:EP, 7, 0:NB], lower[0:EP, 0:EP], counts, start=True, stop=True)
            mm(ps[:, 7, 16:16 + NB], ones[0:EP, :], counts, start=True, stop=True).then_inc(s["totals_ready"], 1)

            def turn(source, b, ready):
                for f, a in enumerate(source):
                    last = nc.tensor.transpose(ps[:, b % 2, f * P:(f + 1) * P], a, ident[:, :])
                last.then_inc(s[ready], 1)

            split = ((0, 0), (0, 1), (1, 0))

            def rows_times(bank, b, w):
                for j, (x_part, w_part) in enumerate(split):
                    for f in range(K):
                        last = mm(ps[:, bank, :], HT[:, x_part, f, b * P:(b + 1) * P], w[:, w_part, f, :],
                                  start=(j == 0 and f == 0), stop=(j == 2 and f == K - 1))
                return last

            def times_neighbours(b, done):
                pe.wait_ge(s["ht_done"], done + 1)
                atleast(pe, s["g_done"], done - 1)
                rows_times(2 + b % 2, b, Wn).then_inc(s["g_ready"], 1)

            def times_own(b):
                pe.wait_ge(s["w_split"], 2)
                atleast(pe, s["own_copied"], b - 1)
                rows_times(2 + b % 2, b, Ws).then_inc(s["own_ready"], 1)

            pe.wait_ge(s["w_split"], 1)
            for b in range(NB + 1):
                if b < NB:
                    pe.wait_ge(s[f"x_loaded_{b % 4}"], 16 * (b // 4 + 1))
                    atleast(pe, s["ht_done"], b - 1)
                    turn([x_in[:, b % 4, f * P:(f + 1) * P] for f in range(K)], b, "h_turned")
                if b >= 1:
                    times_neighbours(b - 1, b - 1)

            def sum_degrees(t, k, first, last):
                pe.wait_ge(s["deg_hots"], t + 1)
                for a, z in SLICES:
                    done = mm(psf[0:1, 2048 + a:2048 + z], ones_bf[0:EP, 0:1], deg_hots[:, k, a:z], start=first, stop=last)
                done.then_inc(s["deg_summed"], 1)

            def some_degrees(first, end):
                with pe.Fori(first, end, 1) as i:
                    for k in range(DH):
                        sum_degrees(i * DH + k, k, False, False)

            pe.wait_ge(s["g_done"], NB)
            for k in range(DH):
                sum_degrees(k, k, k == 0, False)
            turns = (ET // DH - 2) // NB
            for b in range(NB):
                some_degrees(1 + b * turns, 1 + (b + 1) * turns)
                times_own(b)
            some_degrees(1 + NB * turns, ET // DH - 1)
            for k in range(DH):
                sum_degrees(ET - DH + k, k, False, k == DH - 1)
            pe.wait_ge(s["deg_copied"], 1)
            for b in range(NB):
                last = mm(ps[:, 7, b:b + 1], degrees[:, b * P:(b + 1) * P], ones[0:1, 0:1], start=True, stop=True)
            last.then_inc(s["deg_ready"], 1)
            pe.wait_ge(s["max_ready"], 1)
            nc.tensor.transpose(ps[0:1, 6, 0:P], small[:, 9, 0:1], ident[:, :]).then_inc(s["max_turned"], 1)

            pe.wait_ge(s["g_done"], NB)

            def count_group(g, h):
                atleast(pe, s["block_added"], g - 1)
                atleast(pe, s["counts_copied"], g - 1)
                for k in range(GT):
                    pe.wait_ge(s["one_hots"], (GT + 1) * g + k + 2)
                    if k == 1:
                        pe.wait_ge(s["own_hots"], g + 1)
                    for a, z, place in COUNT_SLICES:
                        last = mm(psf[:, 1536 * h + place:1536 * h + place + z - a], oh_own[:, h, k, :], oh_dst[:, k % 4, a:z],
                                  start=(k == 0), stop=(k == GT - 1))
                    last.then_inc(s["tile_summed"], 1)

            over_groups(pe, G, count_group)

            pe.wait_ge(s["many_ready"], 1)
            pe.wait_ge(s["block_added"], G)
            pe.wait_ge(s["counts_added"], G)
            too_many = nc.tensor.value_load(many[0:1, 0:1], min_val=0, max_val=1)
            a_t = AT[:, :].rearrange("p (j n) -> p j n", j=NB)

            def mean_block(bank, b, ready):
                with nc.tensor.If(too_many):
                    for part in range(2):
                        for j in range(NB):
                            last = mm(ps[:, bank, :], a_t[:, j, b * P:(b + 1) * P], GN[:, part, j, :].bitcast(F32),
                                      start=(part == 0 and j == 0), stop=(part == 1 and j == NB - 1))
                    last.then_inc(s[ready], 1)
                with nc.tensor.Else():
                    for part in range(2):
                        for j in range(NB):
                            last = mm(ps[:, bank, :], AT_r[:, j, b * P:(b + 1) * P], GN[:, part, j, :],
                                      start=(part == 0 and j == 0), stop=(part == 1 and j == NB - 1))
                    last.then_inc(s[ready], 1)

            def dense_block(l, b):
                atleast(pe, s["dense_step"], l * (2 * NB) + (2 * b - 2 if b >= 2 else 0))
                if l == 0:
                    mean_block(5 + 2 * (b % 2), b, "dense_ready")
                else:
                    mean_block(5 + 2 * (b % 2), b, "mean_ready")
                    rows_times(4 + 2 * (b % 2), b, Ws).then_inc(s["dense_ready"], 1)

            pe.wait_ge(s["w_split"], 2)
            for i in range(LAYERS - 1):
                def turn_relu(b):
                    pe.wait_ge(s["h_ready"], NB * i + b + 1)
                    pe.wait_ge(s["ht_done"], NB * i + NB + b - 1)
                    turn([tmp[:, b % 2, 0, f * P:(f + 1) * P] for f in range(K)], b, "h_turned")

                pe.wait_ge(s["g_done"], NB * i + NB)
                pe.wait_ge(s["w_split"], 2 * i + 2)
                for b in range(NB):
                    dense_block(i, b)
                    if b >= 1:
                        turn_relu(b - 1)
                turn_relu(NB - 1)
                pe.wait_ge(s["w_split"], 2 * i + 3)
                for b in range(NB):
                    times_neighbours(b, NB * i + NB + b)
            pe.wait_ge(s["g_done"], NB * LAYERS)
            pe.wait_ge(s["w_split"], 2 * LAYERS)
            for b in range(NB):
                dense_block(LAYERS - 1, b)

            pe.wait_ge(s["prep"], 2)
            for b in range(NB + 1):
                if b < NB:
                    pe.wait_ge(s["x1_ready"], b + 1)
                    atleast(pe, s["xt_copied"], b - 1)
                    turn([X[:, b, 0:P]] + [X[:, b, P + i:D:3] for i in range(3)], b, "x_turned")
                if b >= 1:
                    q = b - 1
                    pe.wait_ge(s["xt_copied"], q + 1)
                    atleast(pe, s["table_copied"], q - 1)
                    for f in range(K):
                        last = mm(ps[:, 2 + q % 2, f * P:(f + 1) * P], XT[:, f, q * P:(q + 1) * P],
                                  WIN[:, min(f, 1), :], start=True, stop=True)
                    last.then_inc(s["table_ready"], 1)

            def turn_features(g):
                pe.wait_ge(s["rec_hi"], 2 * g + 2)
                pe.wait_ge(s["staged_f"], g + 1)
                atleast(pe, s["ft_copied"], g)
                for k in range(GT):
                    last = nc.tensor.transpose(ps[:, 0, k * P:(k + 1) * P],
                                               rec_f[:, k, :, :].rearrange("p u c -> p (u c)"), ident[:, :])
                last.then_inc(s["f_turned"], 1)

            def hidden(g):
                pe.wait_ge(s["ft_copied"], g + 1)
                atleast(pe, s["hid_full"], g)
                mm(ps[:, 1, :], WF1[:, :], f_t, start=True, stop=True).then_inc(s["hid_ready"], 1)

            def weights(g, h, k):
                if k == 0:
                    pe.wait_ge(s["hid_done"], g + 1)
                mm(ps[:, 2 + k % 2, :], ones3[:, :], bf3[:, :], start=True, stop=False)
                for j, (h_part, w_part) in enumerate(split):
                    last = mm(ps[:, 2 + k % 2, :], hid[:, h, h_part, k * P:(k + 1) * P], WF[:, w_part, :, :],
                              start=False, stop=(j == 2))
                last.then_inc(s["w_ready"], 1)

            def sums(g, h, k):
                n = g * GT + k
                pe.wait_ge(s["va_ready"], 3 * n + 3)
                if k == 0:
                    atleast(pe, s["agg_added"], g - 1)
                first, last_k = k == 0, k == GT - 1
                bank = 4 + 2 * h
                own = hot[:, k, :]
                mm(ps[:, bank, :], own.bitcast(F32), msg[:, k, 1:5, :], start=first, stop=last_k)
                mm(ps[:, bank + 1, 0:P], own.bitcast(F32), msg[:, k, 5, :], start=first, stop=last_k,
                   skip_group_check=True)
                mm(ps[:, bank + 1, P:], own, vb_hi[:, k, :, :], start=False, stop=False, skip_group_check=True)
                pe.wait_ge(s["vb_lo"], n + 1)
                mm(ps[:, bank + 1, P:], own, vb_lo[:, k, :, :], start=False, stop=last_k,
                   skip_group_check=True).then_inc(s["edges_summed"], 1)

            def edge_group(g, h):
                left = G - 1 - g if isinstance(g, int) else G
                for k in range(GT):
                    if k == 2 and left >= 2:
                        turn_features(g + 2)
                    if k == 3 and left >= 2:
                        hidden(g + 2)
                    pe.wait_ge(s["msg_ready"], 4 * (g * GT + k) + 4)
                    if k + 2 < GT:
                        weights(g, h, k + 2)
                    elif left >= 1:
                        weights(g + 1, 1 - h, k + 2 - GT)
                    if k >= 1:
                        sums(g, h, k - 1)
                    elif not (isinstance(g, int) and g == 0):
                        sums(g - 1, 1 - h, GT - 1)

            pe.wait_ge(s["table_copied"], NB)
            pe.wait_ge(s["filter_prep"], 7)
            turn_features(0)
            hidden(0)
            turn_features(1)
            hidden(1)
            pe.wait_ge(s["prep"], PREPARED)
            weights(0, 0, 0)
            weights(0, 0, 1)
            over_groups(pe, G, edge_group)
            sums(G - 1, (G - 1) % 2, GT - 1)

            pe.wait_ge(s["agg_added"], G)
            ag = agg[:, :].rearrange("p (b m f) -> p b m f", b=NB, m=8)

            def turn_agg(b):
                if b >= 1:
                    pe.wait_ge(s["agg_copied"], 2 * b)
                for m in range(8):
                    last = nc.tensor.transpose(ps[:, m // 4, (m % 4) * P:(m % 4 + 1) * P], ag[:, b, m, :], ident[:, :])
                last.then_inc(s["agg_turned"], 1)

            def mix(b):
                pe.wait_ge(s["agg_copied"], 2 * b + 2)
                if b >= 2:
                    pe.wait_ge(s["sv_ready"], b - 1)
                a = agg_t[:, b % 2, :, :]
                pb = ps[:, 2 + b % 2, :]
                mm(pb[:, 0:P], W1[:, 0, 0, :], a[:, 0, :], start=True, stop=False)
                mm(pb[:, 0:P], W1[:, 0, 1, :], a[:, 1, :], start=False, stop=True)
                mm(pb[:, P:], W1[:, 1, 0, :], a[:, 2:5, :], start=True, stop=False)
                mm(pb[:, P:], W1[:, 1, 1, :], a[:, 5:8, :], start=False, stop=True).then_inc(s["s_ready"], 1)

            def project(b):
                pe.wait_ge(s["sv_ready"], b + 1)
                if b >= 2:
                    pe.wait_ge(s["z_step"], 4 * (b - 1))
                for m in range(4):
                    last = mm(ps[:, 4 + b % 2, m * P:(m + 1) * P], sv[:, b % 2, m, :], W2[:, min(m, 1), :],
                              start=True, stop=True)
                last.then_inc(s["o_ready"], 1)

            turn_agg(0)
            for b in range(NB + 1):
                if b + 1 < NB:
                    turn_agg(b + 1)
                if b < NB:
                    mix(b)
                if b >= 1:
                    project(b - 1)


INS = ("x", "src", "dst", "edge_attr_20", "edge_attr_3", "edge_weight",
       "L0_gnn_Ws_self", "L0_gnn_Ws_neigh", "L0_gnn_bs",
       "L1_gnn_W_in2f_s", "L1_gnn_W_in2f_v", "L1_gnn_Wf1", "L1_gnn_bf1", "L1_gnn_Wf2", "L1_gnn_bf2",
       "L1_gnn_W1_s", "L1_gnn_W1_v", "L1_gnn_W2_s", "L1_gnn_W2_v")


def kernel(**inputs):
    import numpy as np
    import concourse.bacc as bacc
    from concourse.bass_utils import run_bass_kernel_spmd

    nc = bacc.Bacc("TRN2", target_bir_lowering=False, num_devices=1)
    arrays, args = {}, []
    for name in INS:
        a = np.ascontiguousarray(inputs[name])
        arrays[f"in_{name}"] = a
        args.append(nc.dram_tensor(f"in_{name}", a.shape, mybir.dt.from_np(a.dtype), kind="ExternalInput").ap())
    shape = inputs["x"].shape
    out = nc.dram_tensor("out", shape, F32, kind="ExternalOutput").ap()
    gnn_resnorm(nc, *args, out)
    result = run_bass_kernel_spmd(nc, [arrays], core_ids=[0])
    return result.results[0]["out"]
```
